# Optimizing a Trainium2 kernel written in Bass

```python
import numpy as np
import jax
import jax.numpy as jnp

def _softmax(x, axis=-1):
    return jax.nn.softmax(x, axis=axis)

def _gelu(x):
    return jax.nn.gelu(x, approximate=True)

def _silu(x):
    return jax.nn.silu(x)

def _sigmoid(x):
    return jax.nn.sigmoid(x)

def _layernorm(x, axis=-1, eps=1e-05):
    m = jnp.mean(x, axis=axis, keepdims=True)
    v = jnp.var(x, axis=axis, keepdims=True)
    return (x - m) / jnp.sqrt(v + eps)

def _scatter_add(tgt, idx, src, axis=0):
    return tgt.at[idx].add(src)

def _segment_sum(src, seg, n):
    return jax.ops.segment_sum(src, seg, n)
kernel_name = 'mk_perceiver_d1_seqx_r8_bee85c'

def setup_inputs(seed: int=0):
    np.random.seed(seed)
    _w = jnp.asarray

    def _rec_inputs():
        import jax
        import jax.numpy as jnp
        _rk = jax.random.key(seed)
        x = -0.0005146 + 1 * jax.random.normal(jax.random.fold_in(_rk, 1), (8, 32, 512), jnp.float32)
        _lenS = 32 - jax.random.randint(jax.random.fold_in(_rk, 7), (8,), 0, max(1, 32 // 4) + 1, jnp.int32)
        _lenS2 = 512 - jax.random.randint(jax.random.fold_in(_rk, 8), (8,), 0, max(1, 512 // 4) + 1, jnp.int32)
        _ctx_4096P = jax.random.normal(jax.random.fold_in(_rk, 11), (8, 16, 512), jnp.float32)
        _ctx_4096c = jax.random.dirichlet(jax.random.fold_in(_rk, 511), 0.3 * jnp.ones((16,), jnp.float32), (8, 512))
        _ctx_4096t = jnp.einsum('bsk,bkd->bsd', _ctx_4096c, _ctx_4096P)
        _ctx_4096t = _ctx_4096t * jax.lax.rsqrt(jnp.mean(jnp.square(_ctx_4096t)) + 1e-12) * 0.953939
        ctx_4096 = -0.0142356 + 1.00583 * (_ctx_4096t + 0.3 * jax.random.normal(jax.random.fold_in(_rk, 611), (8, 512, 512), jnp.float32))
        return (x, ctx_4096)
    x, ctx_4096 = _rec_inputs()

    def _L0_xattn_setup():
        import jax, jax.numpy as jnp
        import numpy as np
        K = 10
        NUM_BITS = 10
        M_METHODS = 4

        def _quantize(coords, num_bits=NUM_BITS):
            cmin = coords.min(axis=1, keepdims=True)
            cmax = coords.max(axis=1, keepdims=True)
            scale = (2 ** num_bits - 1) / (cmax - cmin + 1e-06)
            q = jnp.floor((coords - cmin) * scale)
            return jnp.clip(q, 0, 2 ** num_bits - 1).astype(jnp.int32)

        def _morton_key(q):
            x, y, z = (q[..., 0], q[..., 1], q[..., 2])
            key = jnp.zeros(x.shape, dtype=jnp.int32)
            for b in range(NUM_BITS):
                key = key | (x >> b & 1) << 3 * b + 2 | (y >> b & 1) << 3 * b + 1 | (z >> b & 1) << 3 * b
            return key

        def _hilbert_key(q, num_bits=NUM_BITS):
            n = 3
            X = [q[..., i] for i in range(n)]
            M = 1 << num_bits - 1
            Q = M
            while Q > 1:
                P = Q - 1
                for i in range(n):
                    cond = X[i] & Q > 0
                    t = (X[0] ^ X[i]) & P
                    new_X0 = jnp.where(cond, X[0] ^ P, X[0] ^ t)
                    if i != 0:
                        X[i] = jnp.where(cond, X[i], X[i] ^ t)
                    X[0] = new_X0
                Q >>= 1
            for i in range(1, n):
                X[i] = X[i] ^ X[i - 1]
            t = jnp.zeros_like(X[0])
            Q = M
            while Q > 1:
                t = jnp.where(X[n - 1] & Q > 0, t ^ Q - 1, t)
                Q >>= 1
            X = [xi ^ t for xi in X]
            key = jnp.zeros(X[0].shape, dtype=jnp.int32)
            for b in range(num_bits - 1, -1, -1):
                for i in range(n):
                    key = key << 1 | X[i] >> b & 1
            return key

        def _sorted_indices(coords_bn3):
            q = _quantize(coords_bn3)
            qt = q[..., jnp.array([1, 0, 2])]
            keys = [_morton_key(q), _morton_key(qt), _hilbert_key(q), _hilbert_key(qt)]
            return [jnp.argsort(kk, axis=1) for kk in keys]

        def _window_inds(sorted_idx, k=K):
            B, N = sorted_idx.shape
            i = jnp.arange(N)
            start = jnp.maximum(0, i - k // 2)
            end = jnp.minimum(N, i + k // 2 + 1)
            pos = jnp.minimum(start[:, None] + jnp.arange(k)[None, :], (end - 1)[:, None])
            return jnp.take(sorted_idx, pos, axis=1)

        def _get_graph_features(feats, inds_list, perm, W_lin, b_lin, k=K):
            B, N, C = feats.shape
            center = feats[:, :, None, :]
            gather = jax.vmap(lambda f, idx: f[idx])
            per_method = []
            for inds in inds_list:
                neigh = gather(feats, inds)
                gf = jnp.concatenate([jnp.broadcast_to(center, (B, N, k, C)), neigh - center], axis=-1)
                per_method.append(gf)
            allf = jnp.stack(per_method, axis=-1)
            allf = allf[..., perm]
            total = 2 * C * M_METHODS
            x = allf.reshape(B * N, k, total)
            x16 = x.astype(jnp.float16).astype(jnp.float32)
            headdim = min(32, total)
            nheads = total // headdim
            qh = x16.reshape(B * N, k, nheads, headdim)
            scores = jnp.einsum('bihd,bjhd->bhij', qh, qh) / np.float32(np.sqrt(headdim))
            attn = jax.nn.softmax(scores, axis=-1)
            out = jnp.einsum('bhij,bjhd->bihd', attn, qh).reshape(B * N, k, total)
            fused = out @ W_lin.T + b_lin
            return fused.reshape(B, N, k, 64)

        def _instance_norm(x, axes):
            mu = x.mean(axis=axes, keepdims=True)
            var = x.var(axis=axes, keepdims=True)
            return (x - mu) / jnp.sqrt(var + 1e-05)

        def _lrelu(x):
            return jnp.where(x > 0, x, 0.2 * x)
        key = jax.random.key(seed)
        ks = jax.random.split(key, 8)
        B, N, C = (2, 512, 32)
        tot = M_METHODS * 2 * C
        s = 0.02
        return {'coords': jax.random.normal(ks[0], (B, 3, N), jnp.float32), 'feats': jax.random.normal(ks[1], (B, C, N), jnp.float32), 'W_lin1': jax.random.normal(ks[2], (64, tot), jnp.float32) * s, 'b_lin1': jnp.zeros((64,), jnp.float32), 'W_lin2': jax.random.normal(ks[3], (64, tot), jnp.float32) * s, 'b_lin2': jnp.zeros((64,), jnp.float32), 'W_conv1': jax.random.normal(ks[4], (C, 2 * C), jnp.float32) * s, 'W_conv2': jax.random.normal(ks[5], (2 * C, 2 * C), jnp.float32) * s, 'W_conv3': jax.random.normal(ks[6], (C, 4 * C), jnp.float32) * s}
    _L0_xattn_all = _L0_xattn_setup()
    _L0_xattn_in = {k: v for k, v in _L0_xattn_all.items() if k in ('W_lin1', 'b_lin1', 'W_lin2', 'b_lin2', 'W_conv1', 'W_conv2', 'W_conv3')}
    del _L0_xattn_all

    def _L0_attn_setup():
        import jax, jax.numpy as jnp
        import numpy as np
        HDC_DIM = 512
        N_HEADS = 4
        HEAD_DIM = HDC_DIM // N_HEADS

        def _ste_sign(w):
            alpha = jnp.mean(jnp.abs(w), axis=-1, keepdims=True)
            hard = alpha * jnp.sign(w)
            hard = jnp.where(hard == 0, alpha, hard)
            return jax.lax.stop_gradient(hard - w) + w
        key = jax.random.key(seed)
        kx, kq, kk, kv = jax.random.split(key, 4)
        B, T = (4, 256)
        x = jax.random.normal(kx, (B, T, HDC_DIM), dtype=jnp.float32)
        bv_q = jax.random.normal(kq, (N_HEADS, HEAD_DIM), dtype=jnp.float32) * 0.02
        bv_k = jax.random.normal(kk, (N_HEADS, HEAD_DIM), dtype=jnp.float32) * 0.02
        bv_v = jax.random.normal(kv, (N_HEADS, HEAD_DIM), dtype=jnp.float32) * 0.02
        return {'x': x, 'bv_q': bv_q, 'bv_k': bv_k, 'bv_v': bv_v}
    _L0_attn_all = _L0_attn_setup()
    _L0_attn_in = {k: v for k, v in _L0_attn_all.items() if k in ('bv_q', 'bv_k', 'bv_v')}
    del _L0_attn_all

    def _L0_ffn_setup():
        import jax, jax.numpy as jnp
        import numpy as np
        M = 512
        K = 512

        def _make_2to4_mask(key, shape):
            scores = jax.random.normal(key, shape)
            g = scores.reshape(shape[0], shape[1] // 4, 4)
            rank = jnp.argsort(jnp.argsort(-jnp.abs(g), axis=-1), axis=-1)
            return (rank < 2).reshape(shape).astype(jnp.float32)
        key = jax.random.key(seed)
        k_x, k_w12, k_b12, k_w3, k_b3, k_m = jax.random.split(key, 6)
        x = jax.random.normal(k_x, (4, 256, K), dtype=jnp.float32)
        w12_dense = jax.random.normal(k_w12, (2 * M, K), dtype=jnp.float32) * (1.0 / np.sqrt(K))
        mask12 = _make_2to4_mask(k_m, (2 * M, K))
        w12 = w12_dense * mask12
        b12 = jax.random.normal(k_b12, (2 * M,), dtype=jnp.float32) * 0.01
        w3 = jax.random.normal(k_w3, (M, M), dtype=jnp.float32) * (1.0 / np.sqrt(M))
        b3 = jax.random.normal(k_b3, (M,), dtype=jnp.float32) * 0.01
        return {'x': x, 'w12': w12, 'b12': b12, 'w3': w3, 'b3': b3}
    _L0_ffn_all = _L0_ffn_setup()
    _L0_ffn_in = {k: v for k, v in _L0_ffn_all.items() if k in ('w12', 'b12', 'w3', 'b3')}
    del _L0_ffn_all
    return {'x': x, 'ctx_4096': ctx_4096, 'L0_xattn_W_lin1': _L0_xattn_in['W_lin1'], 'L0_xattn_b_lin1': _L0_xattn_in['b_lin1'], 'L0_xattn_W_lin2': _L0_xattn_in['W_lin2'], 'L0_xattn_b_lin2': _L0_xattn_in['b_lin2'], 'L0_xattn_W_conv1': _L0_xattn_in['W_conv1'], 'L0_xattn_W_conv2': _L0_xattn_in['W_conv2'], 'L0_xattn_W_conv3': _L0_xattn_in['W_conv3'], 'L0_attn_bv_q': _L0_attn_in['bv_q'], 'L0_attn_bv_k': _L0_attn_in['bv_k'], 'L0_attn_bv_v': _L0_attn_in['bv_v'], 'L0_ffn_w12': _L0_ffn_in['w12'], 'L0_ffn_b12': _L0_ffn_in['b12'], 'L0_ffn_w3': _L0_ffn_in['w3'], 'L0_ffn_b3': _L0_ffn_in['b3']}

def reference(x, ctx_4096, L0_xattn_W_lin1, L0_xattn_b_lin1, L0_xattn_W_lin2, L0_xattn_b_lin2, L0_xattn_W_conv1, L0_xattn_W_conv2, L0_xattn_W_conv3, L0_attn_bv_q, L0_attn_bv_k, L0_attn_bv_v, L0_ffn_w12, L0_ffn_b12, L0_ffn_w3, L0_ffn_b3):
    import jax
    import jax.numpy as jnp

    def _L0_xattn_ref(coords, feats, W_lin1, b_lin1, W_lin2, b_lin2, W_conv1, W_conv2, W_conv3):
        import jax, jax.numpy as jnp
        import numpy as np
        K = 10
        NUM_BITS = 10
        M_METHODS = 4

        def _quantize(coords, num_bits=NUM_BITS):
            cmin = coords.min(axis=1, keepdims=True)
            cmax = coords.max(axis=1, keepdims=True)
            scale = (2 ** num_bits - 1) / (cmax - cmin + 1e-06)
            q = jnp.floor((coords - cmin) * scale)
            return jnp.clip(q, 0, 2 ** num_bits - 1).astype(jnp.int32)

        def _morton_key(q):
            x, y, z = (q[..., 0], q[..., 1], q[..., 2])
            key = jnp.zeros(x.shape, dtype=jnp.int32)
            for b in range(NUM_BITS):
                key = key | (x >> b & 1) << 3 * b + 2 | (y >> b & 1) << 3 * b + 1 | (z >> b & 1) << 3 * b
            return key

        def _hilbert_key(q, num_bits=NUM_BITS):
            n = 3
            X = [q[..., i] for i in range(n)]
            M = 1 << num_bits - 1
            Q = M
            while Q > 1:
                P = Q - 1
                for i in range(n):
                    cond = X[i] & Q > 0
                    t = (X[0] ^ X[i]) & P
                    new_X0 = jnp.where(cond, X[0] ^ P, X[0] ^ t)
                    if i != 0:
                        X[i] = jnp.where(cond, X[i], X[i] ^ t)
                    X[0] = new_X0
                Q >>= 1
            for i in range(1, n):
                X[i] = X[i] ^ X[i - 1]
            t = jnp.zeros_like(X[0])
            Q = M
            while Q > 1:
                t = jnp.where(X[n - 1] & Q > 0, t ^ Q - 1, t)
                Q >>= 1
            X = [xi ^ t for xi in X]
            key = jnp.zeros(X[0].shape, dtype=jnp.int32)
            for b in range(num_bits - 1, -1, -1):
                for i in range(n):
                    key = key << 1 | X[i] >> b & 1
            return key

        def _sorted_indices(coords_bn3):
            q = _quantize(coords_bn3)
            qt = q[..., jnp.array([1, 0, 2])]
            keys = [_morton_key(q), _morton_key(qt), _hilbert_key(q), _hilbert_key(qt)]
            return [jnp.argsort(kk, axis=1) for kk in keys]

        def _window_inds(sorted_idx, k=K):
            B, N = sorted_idx.shape
            i = jnp.arange(N)
            start = jnp.maximum(0, i - k // 2)
            end = jnp.minimum(N, i + k // 2 + 1)
            pos = jnp.minimum(start[:, None] + jnp.arange(k)[None, :], (end - 1)[:, None])
            return jnp.take(sorted_idx, pos, axis=1)

        def _get_graph_features(feats, inds_list, perm, W_lin, b_lin, k=K):
            B, N, C = feats.shape
            center = feats[:, :, None, :]
            gather = jax.vmap(lambda f, idx: f[idx])
            per_method = []
            for inds in inds_list:
                neigh = gather(feats, inds)
                gf = jnp.concatenate([jnp.broadcast_to(center, (B, N, k, C)), neigh - center], axis=-1)
                per_method.append(gf)
            allf = jnp.stack(per_method, axis=-1)
            allf = allf[..., perm]
            total = 2 * C * M_METHODS
            x = allf.reshape(B * N, k, total)
            x16 = x.astype(jnp.float16).astype(jnp.float32)
            headdim = min(32, total)
            nheads = total // headdim
            qh = x16.reshape(B * N, k, nheads, headdim)
            scores = jnp.einsum('bihd,bjhd->bhij', qh, qh) / np.float32(np.sqrt(headdim))
            attn = jax.nn.softmax(scores, axis=-1)
            out = jnp.einsum('bhij,bjhd->bihd', attn, qh).reshape(B * N, k, total)
            fused = out @ W_lin.T + b_lin
            return fused.reshape(B, N, k, 64)

        def _instance_norm(x, axes):
            mu = x.mean(axis=axes, keepdims=True)
            var = x.var(axis=axes, keepdims=True)
            return (x - mu) / jnp.sqrt(var + 1e-05)

        def _lrelu(x):
            return jnp.where(x > 0, x, 0.2 * x)
        inds_sorted = _sorted_indices(coords.transpose(0, 2, 1))
        inds_list = [_window_inds(s) for s in inds_sorted]
        perm1 = jnp.array([2, 0, 3, 1])
        perm2 = jnp.array([1, 3, 0, 2])
        f0 = feats.transpose(0, 2, 1)
        g1 = _get_graph_features(f0, inds_list, perm1, W_lin1, b_lin1)
        h1 = jnp.einsum('oc,bnkc->bonk', W_conv1, g1)
        h1 = _lrelu(_instance_norm(h1, (2, 3)))
        feats1 = h1.max(axis=-1)
        g2 = _get_graph_features(feats1.transpose(0, 2, 1), inds_list, perm2, W_lin2, b_lin2)
        h2 = jnp.einsum('oc,bnkc->bonk', W_conv2, g2)
        h2 = _lrelu(_instance_norm(h2, (2, 3)))
        feats2 = h2.max(axis=-1)
        f3 = jnp.concatenate([feats, feats1, feats2], axis=1)
        h3 = jnp.einsum('oc,bcn->bon', W_conv3, f3)
        return _lrelu(_instance_norm(h3, (2,)))

    def _L0_attn_ref(x, bv_q, bv_k, bv_v):
        import jax, jax.numpy as jnp
        import numpy as np
        HDC_DIM = 512
        N_HEADS = 4
        HEAD_DIM = HDC_DIM // N_HEADS

        def _ste_sign(w):
            alpha = jnp.mean(jnp.abs(w), axis=-1, keepdims=True)
            hard = alpha * jnp.sign(w)
            hard = jnp.where(hard == 0, alpha, hard)
            return jax.lax.stop_gradient(hard - w) + w
        B, T, D = x.shape
        H, HD = (N_HEADS, HEAD_DIM)
        scale = HD ** (-0.5)
        q_bind = _ste_sign(bv_q)
        k_bind = _ste_sign(bv_k)
        v_bind = _ste_sign(bv_v)
        xh = x.reshape(B, T, H, HD)
        Q = xh * q_bind
        K = xh * k_bind
        V = xh * v_bind
        scores = jnp.einsum('bthd,bshd->bhts', Q, K) * scale
        causal = jnp.tril(jnp.ones((T, T), dtype=bool))
        attn = jnp.where(causal, jax.nn.sigmoid(scores * 4.0), 0.0)
        out = jnp.einsum('bhts,bshd->bthd', attn, V)
        return out.reshape(B, T, D)

    def _L0_ffn_ref(x, w12, b12, w3, b3):
        import jax, jax.numpy as jnp
        import numpy as np
        M = 512
        K = 512

        def _make_2to4_mask(key, shape):
            scores = jax.random.normal(key, shape)
            g = scores.reshape(shape[0], shape[1] // 4, 4)
            rank = jnp.argsort(jnp.argsort(-jnp.abs(g), axis=-1), axis=-1)
            return (rank < 2).reshape(shape).astype(jnp.float32)
        x12 = jnp.einsum('bsk,mk->bsm', x, w12) + b12
        x1, x2 = jnp.split(x12, 2, axis=-1)
        x4 = jax.nn.silu(x1) * x2
        return jnp.einsum('bsm,nm->bsn', x4, w3) + b3
    x = x + _L0_xattn_ref(ctx_4096, _layernorm(x, axis=-1), L0_xattn_W_lin1, L0_xattn_b_lin1, L0_xattn_W_lin2, L0_xattn_b_lin2, L0_xattn_W_conv1, L0_xattn_W_conv2, L0_xattn_W_conv3)
    x = x + _L0_attn_ref(_layernorm(x, axis=-1), L0_attn_bv_q, L0_attn_bv_k, L0_attn_bv_v)
    x = x + _L0_ffn_ref(_layernorm(x, axis=-1), L0_ffn_w12, L0_ffn_b12, L0_ffn_w3, L0_ffn_b3)
    return x

_drawn_inputs = setup_inputs


def setup_inputs(seed=0):
    import zlib

    import numpy as np

    out = dict(_drawn_inputs(seed))
    spreads = {'L0_xattn_b_lin1': (0.0, 2.0), 'L0_xattn_b_lin2': (0.0, 2.0)}
    factors = {'L0_attn_bv_q': 64.0, 'L0_attn_bv_k': 64.0, 'L0_ffn_b12': 8.0, 'L0_ffn_b3': 7.529}
    for name, (base, spread) in spreads.items():
        noise = np.random.default_rng([zlib.crc32(name.encode()), seed]).standard_normal(out[name].shape)
        drawn = base * np.exp(spread * noise) if base else spread * noise
        out[name] = jnp.asarray(drawn.astype(out[name].dtype))
    for name, factor in factors.items():
        out[name] = (out[name] * factor).astype(out[name].dtype)
    return out
```

```python
from contextlib import ExitStack
from math import log, sqrt

import numpy as np

import concourse.bass as bass
from concourse import mybir
from concourse.alu_op_type import AluOpType as ALU

ACT = mybir.ActivationFunctionType
AX = mybir.AxisListType
F32 = mybir.dt.float32
F16 = mybir.dt.float16
BF16 = mybir.dt.bfloat16
I32 = mybir.dt.int32

B, C, N = 8, 32, 512
BH = 4
HALVES = B // BH
M = 4
K = 10
HEADS = 4
BITS = 10
NT = N // 128
EPS = 1e-5

G = 12
ROWS = G * K
SPAN = G + K - 1
COLS = HEADS * SPAN
STEPS = -(-N // G)
NPAD = STEPS * G
LEFT = K // 2
SW = 528
HEAD_SCALE = 1.0 / sqrt(32.0)
W_SCALE = 1024.0
PERMS = ([2, 0, 3, 1], [1, 3, 0, 2])
OUTS = (32, 64)
LAST_ROWS = (N - (STEPS - 1) * G) * K


def constants():
    def short(a):
        return (a.astype(np.float32).view(np.uint32) & np.uint32(0xFFFF0000)).view(np.float32)

    n, p = np.arange(G)[:, None], np.arange(SPAN)[None, :]
    far = float(short(np.array(-1e30)))
    inner = np.where((p >= n) & (p <= n + K - 1), 0.0, far)
    edge = np.where(p < LEFT, far, inner)
    for i in range(LEFT):
        edge[i, i + K] = sqrt(32.0) * log(LEFT - i)
    parts, rest = [], edge.astype(np.float64)
    for _ in range(3):
        part = short(rest)
        rest = np.where(edge == far, 0.0, rest - part.astype(np.float64))
        parts.append(part)
    edge3 = np.concatenate(parts, 0)
    ind = np.repeat(np.eye(G), K, axis=1)
    q = np.arange(128)
    s, t = q[:, None], q[None, :]
    return {
        "c_ident": np.eye(128, dtype=np.float32),
        "c_rows": np.concatenate([ind] * 3, 0).astype(np.float32),
        "c_inner": inner.astype(np.float32),
        "c_edge": edge3.astype(np.float32),
        "c_headmask": ((q[:, None] % C) // 8 == np.arange(HEADS)).astype(np.float32),
        "c_iota": np.tile(np.arange(N, dtype=np.float16), (128, 1)),
        "c_causal": ((s // C == t // C) & (s <= t)).astype(np.float32),
        "c_rows3": np.stack([np.ones(B * N), -np.ones(B * N), np.tile(np.arange(N) % 256, B)]).astype(np.float32),
        "c_nhigh": np.tile(((q % 16) * 32 // 256)[:, None], (1, M * 32)).astype(np.int32),
    }


def build(nc, d):
    ctx = ExitStack()
    with ctx:
        def sb(name, shape, dt):
            return ctx.enter_context(nc.sbuf_tensor(name, shape, dt))

        def sem(name):
            return ctx.enter_context(nc.semaphore(name))

        bank = [ctx.enter_context(nc.psum_tensor(f"bank{i}", [128, 512], F32)) for i in range(8)]

        q_dram = nc.dram_tensor("q_scratch", (3, B * N), I32, kind="Internal").ap()
        chunk_dram = nc.dram_tensor("chunk_scratch", (4, M, B * N), BF16, kind="Internal").ap()

        ident = sb("ident", [128, 128], F32)
        rows_ind = sb("rows_ind", [3 * G, ROWS], BF16)
        inner_mask = sb("inner_mask", [G, SPAN], BF16)
        edge_mask = sb("edge_mask", [3 * G, SPAN], BF16)
        headmask = sb("headmask", [128, HEADS], F32)
        iota = sb("iota", [128, N], F16)
        causal = sb("causal", [128, 128], F32)
        nhigh = sb("nhigh", [128, M * 32], I32)
        wlin = [sb(f"wlin{l}", [64, 256], F32) for l in range(2)]
        wconvT = [sb(f"wconvT{l}", [64, 128], F32) for l in range(2)]
        blin = [sb(f"blin{l}", [64, 1], F32) for l in range(2)]
        w3bd = sb("w3bd", [128, 4, 128], F32)
        wv_hi = [sb(f"wv_hi{l}", [128, OUTS[l]], F16) for l in range(2)]
        wv_lo = [sb(f"wv_lo{l}", [128, OUTS[l]], F16) for l in range(2)]
        wcen = [sb(f"wcen{l}", [128, BH * OUTS[l]], F32) for l in range(2)]
        wdif = [sb(f"wdif{l}", [128, BH * OUTS[l]], F32) for l in range(2)]
        bias = [sb(f"bias{l}", [128, 1], F32) for l in range(2)]
        eps_col = sb("eps_col", [128, 1], F32)

        X = sb("X", [128, HALVES, N], F32)
        FX = sb("FX", [128, HALVES, N], F32)
        F1 = sb("F1", [128, N], F32)
        F2 = sb("F2", [128, 2, N], F32)
        ymax = sb("ymax", [128, 2, NPAD], F32)
        z = sb("z", [128, 2, NPAD], F32)
        cen16 = sb("cen16", [128, N], F16)
        cen32 = sb("cen32", [128, N], F32)
        fT = sb("fT", [128, 2, 512], F16)
        bst = sb("bst", [128, 2, STEPS, 6], F32)
        mv = sb("mv", [128, 2, 2], F32)
        rstd = sb("rstd", [128, 2], F32)
        nmr = sb("nmr", [128, 2], F32)
        ranks = sb("ranks", [128, M * B * NT], F32)
        counts = sb("counts", [128, M * B * NT], F32)

        xq = sb("xq", [128, 2, BH * ROWS], F16)
        dif = sb("dif", [128, 2, BH * COLS], F32)
        mx = sb("mx", [128, 2, BH * HEADS], F32)
        ex = sb("ex", [128, 2, BH * COLS], F32)
        sm = sb("sm", [128, 2, BH * HEADS], F32)
        rs = sb("rs", [128, 2, BH * HEADS], F32)
        at = sb("at", [128, 2, BH * COLS], F32)
        atT = sb("atT", [COLS, 2, BH * ROWS], F32)
        val = sb("val", [COLS, 2, BH * 64], F32)
        ys = sb("ys", [128, 2, 2 * ROWS], F32)

        arena = sb("arena", [128, 71040], BF16)
        KN = M * B * N
        LA, RA, LB, RB = (arena[0:r, i * KN:(i + 1) * KN] for i, r in enumerate((6, 6, 4, 4)))
        at0 = 0

        def carve(words, dt, width):
            nonlocal at0
            v = arena[:, at0:at0 + words * width // 2]
            at0 += words * width // 2
            return v.bitcast(dt) if dt != BF16 else v

        perm = carve(M * BH * NT * N, F16, 2).rearrange("p (j r) -> p j r", r=N)
        khi = carve(BH * HEADS * SW, F16, 2).rearrange("p (b c) -> p b c", b=BH)
        klo = carve(BH * HEADS * SW, F16, 2).rearrange("p (b c) -> p b c", b=BH)
        Sx = carve(BH * SW, F32, 4).rearrange("p (b s) -> p b s", b=BH)
        Frep = carve(BH * NPAD, F32, 4).rearrange("p (b n) -> p b n", b=BH)
        w12T = carve(4 * 1024, F32, 4).rearrange("p (k m) -> p k m", k=4)
        w3T = carve(4 * 512, F32, 4).rearrange("p (k m) -> p k m", k=4)
        assert at0 <= 71040, at0

        crd, crf = ymax[0:24, 0, 0:N], ymax[0:24, 1, 0:N]
        crq = dif[0:24, :, :].rearrange("p a b -> p (a b)")[:, 0:N].bitcast(I32)
        cs = sb("cs", [24, 16], F32)
        Q3 = sb("Q3", [128, 3, 32], I32)

        def words(v):
            return v[:, 0:3 * M * 32].bitcast(I32).rearrange("p (w a j) -> p w a j", w=3, a=M)

        XK = words(F2[:, 0, :])
        T1, T2 = words(F2[:, 1, :]), words(F1[:, :])
        T3 = cen32[:, 0:4 * M * 32].bitcast(I32).rearrange("p (c j) -> p c j", c=4)
        chunks = sb("chunks", [128, 4, M * 32], BF16)

        tail = perm.rearrange("p j r -> p (j r)")
        at1 = 0

        def tcarve(words):
            nonlocal at1
            v = tail[:, at1:at1 + 2 * words].bitcast(F32)
            at1 += 2 * words
            return v

        bind, sgb = (tcarve(3 * N).rearrange("p (a n) -> p a n", a=3) for _ in range(2))
        b12 = sb("b12", [128, 8], F32)
        b3row = sb("b3row", [128, N], F32)
        qkv = tcarve(3 * N).rearrange("p (a n) -> p a n", a=3)
        qkT = tcarve(8 * 128).rearrange("p (a n) -> p a n", a=8)
        sg = tcarve(4 * 128).rearrange("p (a n) -> p a n", a=4)
        sgm = tcarve(4 * 128).rearrange("p (a n) -> p a n", a=4)
        xn = tcarve(2 * N).rearrange("p (a n) -> p a n", a=2)
        xnT = tcarve(4 * 256).rearrange("p (a n) -> p a n", a=4)
        gate = tcarve(4 * 256).rearrange("p (a n) -> p a n", a=4)
        x4T = tcarve(4 * 256).rearrange("p (a n) -> p a n", a=4)
        outb = tcarve(2 * N).rearrange("p (a n) -> p a n", a=2)
        res = tcarve(2 * N).rearrange("p (a n) -> p a n", a=2)

        alpha = sb("alpha", [128, 12], F32)

        def spread(v, n):
            return bass.AP(v.tensor, v.offset, list(v.ap) + [[0, n]])

        S = {}
        for name in ("consts coords x_in weights ffn_w q_out q_in chunk_out chunk_in ones dve_link act_link pool_link "
                     "coords_scaled chunks_done cmp_ready act_counted dve_counted ranked onehot "
                     "folded fold_taken zeroed f0_ready f1_ready f2_ready fT_psum fT_hi fT_lo frep sorted_psum sorted_sb "
                     "key_hi key_lo cen_done z_psum z_ready x_ready sc_ready d_ready e_ready r_ready a_ready "
                     "aT_psum aT_sb v_psum v_sb y_psum stat_sqrt stat_var h3_psum h3_done "
                     "att_in att_T att_Tc att_sc att_sg att_m att_o ffn_x ffn_T ffn_Tc ffn_h ffn_g ffn_x4 ffn_o out_ready stored "
                     "mx_done sum_done ys_done x_main ymax_done edge_done lnv lnq bind_in masks").split():
            S[name] = sem(name)

        block = ctx.enter_context(nc.Block())

        def chain(eng, name):
            count = [0]

            def link(ins):
                count[0] += 1
                ins.then_inc(S[name], 1)
                eng.wait_ge(S[name], count[0])
            return link

        def pipeline(eng, step, last):
            for t in range(6):
                step(t, t % 2)
            lo, hi = 3, (STEPS - 1) // 2
            with eng.Fori(lo, hi) as i:
                step(2 * i, 0)
                step(2 * i + 1, 1)
            for t in range(2 * hi, STEPS + last):
                step(t, t % 2)

        def features_ready(eng, u, l):
            eng.wait_ge(S["f0_ready" if l == 0 else "f1_ready"], 1 if l == 0 else u + 1)

        def live(t):
            return not isinstance(t, int) or 0 <= t < STEPS

        def freed(eng, s, name, lag=2):
            if not isinstance(s, int) or s >= lag:
                eng.wait_ge(S[name], s + 1 - lag)

        def sl(v, start, n):
            return v[:, bass.ds(start, n)]

        NWEIGHTS = 24
        PASSES = [(u, l) for u in range(HALVES) for l in range(2)]

        def window(base, n0, n, step_list):
            v = base[:, bass.ds(n0, n)] if not isinstance(n0, int) else base[:, n0:n0 + n]
            return bass.AP(v.tensor, v.offset, [v.ap[0]] + step_list)

        def by_head(v):
            return v.rearrange("p (b s h) -> p b h s", b=BH, h=HEADS)

        def heads(v):
            return v.rearrange("p (b h) -> p b h", b=BH)

        @block.sync
        def _(sp):
            ctx4 = d["ctx_4096"]
            for c in range(3):
                sp.dma_start(crd[8 * c:8 * c + 8, :], ctx4[:, c, :]).then_inc(S["coords"], 16)
            for u in range(HALVES):
                sp.dma_start(X[:, u, :], d["x"][BH * u:BH * u + BH].rearrange("b c n -> (b c) n")).then_inc(S["x_in"], 16)
            for dst, name in ((ident, "c_ident"), (headmask, "c_headmask"), (iota, "c_iota"), (causal, "c_causal"), (nhigh, "c_nhigh")):
                sp.dma_start(dst[:, :], d[name]).then_inc(S["consts"], 16)
            sp.wait_ge(S["coords_scaled"], 1)
            sp.dma_start(q_dram.rearrange("c (b n) -> (c b) n", b=B), crq[:, :]).then_inc(S["q_out"], 16)
            sp.wait_ge(S["q_out"], 16)
            sp.dma_start(Q3[:, :, :], q_dram.rearrange("c (p j) -> p c j", j=32)).then_inc(S["q_in"], 16)
            sp.wait_ge(S["chunks_done"], 1)
            for j in range(4):
                sp.dma_start(chunk_dram[j].rearrange("m (p j) -> p m j", j=32),
                             chunks[:, j, :].rearrange("p (m j) -> p m j", m=M)).then_inc(S["chunk_out"], 16)
            sp.wait_ge(S["chunk_out"], 16 * 4)
            top = chunk_dram.rearrange("j m n -> j (m n)")
            sp.dma_start(LA[3:6, :], top[1:4, :]).then_inc(S["chunk_in"], 16)
            sp.dma_start(RA[0:3, :], top[1:4, :]).then_inc(S["chunk_in"], 16)
            sp.dma_start(LB[2:3, :], top[0:1, :]).then_inc(S["chunk_in"], 16)
            sp.dma_start(RB[0:1, :], top[0:1, :]).then_inc(S["chunk_in"], 16)
            sp.wait_ge(S["ranked"], 1)
            sp.dma_start(w12T, d["w12T"].rearrange("(k p) m -> p k m", p=128)).then_inc(S["ffn_w"], 16)
            sp.dma_start(w3T, d["w3T"].rearrange("(k p) m -> p k m", p=128)).then_inc(S["ffn_w"], 16)
            sp.wait_ge(S["zeroed"], 3)
            for p, (u, l) in enumerate(PASSES):
                F = FX[:, u, :] if l == 0 else F1[:, :]
                features_ready(sp, u, l)
                if p:
                    sp.wait_ge(S["x_ready"], STEPS * p)
                for m in range(M):
                    for b in range(BH):
                        sp.dma_start(Frep[C * m:C * m + C, b, 0:N], F[C * b:C * b + C, :]).then_inc(S["frep"], 16)
            for u in range(HALVES):
                sp.wait_ge(S["out_ready"], u + 1)
                sp.dma_start(d["out"][BH * u:BH * u + BH].rearrange("b c n -> (b c) n"), outb[:, u, :]).then_inc(S["stored"], 16)
            sp.wait_ge(S["stored"], 16 * HALVES)

        @block.gpsimd
        def _(pool):
            link = chain(pool, "pool_link")
            for dst, r, k in ((LA[0:3], 0, 3), (RA[3:6], 1, 3), (LB[0:2], 0, 2), (RB[2:4], 1, 2), (LB[3:4], 2, 1),
                              (RB[1:2], 2, 1)):
                row = d["c_rows3"][r:r + 1, :]
                pool.dma_start(dst.rearrange("k (m n) -> k m n", m=M),
                               bass.AP(row.tensor, row.offset, [[0, k], [0, M], [1, B * N]])).then_inc(S["ones"], 16)
            for dst, name in ((rows_ind, "c_rows"), (inner_mask, "c_inner"), (edge_mask, "c_edge")):
                pool.dma_start(dst[:, :], d[name]).then_inc(S["masks"], 16)
            for l in range(2):
                rep = 128 // OUTS[l]
                for r in range(rep):
                    pool.dma_start(wconvT[l][:, r * OUTS[l]:(r + 1) * OUTS[l]], d[f"wc{l}T"]).then_inc(S["weights"], 16)
                pool.dma_start(wlin[l][:, :], d[f"wl{l}"]).then_inc(S["weights"], 16)
                pool.dma_start(blin[l][:, :], d[f"bl{l}"].rearrange("(j a) -> j a", a=1)).then_inc(S["weights"], 16)
            link(nc.gpsimd.memset(w3bd[:, :, :], 0.0))
            for b in range(BH):
                o = slice(C * b, C * b + C)
                pool.dma_start(w3bd[C * b:C * b + C, 0, o], d["w3cT"][0:C, :]).then_inc(S["weights"], 16)
                pool.dma_start(w3bd[C * b:C * b + C, 1, o], d["w3cT"][C:2 * C, :]).then_inc(S["weights"], 16)
                r = 64 * (b % 2)
                pool.dma_start(w3bd[r:r + 64, 2 + b // 2, o], d["w3cT"][2 * C:4 * C, :]).then_inc(S["weights"], 16)
            pool.dma_start(b12[:, :], d["b12"]).then_inc(S["weights"], 16)
            b3 = d["b3"]
            pool.dma_start(b3row[:, :], bass.AP(b3.tensor, b3.offset, [[0, 128], [1, N]])).then_inc(S["weights"], 16)
            nc.gpsimd.memset(z[:, :, :], 0.0).then_inc(S["zeroed"], 1)
            pool.wait_ge(S["ranked"], 1)
            nc.gpsimd.memset(Sx, 0.0).then_inc(S["zeroed"], 1)
            nc.gpsimd.memset(Frep[:, :, N:NPAD], 0.0).then_inc(S["zeroed"], 1)

            for p, (u, l) in enumerate(PASSES):
                base = STEPS * p
                if p == len(PASSES) - 1:
                    pool.wait_ge(S["sorted_psum"], BH * len(PASSES))
                    for i, name in enumerate(("bv_q", "bv_k", "bv_v")):
                        row = d[name].rearrange("h e -> (h e)").rearrange("(a n) -> a n", a=1)
                        pool.dma_start(bind[:, i, :], bass.AP(row.tensor, row.offset, [[0, 128], [1, N]])).then_inc(S["bind_in"], 16)

                def form_x(t, k):
                    s = base + t
                    freed(pool, s, "sc_ready")
                    if isinstance(t, int) and t == 0:
                        pool.wait_ge(S["frep"], 16 * 16 * (p + 1))
                        pool.wait_ge(S["sorted_sb"], 8 * (p + 1))
                    src = window(Sx[:, 0, :], G * t, 1, [[SW, BH], [1, G], [1, K]])
                    cen = window(Frep[:, 0, :], G * t, 1, [[NPAD, BH], [1, G], [0, K]])
                    out = xq[:, k, :].rearrange("p (b n i) -> p b n i", b=BH, n=G)
                    ins = nc.gpsimd.tensor_tensor(out, src, cen, ALU.subtract)
                    if isinstance(t, int) and t == 0:
                        ins.then_inc(S["x_main"], 1)
                        pool.wait_ge(S["x_main"], p + 1)
                        for n in range(LEFT):
                            w = LEFT - n
                            ins = nc.gpsimd.tensor_tensor(
                                out[:, :, n, 0:w],
                                window(Sx[:, 0, :], n + K, 1, [[SW, BH], [0, w]]),
                                window(Frep[:, 0, :], n, 1, [[NPAD, BH], [0, w]]), ALU.subtract)
                            if n < LEFT - 1:
                                ins.then_inc(S["edge_done"], 1)
                        pool.wait_ge(S["edge_done"], (LEFT - 1) * (p + 1))
                    ins.then_inc(S["x_ready"], 1)

                def normalise(t, k):
                    s = base + t
                    pool.wait_ge(S["r_ready"], s + 1)
                    freed(pool, s, "aT_psum")
                    r = rs[0:ROWS, k, :]
                    nc.gpsimd.tensor_tensor(by_head(at[0:ROWS, k, :]), by_head(ex[0:ROWS, k, :]),
                                            spread(heads(r), SPAN), ALU.mult).then_inc(S["a_ready"], 1)

                form_x(0, 0)

                def step(t, k):
                    if live(t + 1) and not (isinstance(t, int) and t + 1 >= STEPS):
                        form_x(t + 1, 1 - k)
                    if live(t - 1):
                        normalise(t - 1, 1 - k)

                pipeline(pool, step, 1)

        @block.scalar
        def _(act):
            link = chain(act, "act_link")
            act.wait_ge(S["dve_link"], 3)
            act.wait_ge(S["lnv"], 1)
            nc.scalar.activation(rstd[:, :], mv[:, :, 1], ACT.Sqrt, bias=eps_col[:, 0:1]).then_inc(S["lnq"], 1)
            def count(j, i4):
                act.wait_ge(S["cmp_ready"], j + 1)
                for nt in (0, 1):
                    ins = nc.scalar.activation(bank[i4 + nt][:, :], bank[i4 + nt][:, :], ACT.Sign,
                                               accum_out=counts[:, bass.ds(NT * j + nt, 1)])
                ins.then_inc(S["act_counted"], 1)

            with act.Fori(0, M * B // 2) as i:
                count(2 * i, 0)
                count(2 * i + 1, 4)
            for l in range(2):
                O = OUTS[l]
                act.wait_ge(S["folded"], 2 * l + 1)
                wv = bank[0][:, 0:O]
                link(nc.scalar.activation(cen32[:, 0:O], wv, ACT.Copy, scale=W_SCALE))
                link(nc.scalar.copy(wv_hi[l][:, :], cen32[:, 0:O]))
                link(nc.scalar.activation(cen32[:, 128:128 + O], wv_hi[l][:, :], ACT.Copy))
                act.wait_ge(S["folded"], 2 * l + 2)
                for b in range(BH):
                    nc.scalar.copy(wcen[l][C * b:C * b + C, O * b:O * b + O], bank[1][C * b:C * b + C, 0:O])
                    nc.scalar.mul(wdif[l][C * b:C * b + C, O * b:O * b + O], bank[1][C * b:C * b + C, 64:64 + O], -1.0)
                nc.scalar.copy(bias[l][:, :], bank[1][:, 128:129]).then_inc(S["fold_taken"], 1)

            act.wait_ge(S["fold_taken"], 4)
            for p, (u, l) in enumerate(PASSES):
                O = OUTS[l]
                base = STEPS * p
                F = FX[:, u, :] if l == 0 else F1[:, :]
                act.wait_ge(S["fT_psum"], p + 1)
                nc.scalar.copy(fT[:, 0, :], bank[2][:, :]).then_inc(S["fT_hi"], 1)
                features_ready(act, u, l)
                if p:
                    act.wait_ge(S["y_psum"], STEPS * p)
                link(nc.scalar.copy(cen16[:, :], F))
                nc.scalar.copy(cen32[:, :], cen16[:, :]).then_inc(S["cen_done"], 1)
                for b in range(BH):
                    act.wait_ge(S["sorted_psum"], BH * p + b + 1)
                    if b == 0:
                        act.wait_ge(S["zeroed"], 3)
                        if p:
                            act.wait_ge(S["x_ready"], STEPS * p)
                            act.wait_ge(S["v_psum"], STEPS * p)
                    nc.scalar.copy(Sx[:, b, LEFT:LEFT + N], bank[4 + b][:, :]).then_inc(S["sorted_sb"], 1)
                    act.wait_ge(S["sorted_sb"], 8 * p + 2 * b + 1)
                    nc.scalar.copy(Sx[:, b, LEFT + N:LEFT + N + 4],
                                   window(Sx[:, b, :], LEFT + N - 1, 1, [[0, 4]])).then_inc(S["sorted_sb"], 1)
                    act.wait_ge(S["sorted_sb"], 8 * p + 2 * b + 2)
                    for h in range(HEADS):
                        ins = nc.scalar.activation(khi[:, b, h::HEADS], Sx[:, b, :], ACT.Copy, scale=headmask[:, h:h + 1])
                    ins.then_inc(S["key_hi"], 1)
                act.wait_ge(S["z_psum"], p + 1)
                for g in range(l + 1):
                    ins = nc.scalar.activation(z[:, g, 0:N], bank[g][:, :], ACT.Identity, bias=bias[l][:, 0:1])
                ins.then_inc(S["z_ready"], 1)

                def step(t, k):
                    s = base + t
                    if live(t):
                        act.wait_ge(S["d_ready"], s + 1)
                        freed(act, s, "a_ready")
                        nc.scalar.activation(ex[0:ROWS, k, :], dif[0:ROWS, k, :], ACT.Exp,
                                             scale=HEAD_SCALE).then_inc(S["e_ready"], 1)
                    if live(t - 2):
                        act.wait_ge(S["aT_psum"], s - 1)
                        freed(act, s - 2, "y_psum")
                        nc.scalar.copy(atT[:, k, :], bank[2 + k][0:COLS, 0:BH * ROWS]).then_inc(S["aT_sb"], 1)
                        act.wait_ge(S["v_psum"], s - 1)
                        nc.scalar.activation(val[:, k, 0:BH * O], bank[4 + k][0:COLS, 0:BH * O], ACT.Copy,
                                             scale=1.0 / W_SCALE).then_inc(S["v_sb"], 1)

                pipeline(act, step, 2)
                act.wait_ge(S["stat_var"], p + 1)
                nc.scalar.activation(rstd[:, 0:l + 1], mv[:, 0:l + 1, 1], ACT.Sqrt, bias=eps_col[:, 0:1])\
                    .then_inc(S["stat_sqrt"], 1)
                if l == 1:
                    act.wait_ge(S["lnv"], 2 + u)
                    nc.scalar.activation(rstd[:, 0:1], mv[:, 0:1, 1], ACT.Sqrt, bias=eps_col[:, 0:1]).then_inc(S["lnq"], 1)

            for u in range(HALVES):
                act.wait_ge(S["lnv"], 4 + 2 * u)
                nc.scalar.activation(rstd[:, 0:1], mv[:, 0:1, 1], ACT.Sqrt, bias=eps_col[:, 0:1]).then_inc(S["lnq"], 1)
                for a in range(2):
                    act.wait_ge(S["att_T"], 2 * u + a + 1)
                    nc.scalar.copy(qkT[:, 4 * a:4 * a + 4, :], bank[a][:, :].rearrange("p (a n) -> p a n", a=4))\
                        .then_inc(S["att_Tc"], 1)
                act.wait_ge(S["att_sc"], u + 1)
                nc.scalar.activation(sg[:, :, :], bank[2][:, :].rearrange("p (a n) -> p a n", a=4), ACT.Sigmoid,
                                     scale=4.0 * 128 ** -0.5).then_inc(S["att_sg"], 1)
                act.wait_ge(S["lnv"], 5 + 2 * u)
                nc.scalar.activation(rstd[:, 0:1], mv[:, 0:1, 1], ACT.Sqrt, bias=eps_col[:, 0:1]).then_inc(S["lnq"], 1)
            for u in range(HALVES):
                act.wait_ge(S["ffn_T"], u + 1)
                nc.scalar.copy(xnT[:, :, 128 * u:128 * u + 128], bank[4 + u][:, :].rearrange("p (a n) -> p a n", a=4))\
                    .then_inc(S["ffn_Tc"], 1)
            for m in range(4):
                act.wait_ge(S["ffn_h"], m + 1)
                nc.scalar.activation(gate[:, m, :], bank[m][:, 0:256], ACT.Silu, bias=b12[:, m:m + 1]).then_inc(S["ffn_g"], 1)

        @block.tensor
        def _(pe):
            pe.wait_ge(S["chunk_in"], 16 * 4)
            pe.wait_ge(S["ones"], 16 * 6)

            def compare(j, i4):
                if not isinstance(j, int) or j >= 2:
                    pe.wait_ge(S["act_counted"], j - 1)
                    pe.wait_ge(S["dve_counted"], j - 1)
                for nt in range(NT):
                    o = bank[i4 + nt][:, :]
                    a = N * j
                    nc.tensor.matmul(o, sl(LA, a + 128 * nt, 128), sl(RA, a, N), start=True, stop=False)
                    ins = nc.tensor.matmul(o, sl(LB, a + 128 * nt, 128), sl(RB, a, N), start=False, stop=True)
                ins.then_inc(S["cmp_ready"], 1)

            compare(0, 0)
            compare(1, 4)
            with pe.Fori(1, M * B // 2) as i:
                compare(2 * i, 0)
                compare(2 * i + 1, 4)
            pe.wait_ge(S["act_counted"], M * B)
            pe.wait_ge(S["dve_counted"], M * B)

            pe.wait_ge(S["weights"], 16 * NWEIGHTS)
            pe.wait_ge(S["consts"], 16 * 5)
            pe.wait_ge(S["masks"], 16 * 3)
            for l in range(2):
                O = OUTS[l]
                if l:
                    pe.wait_ge(S["fold_taken"], 2 * l)
                for m in range(M):
                    slot = PERMS[l].index(m)
                    ins = nc.tensor.matmul(bank[0][C * m:C * m + C, 0:O], wlin[l][:, 4 * C + slot:8 * C:4],
                                           wconvT[l][:, 0:O], start=True, stop=True)
                ins.then_inc(S["folded"], 1)
                for b in range(BH):
                    for kind in range(2):
                        for slot in range(M):
                            nc.tensor.matmul(bank[1][C * b:C * b + C, 64 * kind:64 * kind + O],
                                             wlin[l][:, 4 * C * kind + slot:4 * C * (kind + 1):4],
                                             wconvT[l][:, 0:O], start=(slot == 0), stop=(slot == M - 1))
                ins = nc.tensor.matmul(bank[1][:, 128:129], wconvT[l][:, :], blin[l][:, :], start=True, stop=True)
                ins.then_inc(S["folded"], 1)
            pe.wait_ge(S["fold_taken"], 4)

            for p, (u, l) in enumerate(PASSES):
                O = OUTS[l]
                base = STEPS * p
                F = FX[:, u, :] if l == 0 else F1[:, :]
                features_ready(pe, u, l)
                if p:
                    pe.wait_ge(S["ymax_done"], STEPS * p)
                    if l == 0:
                        pe.wait_ge(S["h3_done"], u)
                for nt in range(NT):
                    ins = nc.tensor.transpose(bank[2][:, 128 * nt:128 * nt + 128], F[:, 128 * nt:128 * nt + 128],
                                              ident[:, :])
                ins.then_inc(S["fT_psum"], 1)
                pe.wait_ge(S["fT_lo"], p + 1)
                pe.wait_ge(S["fT_hi"], p + 1)
                pe.wait_ge(S["onehot"], u + 1)
                for b in range(BH):
                    for nt in range(NT):
                        for part in range(2):
                            for m in range(M):
                                ins = nc.tensor.matmul(bank[4 + b][C * m:C * m + C, :],
                                                       fT[:, part, 128 * nt + C * b:128 * nt + C * b + C],
                                                       perm[:, (m * BH + b) * NT + nt, :],
                                                       start=(nt == 0 and part == 0), stop=(nt == NT - 1 and part == 1))
                    ins.then_inc(S["sorted_psum"], 1)
                pe.wait_ge(S["cen_done"], p + 1)
                for g in range(l + 1):
                    w = slice(128 * g, 128 * g + 128)
                    nc.tensor.matmul(bank[g][:, :], wcen[l][:, w], cen32[:, :], start=True, stop=False)
                    ins = nc.tensor.matmul(bank[g][:, :], wdif[l][:, w], F, start=False, stop=True)
                ins.then_inc(S["z_psum"], 1)
                pe.wait_ge(S["key_hi"], BH * (p + 1))
                pe.wait_ge(S["key_lo"], BH * (p + 1))
                pe.wait_ge(S["z_ready"], p + 1)

                def scores(t, k):
                    s = base + t
                    edge = isinstance(t, int) and t == 0
                    freed(pe, s, "d_ready")
                    sc = bank[k][0:ROWS, 0:BH * COLS]
                    rows = 3 * G if edge else G
                    msk = (edge_mask if edge else inner_mask)[:, :]
                    msk = bass.AP(msk.tensor, msk.offset, [msk.ap[0], [0, BH], [1, SPAN], [0, HEADS]])
                    nc.tensor.matmul(sc, rows_ind[0:rows, :], msk, start=True, stop=False, skip_group_check=True)
                    pe.wait_ge(S["x_ready"], s + 1)
                    for b in range(BH):
                        for keys in (khi, klo):
                            ins = nc.tensor.matmul(sc[:, COLS * b:COLS * b + COLS], xq[:, k, ROWS * b:ROWS * b + ROWS],
                                                   keys[:, b, bass.ds(HEADS * G * t, COLS)], start=False,
                                                   stop=True, skip_group_check=True)
                    ins.then_inc(S["sc_ready"], 1)

                def values(t, k):
                    s = base + t
                    freed(pe, s, "v_sb")
                    for b in range(BH):
                        o = bank[4 + k][0:COLS, O * b:O * b + O]
                        hi, lo = (keys[:, b, bass.ds(HEADS * G * t, COLS)] for keys in (khi, klo))
                        nc.tensor.matmul(o, hi, wv_hi[l][:, :], start=True, stop=False)
                        nc.tensor.matmul(o, hi, wv_lo[l][:, :], start=False, stop=False)
                        ins = nc.tensor.matmul(o, lo, wv_hi[l][:, :], start=False, stop=True)
                    ins.then_inc(S["v_psum"], 1)

                def turn(t, k):
                    s = base + t
                    pe.wait_ge(S["a_ready"], s + 1)
                    freed(pe, s, "aT_sb")
                    for b in range(BH):
                        ins = nc.tensor.transpose(bank[2 + k][0:COLS, ROWS * b:ROWS * b + ROWS],
                                                  at[0:ROWS, k, COLS * b:COLS * b + COLS], ident[0:ROWS, 0:ROWS])
                    ins.then_inc(S["aT_psum"], 1)

                def products(t, k):
                    s = base + t
                    pe.wait_ge(S["aT_sb"], s + 1)
                    pe.wait_ge(S["v_sb"], s + 1)
                    freed(pe, s, "ys_done")
                    for b in range(BH):
                        r, c = (C * b, 0) if l == 0 else (64 * (b % 2), ROWS * (b // 2))
                        ins = nc.tensor.matmul(bank[6 + k][r:r + O, c:c + ROWS], val[:, k, O * b:O * b + O],
                                               atT[:, k, ROWS * b:ROWS * b + ROWS], start=True, stop=True,
                                               skip_group_check=True)
                    ins.then_inc(S["y_psum"], 1)

                def step(t, k):
                    if live(t):
                        scores(t, k)
                    if live(t - 2):
                        turn(t - 2, k)
                        values(t - 2, k)
                    if live(t - 3):
                        products(t - 3, 1 - k)

                pipeline(pe, step, 3)
                if l == 1:
                    pe.wait_ge(S["f2_ready"], u + 1)
                    nc.tensor.matmul(bank[0][:, :], w3bd[:, 0, :], FX[:, u, :], start=True, stop=False)
                    nc.tensor.matmul(bank[0][:, :], w3bd[:, 1, :], F1[:, :], start=False, stop=False)
                    nc.tensor.matmul(bank[0][:, :], w3bd[:, 2, :], F2[:, 0, :], start=False, stop=False)
                    nc.tensor.matmul(bank[0][:, :], w3bd[:, 3, :], F2[:, 1, :], start=False, stop=True)\
                        .then_inc(S["h3_psum"], 1)

            for u in range(HALVES):
                pe.wait_ge(S["att_in"], u + 1)
                for a in range(2):
                    for h in range(4):
                        ins = nc.tensor.transpose(bank[a][:, 128 * h:128 * h + 128], qkv[:, a, 128 * h:128 * h + 128],
                                                  ident[:, :])
                    ins.then_inc(S["att_T"], 1)
                pe.wait_ge(S["att_Tc"], 2 * u + 2)
                for h in range(4):
                    ins = nc.tensor.matmul(bank[2][:, 128 * h:128 * h + 128], qkT[:, 4 + h, :], qkT[:, h, :],
                                           start=True, stop=True)
                ins.then_inc(S["att_sc"], 1)
                pe.wait_ge(S["att_m"], u + 1)
                for h in range(4):
                    ins = nc.tensor.matmul(bank[3][:, 128 * h:128 * h + 128], sgm[:, h, :],
                                           qkv[:, 2, 128 * h:128 * h + 128], start=True, stop=True)
                ins.then_inc(S["att_o"], 1)
                pe.wait_ge(S["ffn_x"], u + 1)
                for c in range(4):
                    ins = nc.tensor.transpose(bank[4 + u][:, 128 * c:128 * c + 128], xn[:, u, 128 * c:128 * c + 128],
                                              ident[:, :])
                ins.then_inc(S["ffn_T"], 1)
            pe.wait_ge(S["ffn_Tc"], 2)
            pe.wait_ge(S["ffn_w"], 32)
            for m in range(4):
                for half in range(2):
                    for c in range(4):
                        col = 128 * (m + 4 * half)
                        ins = nc.tensor.matmul(bank[m + 4 * half][:, 0:256], w12T[:, c, col:col + 128], xnT[:, c, :],
                                               start=(c == 0), stop=(c == 3))
                ins.then_inc(S["ffn_h"], 1)
            pe.wait_ge(S["ffn_x4"], 4)
            for u in range(HALVES):
                for c in range(4):
                    ins = nc.tensor.matmul(bank[u][:, :], x4T[:, c, 128 * u:128 * u + 128], w3T[:, c, :],
                                           start=(c == 0), stop=(c == 3))
                ins.then_inc(S["ffn_o"], 1)

        @block.vector
        def _(dve):
            v = nc.vector
            link = chain(dve, "dve_link")
            for l in range(2):
                v.memset(wcen[l][:, :], 0.0)
                link(v.memset(wdif[l][:, :], 0.0))
            link(v.memset(eps_col[:, :], EPS))

            c1 = lambda i: cs[:, i:i + 1]
            dve.wait_ge(S["coords"], 48)
            link(v.tensor_reduce(c1(0), crd[:, :], AX.X, ALU.min))
            link(v.tensor_reduce(c1(1), crd[:, :], AX.X, ALU.max))
            link(v.tensor_tensor(c1(2), c1(1), c1(0), ALU.subtract))
            link(v.tensor_scalar(c1(2), c1(2), 1e-6, None, ALU.add))
            top = float(2 ** BITS - 1)
            link(v.reciprocal(c1(3), c1(2)))
            link(v.tensor_scalar(c1(4), c1(3), top, None, ALU.mult))
            for src, hi, lo in ((2, 5, 6), (4, 7, 8)):
                link(v.tensor_scalar(c1(9), c1(src), 4097.0, None, ALU.mult))
                link(v.tensor_tensor(c1(10), c1(9), c1(src), ALU.subtract))
                link(v.tensor_tensor(c1(hi), c1(9), c1(10), ALU.subtract))
                link(v.tensor_tensor(c1(lo), c1(src), c1(hi), ALU.subtract))
            link(v.tensor_tensor(c1(11), c1(5), c1(7), ALU.mult))
            link(v.tensor_scalar(c1(11), c1(11), -1.0, top, ALU.mult, ALU.add))
            for x, y in ((5, 8), (6, 7), (6, 8)):
                link(v.tensor_tensor(c1(12), c1(x), c1(y), ALU.mult))
                link(v.tensor_tensor(c1(11), c1(11), c1(12), ALU.subtract))
            link(v.tensor_tensor(c1(12), c1(11), c1(3), ALU.mult))
            link(v.tensor_tensor(c1(4), c1(4), c1(12), ALU.add))
            link(v.tensor_scalar(crd[:, :], crd[:, :], c1(0), None, ALU.subtract))
            link(v.tensor_scalar(crd[:, :], crd[:, :], c1(4), None, ALU.mult))
            link(v.tensor_copy(crq[:, :], crd[:, :]))
            link(v.tensor_copy(crf[:, :], crq[:, :]))
            link(v.tensor_tensor(crd[:, :], crf[:, :], crd[:, :], ALU.is_gt))
            link(v.tensor_tensor(crf[:, :], crf[:, :], crd[:, :], ALU.subtract))
            v.tensor_scalar(crq[:, :], crf[:, :], 0.0, top, ALU.max, ALU.min).then_inc(S["coords_scaled"], 1)

            dve.wait_ge(S["x_in"], 32)

            def norm_stats(src, i):
                link(v.bn_stats(bst[:, i, 0, :], src))
                return v.bn_aggr(mv[:, i, :], bst[:, i, 0, :])

            link(norm_stats(X[:, 0, :], 0))
            norm_stats(X[:, 1, :], 1).then_inc(S["lnv"], 1)
            dve.wait_ge(S["lnq"], 1)
            link(v.reciprocal(rstd[:, :], rstd[:, :]))
            for u in range(HALVES):
                ins = v.tensor_scalar(FX[:, u, :], X[:, u, :], mv[:, u, 0:1], rstd[:, u:u + 1], ALU.subtract, ALU.mult)
            ins.then_inc(S["f0_ready"], 1)

            dve.wait_ge(S["q_in"], 16)
            for a, order in ((0, (0, 1, 2)), (1, (1, 0, 2))):
                for w in range(3):
                    v.tensor_copy(XK[:, w, a, :], Q3[:, order[w], :])
                    ins = v.tensor_copy(XK[:, w, 2 + a, :], Q3[:, order[w], :])
            link(ins)
            H = [XK[:, w, 2:4, :].rearrange("p a j -> p (a j)") for w in range(3)]
            t1, t2, t3, t4 = (T1[:, i, 0:2, :].rearrange("p a j -> p (a j)") for i in (0, 1, 2, 0))
            t4 = T2[:, 0, 0:2, :].rearrange("p a j -> p (a j)")
            SHL, SHR, SAR = ALU.logical_shift_left, ALU.logical_shift_right, ALU.arith_shift_right
            AND, OR, XOR = ALU.bitwise_and, ALU.bitwise_or, ALU.bitwise_xor
            for bit in range(BITS - 1, 0, -1):
                low = (1 << bit) - 1
                link(v.tensor_scalar(t1, H[0], 31 - bit, 31, SHL, SAR))
                link(v.scalar_tensor_tensor(H[0], t1, low, H[0], AND, XOR))
                for w in (1, 2):
                    v.tensor_scalar(t1, H[w], 31 - bit, 31, SHL, SAR)
                    link(v.tensor_tensor(t2, H[0], H[w], XOR))
                    link(v.tensor_tensor(t3, t2, t1, OR))
                    v.scalar_tensor_tensor(H[0], t3, low, H[0], AND, XOR)
                    link(v.tensor_tensor(t4, t3, t1, XOR))
                    link(v.scalar_tensor_tensor(H[w], t4, low, H[w], AND, XOR))
            link(v.tensor_tensor(H[1], H[1], H[0], XOR))
            link(v.tensor_tensor(H[2], H[2], H[1], XOR))
            link(v.tensor_scalar(t1, H[2], 1, None, SHR))
            for sh in (1, 2, 4, 8):
                link(v.scalar_tensor_tensor(t2, t1, sh, t1, SHR, XOR))
                link(v.tensor_copy(t1, t2))
            for w in range(3):
                ins = v.tensor_tensor(H[w], H[w], t1, XOR)
            link(ins)
            xk, s1, s2 = (T[:, :, :, :].rearrange("p w a j -> p (w a j)") for T in (XK, T1, T2))
            for sh, keep in ((16, 0x030000FF), (8, 0x0300F00F), (4, 0x030C30C3), (2, 0x09249249)):
                link(v.scalar_tensor_tensor(s1, xk, sh, xk, SHL, OR))
                link(v.tensor_scalar(xk, s1, keep, None, AND))
            word = [XK[:, w, :, :].rearrange("p a j -> p (a j)") for w in range(3)]
            k1 = T1[:, 0, :, :].rearrange("p a j -> p (a j)")
            key = T2[:, 0, :, :].rearrange("p a j -> p (a j)")
            link(v.scalar_tensor_tensor(k1, word[0], 1, word[1], SHL, OR))
            link(v.scalar_tensor_tensor(key, k1, 1, word[2], SHL, OR))
            dve.wait_ge(S["consts"], 16 * 5)
            link(v.tensor_scalar(T3[:, 0, :], key, 127, 1, AND, SHL))
            link(v.tensor_tensor(T3[:, 0, :], T3[:, 0, :], nhigh[:, :], OR))
            v.tensor_scalar(T3[:, 1, :], key, 7, 255, SHR, AND)
            v.tensor_scalar(T3[:, 2, :], key, 15, 255, SHR, AND)
            link(v.tensor_scalar(T3[:, 3, :], key, 23, None, SHR))
            for j in range(4):
                ins = v.tensor_scalar(chunks[:, j, :], T3[:, j, :], float(2 ** (8 * j + 8)), None, ALU.mult)
            ins.then_inc(S["chunks_done"], 1)

            def count(j, i4):
                dve.wait_ge(S["cmp_ready"], j + 1)
                for nt in (2, 3):
                    ins = v.tensor_scalar(bank[i4 + nt][:, :], bank[i4 + nt][:, :], 0.0, 0.0, ALU.is_lt, ALU.add,
                                          accum_out=ranks[:, bass.ds(NT * j + nt, 1)])
                ins.then_inc(S["dve_counted"], 1)

            with dve.Fori(0, M * B // 2) as i:
                count(2 * i, 0)
                count(2 * i + 1, 4)
            dve.wait_ge(S["act_counted"], M * B)
            dve.wait_ge(S["dve_counted"], M * B)
            cv = counts[:, :].rearrange("p (j t) -> p j t", t=NT)
            rv = ranks[:, :].rearrange("p (j t) -> p j t", t=NT)
            v.tensor_scalar(rv[:, :, 0:2], cv[:, :, 0:2], -0.5, 0.5 * (N - 1), ALU.mult, ALU.add)\
                .then_inc(S["ranked"], 1)
            dve.wait_ge(S["ranked"], 1)

            for l in range(2):
                O = OUTS[l]
                dve.wait_ge(S["act_link"], 3 * l + 3)
                v.tensor_tensor(wv_lo[l][:, :], cen32[:, 0:O], cen32[:, 128:128 + O], ALU.subtract)\
                    .then_inc(S["fold_taken"], 1)

            for p, (u, l) in enumerate(PASSES):
                base = STEPS * p
                if l == 0:
                    for m in range(M):
                        for b in range(BH):
                            for nt in range(NT):
                                r = (m * B + BH * u + b) * NT + nt
                                ins = v.tensor_scalar(perm[:, (m * BH + b) * NT + nt, :], iota[:, :],
                                                      ranks[:, r:r + 1], None, ALU.is_equal)
                    ins.then_inc(S["onehot"], 1)
                dve.wait_ge(S["fT_hi"], p + 1)
                v.tensor_tensor(fT[:, 1, :], bank[2][:, :], fT[:, 0, :], ALU.subtract).then_inc(S["fT_lo"], 1)
                for b in range(BH):
                    dve.wait_ge(S["key_hi"], BH * p + b + 1)
                    for h in range(HEADS):
                        ins = v.scalar_tensor_tensor(klo[:, b, h::HEADS], Sx[:, b, :], headmask[:, h:h + 1], khi[:, b, h::HEADS],
                                                     ALU.mult, ALU.subtract)
                    ins.then_inc(S["key_lo"], 1)
                dve.wait_ge(S["z_ready"], p + 1)

                def softmax_in(t, k):
                    s = base + t
                    sc = by_head(bank[k][0:ROWS, 0:BH * COLS])
                    dve.wait_ge(S["sc_ready"], s + 1)
                    v.tensor_reduce(heads(mx[0:ROWS, k, :]), sc, AX.X, ALU.max).then_inc(S["mx_done"], 1)
                    dve.wait_ge(S["mx_done"], s + 1)
                    freed(dve, s, "e_ready")
                    v.tensor_tensor(by_head(dif[0:ROWS, k, :]), sc,
                                    spread(heads(mx[0:ROWS, k, :]), SPAN), ALU.subtract).then_inc(S["d_ready"], 1)

                def softmax_sum(t, k):
                    s = base + t
                    dve.wait_ge(S["e_ready"], s + 1)
                    v.tensor_reduce(heads(sm[0:ROWS, k, :]), by_head(ex[0:ROWS, k, :]),
                                    AX.X, ALU.add).then_inc(S["sum_done"], 1)
                    dve.wait_ge(S["sum_done"], s + 1)
                    freed(dve, s, "a_ready")
                    v.reciprocal(rs[0:ROWS, k, :], sm[0:ROWS, k, :]).then_inc(S["r_ready"], 1)

                def outputs(t, k):
                    s = base + t
                    w = ROWS * (l + 1)
                    dve.wait_ge(S["y_psum"], s + 1)
                    freed(dve, s, "ymax_done")
                    zz = window(z[:, 0, :], G * t, 1, [[NPAD, l + 1], [1, G], [0, K]])
                    v.tensor_tensor(ys[:, k, 0:w].rearrange("p (g n i) -> p g n i", g=l + 1, n=G),
                                    bank[6 + k][:, 0:w].rearrange("p (g n i) -> p g n i", g=l + 1, n=G),
                                    zz, ALU.add).then_inc(S["ys_done"], 1)
                    dve.wait_ge(S["ys_done"], s + 1)
                    real = LAST_ROWS if isinstance(t, int) and t == STEPS - 1 else ROWS
                    for g in range(l + 1):
                        v.bn_stats(bst[:, g, bass.ds(t, 1), :], ys[:, k, ROWS * g:ROWS * g + real])
                    v.tensor_reduce(ymax[:, 0:l + 1, bass.ds(G * t, G)],
                                    ys[:, k, 0:w].rearrange("p (g n i) -> p g n i", g=l + 1, n=G),
                                    AX.X, ALU.max).then_inc(S["ymax_done"], 1)

                def step(t, k):
                    if live(t):
                        softmax_in(t, k)
                    if live(t - 1):
                        softmax_sum(t - 1, 1 - k)
                    if live(t - 4):
                        outputs(t - 4, k)

                pipeline(dve, step, 4)
                dve.wait_ge(S["ymax_done"], base + STEPS)
                for g in range(l + 1):
                    ins = v.bn_aggr(mv[:, g, :], bst[:, g, :, :].rearrange("p a b -> p (a b)"))
                ins.then_inc(S["stat_var"], 1)
                dve.wait_ge(S["stat_sqrt"], p + 1)
                link(v.reciprocal(rstd[:, 0:l + 1], rstd[:, 0:l + 1]))
                for g in range(l + 1):
                    link(v.tensor_scalar(ymax[:, g, 0:N], ymax[:, g, 0:N], mv[:, g, 0:1], rstd[:, g:g + 1],
                                         ALU.subtract, ALU.mult))
                    dst = F1[:, :] if l == 0 else F2[:, g, :]
                    ins = v.scalar_tensor_tensor(dst, ymax[:, g, 0:N], 0.2, ymax[:, g, 0:N], ALU.mult, ALU.max)
                if l == 0:
                    ins.then_inc(S["f1_ready"], 1)
                    continue
                ins.then_inc(S["f2_ready"], 1)
                dve.wait_ge(S["h3_psum"], u + 1)
                link(v.bn_stats(bst[:, 0, 0, :], bank[0][:, :]))
                v.bn_aggr(mv[:, 0, :], bst[:, 0, 0, :]).then_inc(S["lnv"], 1)
                dve.wait_ge(S["lnq"], 2 + u)
                link(v.reciprocal(rstd[:, 0:1], rstd[:, 0:1]))
                link(v.tensor_scalar(ymax[:, 0, 0:N], bank[0][:, :], mv[:, 0, 0:1], rstd[:, 0:1], ALU.subtract, ALU.mult))
                link(v.scalar_tensor_tensor(ymax[:, 1, 0:N], ymax[:, 0, 0:N], 0.2, ymax[:, 0, 0:N], ALU.mult, ALU.max))
                v.tensor_tensor(X[:, u, :], X[:, u, :], ymax[:, 1, 0:N], ALU.add).then_inc(S["h3_done"], 1)
            dve.wait_ge(S["h3_done"], 2)

            dve.wait_ge(S["bind_in"], 48)
            wb = bind[:, :, :].rearrange("p a (h e) -> p (a h) e", h=4)
            sb3 = sgb[:, :, :].rearrange("p a (h e) -> p (a h) e", h=4)
            link(v.tensor_reduce(alpha[:, :], wb, AX.X, ALU.add, apply_absolute_value=True))
            link(v.tensor_scalar(alpha[:, :], alpha[:, :], 1.0 / 128, None, ALU.mult))
            link(v.tensor_scalar(sb3, wb, 0.0, 2.0, ALU.is_ge, ALU.mult))
            link(v.tensor_scalar(sb3, sb3, -1.0, None, ALU.add))
            link(v.tensor_tensor(sb3, sb3, spread(alpha[:, :], 128), ALU.mult))
            link(v.tensor_tensor(sb3, sb3, wb, ALU.subtract))
            link(v.tensor_tensor(wb, sb3, wb, ALU.add))

            for u in range(HALVES):
                def layernorm(src, dst, n):
                    link(v.bn_stats(bst[:, 0, 0, :], src))
                    v.bn_aggr(mv[:, 0, :], bst[:, 0, 0, :]).then_inc(S["lnv"], 1)
                    dve.wait_ge(S["lnq"], n)
                    link(v.reciprocal(rstd[:, 0:1], rstd[:, 0:1]))
                    return v.tensor_scalar(dst, src, mv[:, 0, 0:1], rstd[:, 0:1], ALU.subtract, ALU.mult)

                link(layernorm(X[:, u, :], xn[:, u, :], 4 + 2 * u))
                for a in range(3):
                    ins = v.tensor_tensor(qkv[:, a, :], xn[:, u, :], bind[:, a, :], ALU.mult)
                ins.then_inc(S["att_in"], 1)
                dve.wait_ge(S["att_sg"], u + 1)
                mask = window(causal, 0, 128, [[0, 4], [1, 128]])
                v.tensor_tensor(sgm[:, :, :], sg[:, :, :], mask, ALU.mult).then_inc(S["att_m"], 1)
                dve.wait_ge(S["att_o"], u + 1)
                link(v.tensor_tensor(X[:, u, :], bank[3][:, :], X[:, u, :], ALU.add))
                layernorm(X[:, u, :], xn[:, u, :], 5 + 2 * u).then_inc(S["ffn_x"], 1)
                dve.wait_ge(S["ffn_x"], u + 1)
                link(v.tensor_tensor(res[:, u, :], X[:, u, :], b3row[:, :], ALU.add))
            for m in range(4):
                dve.wait_ge(S["ffn_g"], m + 1)
                v.scalar_tensor_tensor(x4T[:, m, :], bank[4 + m][:, 0:256], b12[:, 4 + m:5 + m], gate[:, m, :],
                                       ALU.add, ALU.mult).then_inc(S["ffn_x4"], 1)
            for u in range(HALVES):
                dve.wait_ge(S["ffn_o"], u + 1)
                v.tensor_tensor(outb[:, u, :], bank[u][:, :], res[:, u, :], ALU.add).then_inc(S["out_ready"], 1)


def kernel(**inputs):
    import concourse.bacc as bacc
    from concourse.bass_utils import run_bass_kernel_spmd

    pre = "L0_"
    arrays = {
        "x": inputs["x"], "ctx_4096": inputs["ctx_4096"],
        "wl0": inputs[pre + "xattn_W_lin1"], "wl1": inputs[pre + "xattn_W_lin2"],
        "bl0": inputs[pre + "xattn_b_lin1"], "bl1": inputs[pre + "xattn_b_lin2"],
        "wc0T": np.transpose(inputs[pre + "xattn_W_conv1"]), "wc1T": np.transpose(inputs[pre + "xattn_W_conv2"]),
        "w3cT": np.transpose(inputs[pre + "xattn_W_conv3"]),
        "bv_q": inputs[pre + "attn_bv_q"], "bv_k": inputs[pre + "attn_bv_k"], "bv_v": inputs[pre + "attn_bv_v"],
        "w12T": np.transpose(inputs[pre + "ffn_w12"]), "b12": np.transpose(np.reshape(inputs[pre + "ffn_b12"], (8, 128))),
        "w3T": np.transpose(inputs[pre + "ffn_w3"]), "b3": inputs[pre + "ffn_b3"],
        **constants(),
    }
    arrays = {f"in_{k}": np.ascontiguousarray(v) for k, v in arrays.items()}
    nc = bacc.Bacc("TRN2", target_bir_lowering=False, num_devices=1)
    d = {k[3:]: nc.dram_tensor(k, a.shape, mybir.dt.from_np(a.dtype), kind="ExternalInput").ap()
         for k, a in arrays.items()}
    d["out"] = nc.dram_tensor("out", (B, C, N), F32, kind="ExternalOutput").ap()
    build(nc, d)
    result = run_bass_kernel_spmd(nc, [arrays], core_ids=[0])
    return result.results[0]["out"]
```

```python
from contextlib import ExitStack
from math import log, sqrt

import numpy as np

import concourse.bass as bass
from concourse import mybir
from concourse.alu_op_type import AluOpType as ALU

ACT = mybir.ActivationFunctionType
AX = mybir.AxisListType
F32 = mybir.dt.float32
F16 = mybir.dt.float16
BF16 = mybir.dt.bfloat16
I32 = mybir.dt.int32

B, C, N = 8, 32, 512
BH = 4
HALVES = B // BH
M = 4
K = 10
HEADS = 4
BITS = 10
NT = N // 128
CMP = 2 * B + BH
EPS = 1e-5

G = 12
ROWS = G * K
SPAN = G + K - 1
COLS = HEADS * SPAN
STEPS = -(-N // G)
NPAD = STEPS * G
LEFT = K // 2
SW = 528
HEAD_SCALE = 1.0 / sqrt(32.0)
W_SCALE = 1024.0
PERMS = ([2, 0, 3, 1], [1, 3, 0, 2])
OUTS = (32, 64)
LAST_ROWS = (N - (STEPS - 1) * G) * K


def constants():
    def short(a):
        return (a.astype(np.float32).view(np.uint32) & np.uint32(0xFFFF0000)).view(np.float32)

    def pairs(a):
        w = a.astype(np.float32).view(np.uint32) >> np.uint32(16)
        return (w[:, 0::2] | (w[:, 1::2] << np.uint32(16))).view(np.int32)

    n, p = np.arange(G)[:, None], np.arange(SPAN)[None, :]
    far = float(short(np.array(-1e30)))
    inner = np.where((p >= n) & (p <= n + K - 1), 0.0, far)
    edge = np.where(p < LEFT, far, inner)
    for i in range(LEFT):
        edge[i, i + K] = sqrt(32.0) * log(LEFT - i)
    parts, rest = [], edge.astype(np.float64)
    for _ in range(3):
        part = short(rest)
        rest = np.where(edge == far, 0.0, rest - part.astype(np.float64))
        parts.append(part)
    edge3 = np.concatenate(parts, 0)
    ind = np.repeat(np.eye(G), K, axis=1)
    q = np.arange(128)
    s, t = q[:, None], q[None, :]
    return {
        "c_ident": np.eye(128, dtype=np.float32),
        "c_rows": np.concatenate([ind] * 3, 0).astype(np.float32),
        "c_inner": inner.astype(np.float32),
        "c_edge": edge3.astype(np.float32),
        "c_headmask": ((q[:, None] % C) // 8 == np.arange(HEADS)).astype(np.float32),
        "c_iota": np.tile(np.arange(N, dtype=np.float16), (128, 1)),
        "c_causal": ((s // C == t // C) & (s <= t)).astype(np.float32),
        "c_key_rows": pairs(np.stack([np.ones(CMP * N), -np.ones(CMP * N), np.tile(np.arange(N) % 256, CMP)])),
        "c_to_points": (np.eye(3)[:, None, :, None] * (q // 16 == np.arange(B)[:, None])[None, :, None, :])
        .reshape(3 * B, 3 * 128).astype(np.float32),
        "c_n": np.tile((q[:, None] % 16) * 32 + np.arange(32), (1, 2)).astype(np.int32),
    }


def build(nc, d):
    ctx = ExitStack()
    with ctx:
        def sb(name, shape, dt):
            return ctx.enter_context(nc.sbuf_tensor(name, shape, dt))

        def sem(name):
            return ctx.enter_context(nc.semaphore(name))

        bank = [ctx.enter_context(nc.psum_tensor(f"bank{i}", [128, 512], F32)) for i in range(8)]

        chunk_dram = nc.dram_tensor("chunk_scratch", (4, CMP * N), BF16, kind="Internal").ap()
        split_dram = nc.dram_tensor("split_scratch", (2, 2, B * N), F32, kind="Internal").ap()

        ident = sb("ident", [128, 128], F32)
        rows_ind = sb("rows_ind", [3 * G, ROWS], BF16)
        inner_mask = sb("inner_mask", [G, SPAN], BF16)
        edge_mask = sb("edge_mask", [3 * G, SPAN], BF16)
        headmask = sb("headmask", [128, HEADS], F32)
        iota = sb("iota", [128, N], F16)
        ident16 = sb("ident16", [128, 128], F16)
        npoint = sb("npoint", [128, 2 * 32], I32)
        blin = [sb(f"blin{l}", [64, 1], F32) for l in range(2)]
        w3bd = sb("w3bd", [128, 4, 128], F32)
        wv_hi = [sb(f"wv_hi{l}", [128, OUTS[l]], F16) for l in range(2)]
        wv_lo = [sb(f"wv_lo{l}", [128, OUTS[l]], F16) for l in range(2)]
        wcen = [sb(f"wcen{l}", [128, BH * OUTS[l]], F32) for l in range(2)]
        wdif = [sb(f"wdif{l}", [128, BH * OUTS[l]], F32) for l in range(2)]
        bias = [sb(f"bias{l}", [128, 1], F32) for l in range(2)]
        eps_col = sb("eps_col", [128, 1], F32)

        X = sb("X", [128, HALVES, N], F32)
        FX = sb("FX", [128, HALVES, N], F32)
        F1 = sb("F1", [128, HALVES, N], F32)
        ymax = sb("ymax", [128, 2, NPAD], F32)
        z = sb("z", [128, 2, 2, NPAD], F32)
        cen16 = sb("cen16", [128, N], F16)
        cen32 = sb("cen32", [128, N], F32)
        fT = sb("fT", [128, 2, 512], F16)
        bst = sb("bst", [128, 2, STEPS, 6], F32)
        mv = sb("mv", [128, 2, 2], F32)
        rstd = sb("rstd", [128, 2], F32)
        nmr = sb("nmr", [128, 2], F32)
        ranks = sb("ranks", [128, M * B * NT], F32)
        counts = sb("counts", [128, CMP * NT], F32)
        lst = sb("lst", [128, 6], F32)


        xq = sb("xq", [128, 2, BH * ROWS], F16)
        dif = sb("dif", [128, 2, BH * COLS], F32)
        mx = sb("mx", [128, 2, BH * HEADS], F32)
        ex = sb("ex", [128, 2, BH * COLS], F32)
        sm = sb("sm", [128, 2, BH * HEADS], F32)
        rs = sb("rs", [128, 2, BH * HEADS], F32)
        at = sb("at", [128, 2, BH * COLS], F32)
        atT = sb("atT", [COLS, 2, BH * ROWS], F32)
        wlin = [at[0:64, l, 0:256] for l in range(2)]
        wconvT = [atT[0:64, l, 0:128] for l in range(2)]
        val = sb("val", [COLS, 2, BH * 64], F32)
        ys = sb("ys", [128, 2, 2 * ROWS], F32)

        VW = HEADS * (SW - 3)
        SET = 2 * BH * HEADS * SW + 2 * BH * SW + 2 * BH * NPAD
        AREA = 2 * M * NT * N + 2 * SET + 2 * VW
        arena = sb("arena", [128, AREA], BF16)
        at_, operands = 0, []
        for width in (CMP * N, CMP * N, CMP * 128, CMP * 128):
            operands.append(arena[:, at_:at_ + width])
            at_ += width
        RA, RB, LA, LB = operands

        def carver(v, at):
            def take(count, dt=F32):
                nonlocal at
                n = count * (2 if dt == F32 else 1)
                at += n
                return v[:, at - n:at].bitcast(dt)
            return take

        take = carver(arena, 0)
        perm = take(2 * M * NT * N, F16).rearrange("p (s j r) -> p s j r", s=4, r=N)
        khi, klo, Sx, Frep = [], [], [], []
        for _ in range(2):
            khi.append(take(BH * HEADS * SW, F16).rearrange("p (b c) -> p b c", b=BH))
            klo.append(take(BH * HEADS * SW, F16).rearrange("p (b c) -> p b c", b=BH))
            Sx.append(take(BH * SW).rearrange("p (b s) -> p b s", b=BH))
            Frep.append(take(BH * NPAD).rearrange("p (b n) -> p b n", b=BH))
        vT = take(2 * VW, F16).rearrange("p (a c) -> p a c", a=2)
        take = carver(arena, 2 * M * NT * N + SET)
        key_rows = take(4 * 2 * N).rearrange("p (s a n) -> p s a n", s=4, a=2)
        low_dif = take(8 * N).rearrange("p (s n) -> p s n", s=8)
        XK, T1, T2, XH = (take(3 * 64).bitcast(I32).rearrange("p (w a j) -> p w a j", w=3, a=2) for _ in range(4))
        T3 = take(4 * 64).bitcast(I32).rearrange("p (c j) -> p c j", c=4)
        split = take(2 * 64).rearrange("p (c j) -> p c j", c=2)
        xyz, xyz_r, xyz_up = (take(3 * 32).rearrange("p (c j) -> p c j", c=3) for _ in range(3))
        xyz_q = take(3 * 32).bitcast(I32).rearrange("p (c j) -> p c j", c=3)
        to_points = take(3 * 128)[0:3 * B, :]
        wfull, wback = ([take(OUTS[l]) for l in range(2)] for _ in range(2))
        crd = ymax[0:3 * B, 0, 0:N]
        cs = sb("cs", [3 * B, 16], F32)
        scales = sb("scales", [128, 6], F32)

        chunks = ys[:, 0, 0:128].bitcast(BF16).rearrange("p (c j) -> p c j", c=4)
        chunks_h = ys[0:64, 0, 128:192].bitcast(BF16).rearrange("p (c j) -> p c j", c=4)
        split_rows = ex[0:2 * B * NT, :, :].rearrange("p a b -> p (a b)")[:, 0:256].rearrange("p (a n) -> p a n", a=2)
        s_hi = sb("s_hi", [128, SW], F16)
        s_lo = sb("s_lo", [128, SW], F16)
        own = sb("own", [128, 2, 2 * B * NT], F32)

        take = carver(arena, 0)
        w12T = take(4 * 1024).rearrange("p (k m) -> p k m", k=4)
        w3T = take(4 * 512).rearrange("p (k m) -> p k m", k=4)
        bind, sgb = (take(3 * N).rearrange("p (a n) -> p a n", a=3) for _ in range(2))
        b12 = sb("b12", [128, 8], F32)
        F2 = take(2 * N).rearrange("p (a n) -> p a n", a=2)
        tmp = take(2 * N).rearrange("p (a n) -> p a n", a=2)
        b3row, causal = take(N), take(128)
        qkv = take(3 * N).rearrange("p (a n) -> p a n", a=3)
        qkT = take(8 * 128).rearrange("p (a n) -> p a n", a=8)
        sg = take(4 * 128).rearrange("p (a n) -> p a n", a=4)
        sgm = take(4 * 128).rearrange("p (a n) -> p a n", a=4)
        xn = take(2 * N).rearrange("p (a n) -> p a n", a=2)
        xnT = take(4 * 256).rearrange("p (a n) -> p a n", a=4)
        gate = take(4 * 256).rearrange("p (a n) -> p a n", a=4)
        x4T = take(4 * 256).rearrange("p (a n) -> p a n", a=4)
        outb = take(2 * N).rearrange("p (a n) -> p a n", a=2)
        res = take(2 * N).rearrange("p (a n) -> p a n", a=2)

        alpha = sb("alpha", [128, 12], F32)

        def spread(v, n):
            return bass.AP(v.tensor, v.offset, list(v.ap) + [[0, n]])

        S = {name: sem(name) for name in (
            "coords x_in consts masks fold_in key_rows_in weights first_consts points_in chunk_out chunk_in split_out split_in rows_in0 rows_in1 rows_in2 rows_in3 "
            "bind_in ffn_w frep0 frep1 stored "
            "scales_ready scales_psum chunks_done chunks_h_done chunk_h_in split_done own_psum own_ready cmp_ready act_counted low_ready dve_counted ranked "
            "folded fold_taken folded_low zeroed ident16_ready "
            "dve_link act_link pool_link "
            "f0_ready f1_ready f2_ready fT_psum fT_hi fT_lo onehot sorted_psum sorted_sb sorted_low key_hi key_lo "
            "cen_done z_psum z_ready vT_psum vT_hi vT_lo "
            "x_main edge_done x_ready sc_ready mx_done d_ready e_ready sum_done r_ready a_ready aT_psum aT_sb "
            "v_psum v_sb y_psum ys_done ymax_done "
            "var_ready std_ready "
            "h3_psum x_updated att_in att_T att_Tc att_sc att_sg att_m att_o ffn_x ffn_T ffn_Tc "
            "ffn_h ffn_g ffn_x4 ffn_o out_ready").split()}

        block = ctx.enter_context(nc.Block())

        def chain(eng, name):
            count = [0]

            def link(ins):
                count[0] += 1
                ins.then_inc(S[name], 1)
                eng.wait_ge(S[name], count[0])
            return link

        PEEL = 6

        def pipeline(eng, step, lag, inserts):
            def insert(t):
                for work in inserts.get(t, ()):
                    work()

            for t in range(PEEL):
                step(t, t % 2)
                insert(t)
            end = STEPS - 1
            cuts = [PEEL] + [t + 1 for t in sorted(inserts) if PEEL <= t < end - 1] + [end]
            for lo, hi in zip(cuts, cuts[1:]):
                if hi - lo == 2:
                    step(lo, 0)
                    step(lo + 1, 1)
                else:
                    with eng.Fori(lo // 2, hi // 2) as i:
                        step(2 * i, 0)
                        step(2 * i + 1, 1)
                insert(hi - 1)
            for t in range(end, STEPS + lag):
                step(t, t % 2)

        def features_ready(eng, u, l):
            eng.wait_ge(S["f0_ready" if l == 0 else "f1_ready"], 1 if l == 0 else u + 1)

        def live(t):
            return not isinstance(t, int) or 0 <= t < STEPS

        def freed(eng, s, name, lag=2):
            if not isinstance(s, int) or s >= lag:
                eng.wait_ge(S[name], s + 1 - lag)

        def past(eng, q, name, each=1):
            if q >= 2:
                eng.wait_ge(S[name], each * STEPS * (q - 1))

        OWN_AT = 10
        PASSES = [(u, l) for l in range(2) for u in range(HALVES)]
        Z_BEFORE = [0, 1, 2, 4, 6]
        VC = 5
        VCW = VW // VC
        PREP = 12
        AFTER = 10

        def features(u, l):
            return FX[:, u, :] if l == 0 else F1[:, u, :]

        def spare_work(p, first, values, prepare, after):
            plan = {t: list(work) for t, work in first.items()}
            if PASSES[p][1] == 0:
                for c in range(VC):
                    plan.setdefault(c, []).append(lambda c=c: values(p, c))
            if p + 1 < len(PASSES):
                for j in range(PREP):
                    plan[7 + 2 * j] = [lambda j=j: prepare(p + 1, j)]
            else:
                for j in range(AFTER):
                    plan[7 + 2 * j] = [lambda j=j: after(0, j)]
            return plan

        def window(base, n0, step_list):
            v = base[:, bass.ds(n0, 1)]
            return bass.AP(v.tensor, v.offset, [v.ap[0]] + step_list)

        def by_head(v):
            return v.rearrange("p (b s h) -> p b h s", b=BH, h=HEADS)

        def heads(v):
            return v.rearrange("p (b h) -> p b h", b=BH)

        def spread(v, n):
            return bass.AP(v.tensor, v.offset, list(v.ap) + [[0, n]])

        def four(v):
            return v.rearrange("p (a n) -> p a n", a=4)

        SORT_BANK = (6, 7)
        VAL_BANK, Y_BANK = 4, 5

        @block.sync
        def _(sp):
            ctx4 = d["ctx_4096"]
            for c in range(3):
                sp.dma_start(crd[8 * c:8 * c + 8, :], ctx4[:, c, :]).then_inc(S["coords"], 16)
            sp.dma_start(to_points, d["c_to_points"]).then_inc(S["first_consts"], 16)
            for b in range(B):
                sp.dma_start(xyz[16 * b:16 * b + 16, :, :], ctx4[b, 0:3, :].rearrange("c (p j) -> p c j", j=32))\
                    .then_inc(S["points_in"], 16)
            sp.dma_start(npoint[:, :], d["c_n"]).then_inc(S["first_consts"], 16)
            for u in range(HALVES):
                sp.dma_start(X[:, u, :], d["x"][BH * u:BH * u + BH].rearrange("b c n -> (b c) n"))\
                    .then_inc(S["x_in"], 16)
            for dst, name in ((ident, "c_ident"), (headmask, "c_headmask"), (iota, "c_iota")):
                sp.dma_start(dst[:, :], d[name]).then_inc(S["consts"], 16)
            for l in range(2):
                src = d[f"wc{l}T"]
                sp.dma_start(wconvT[l].rearrange("k (r o) -> k r o", o=OUTS[l]),
                             bass.AP(src.tensor, src.offset, [src.ap[0], [0, 128 // OUTS[l]], src.ap[1]]))\
                    .then_inc(S["fold_in"], 16)
                sp.dma_start(wlin[l], d[f"wl{l}"]).then_inc(S["fold_in"], 16)
                sp.dma_start(blin[l][:, :], d[f"bl{l}"].rearrange("(j a) -> j a", a=1)).then_inc(S["fold_in"], 16)
            def constant_rows(v, rows, row):
                tiles = v.shape[1] == CMP * 128
                reps, words = (CMP, 64) if tiles else (1, v.shape[1] // 2)
                src = d["c_key_rows"][row:row + 1, :]
                for r in rows:
                    sp.dma_start(v[r::32, :].bitcast(I32).rearrange("g (b n) -> g b n", b=reps),
                                 bass.AP(src.tensor, src.offset, [[64 if tiles else 0, NT], [0, reps], [1, words]]))\
                        .then_inc(S["key_rows_in"], 16)

            constant_rows(RA, (3, 4, 5), 1)
            constant_rows(LA, (0, 1, 2), 0)
            for v, rows, row in ((RB, (2, 3), 1), (RB, (1,), 2), (LB, (0, 1), 0), (LB, (3,), 2)):
                constant_rows(v, rows, row)
            def operands_in(j0, j1, name):
                for i, (R, L, r, l) in enumerate(((RB, LB, 0, 2), (RA, LA, 0, 3), (RA, LA, 1, 4), (RA, LA, 2, 5))):
                    src = chunk_dram[i:i + 1, N * j0:N * j1]
                    sp.dma_start(R[r::32, N * j0:N * j1], bass.AP(src.tensor, src.offset, [[0, NT], src.ap[1]]))\
                        .then_inc(S[name], 16)
                    sp.dma_start(L[l::32, 128 * j0:128 * j1].rearrange("g (j n) -> g j n", n=128),
                                 src[0].rearrange("(j g n) -> g j n", g=NT, n=128)).then_inc(S[name], 16)

            sp.wait_ge(S["chunks_done"], 1)
            for m in range(2):
                sp.dma_start(chunk_dram[:, B * N * m:B * N * (m + 1)].rearrange("c (p j) -> p c j", j=32),
                             chunks[:, :, 32 * m:32 * m + 32]).then_inc(S["chunk_out"], 16)
            sp.wait_ge(S["chunk_out"], 16 * 2)
            operands_in(0, 2 * B, "chunk_in")
            sp.wait_ge(S["split_done"], 1)
            sp.dma_start(split_dram.rearrange("a m (p j) -> p a m j", j=32),
                         split.rearrange("p a (m j) -> p a m j", m=2)).then_inc(S["split_out"], 16)
            sp.wait_ge(S["split_out"], 16)
            flat = split_dram.rearrange("a m n -> a (m n)")
            sp.dma_start(split_rows, flat.rearrange("a (r p) -> r a p", p=128)).then_inc(S["split_in"], 16)

            def key_rows_of(j):
                i = j - BH
                row = flat[:, N * j:N * j + N]
                sp.dma_start(key_rows[:, i % 4, :, :],
                             bass.AP(row.tensor, row.offset, [[0, 128], [2 * B * N, 2], [1, N]]))\
                    .then_inc(S[f"rows_in{i % 4}"], 16)

            for j in range(BH, BH + 4):
                key_rows_of(j)
            sp.wait_ge(S["chunks_h_done"], 1)
            sp.dma_start(chunk_dram[:, 2 * B * N:].rearrange("c (p j) -> p c j", j=32), chunks_h[:, :, :])\
                .then_inc(S["chunk_out"], 16)
            sp.wait_ge(S["chunk_out"], 16 * 3)
            operands_in(2 * B, CMP, "chunk_h_in")
            for j in range(BH + 4, 2 * B):
                sp.wait_ge(S["dve_counted"], j - BH - 3)
                key_rows_of(j)

            for p, (u, l) in enumerate(PASSES):
                F = features(u, l)
                features_ready(sp, u, l)
                sp.wait_ge(S["zeroed"], 5)
                past(sp, p, "x_ready")
                for m in range(M):
                    for b in range(BH):
                        sp.dma_start(Frep[p % 2][C * m:C * m + C, b, 0:N], F[C * b:C * b + C, :])\
                            .then_inc(S[f"frep{p % 2}"], 16)
            sp.wait_ge(S["v_psum"], STEPS * 3)
            sp.wait_ge(S["x_ready"], STEPS * 3)
            for i, name in enumerate(("bv_q", "bv_k", "bv_v")):
                row = d[name].rearrange("h e -> (h e)")
                sp.dma_start(bind[:, i, :], bass.AP(row.tensor, row.offset, [[0, 128], [1, N]]))\
                    .then_inc(S["bind_in"], 16)
            b3 = d["b3"]
            sp.dma_start(b3row, bass.AP(b3.tensor, b3.offset, [[0, 128], [1, N]])).then_inc(S["bind_in"], 16)
            sp.dma_start(causal, d["c_causal"]).then_inc(S["bind_in"], 16)
            sp.dma_start(w12T, d["w12T"].rearrange("(k p) m -> p k m", p=128)).then_inc(S["ffn_w"], 16)
            sp.dma_start(w3T, d["w3T"].rearrange("(k p) m -> p k m", p=128)).then_inc(S["ffn_w"], 16)
            for u in range(HALVES):
                sp.wait_ge(S["out_ready"], u + 1)
                sp.dma_start(d["out"][BH * u:BH * u + BH].rearrange("b c n -> (b c) n"), outb[:, u, :])\
                    .then_inc(S["stored"], 16)
            sp.wait_ge(S["stored"], 16 * HALVES)

        @block.gpsimd
        def _(pool):
            g = nc.gpsimd
            for dst, name in ((rows_ind, "c_rows"), (inner_mask, "c_inner"), (edge_mask, "c_edge")):
                pool.dma_start(dst[:, :], d[name]).then_inc(S["masks"], 16)
            g.memset(w3bd[:, :, :], 0.0).then_inc(S["pool_link"], 1)
            pool.wait_ge(S["pool_link"], 1)
            for b in range(BH):
                o = slice(C * b, C * b + C)
                r = 64 * (b % 2)
                for dst, src in ((w3bd[o, 0, o], d["w3cT"][0:C, :]), (w3bd[o, 1, o], d["w3cT"][C:2 * C, :]),
                                 (w3bd[r:r + 64, 2 + b // 2, o], d["w3cT"][2 * C:4 * C, :])):
                    pool.dma_start(dst, src).then_inc(S["weights"], 16)
            pool.dma_start(b12[:, :], d["b12"]).then_inc(S["weights"], 16)
            g.memset(z[:, :, :, N:NPAD], 0.0).then_inc(S["zeroed"], 1)

            pool.wait_ge(S["own_ready"], 1)

            def lower_differences(j):
                i, slot, half = j - BH, j % 4, j % 2
                pool.wait_ge(S[f"rows_in{slot}"], 16 * (i // 4) + 16)
                freed(pool, i, "dve_counted")
                for nt in range(NT):
                    g.tensor_scalar(low_dif[:, 4 * half + nt, :], key_rows[:, slot, 1, :], -1.0,
                                    own[:, 1, NT * j + nt:NT * j + nt + 1], ALU.mult, ALU.add)\
                        .then_inc(S["low_ready"], 1)

            for j in range(BH, 2 * B):
                lower_differences(j)

            pool.wait_ge(S["ranked"], 1)
            for k in range(2):
                g.memset(Sx[k][:, :, 0:LEFT], 0.0)
                g.memset(Sx[k][:, :, LEFT + N + 4:SW], 0.0).then_inc(S["zeroed"], 1)
                g.memset(Frep[k][:, :, N:NPAD], 0.0).then_inc(S["zeroed"], 1)

            for p, (u, l) in enumerate(PASSES):
                base = STEPS * p
                sx, fr = Sx[p % 2], Frep[p % 2]

                def form_x(t, k):
                    s = base + t
                    freed(pool, s, "sc_ready")
                    if isinstance(t, int) and t == 0:
                        pool.wait_ge(S[f"frep{p % 2}"], 16 * 16 * (p // 2 + 1))
                        pool.wait_ge(S["sorted_sb"], 3 * BH * (p + 1))
                    src = window(sx[:, 0, :], G * t, [[SW, BH], [1, G], [1, K]])
                    cen = window(fr[:, 0, :], G * t, [[NPAD, BH], [1, G], [0, K]])
                    out = xq[:, k, :].rearrange("p (b n i) -> p b n i", b=BH, n=G)
                    ins = g.tensor_tensor(out, src, cen, ALU.subtract)
                    if isinstance(t, int) and t == 0:
                        ins.then_inc(S["x_main"], 1)
                        pool.wait_ge(S["x_main"], p + 1)
                        for n in range(LEFT):
                            w = LEFT - n
                            ins = g.tensor_tensor(out[:, :, n, 0:w], window(sx[:, 0, :], n + K, [[SW, BH], [0, w]]),
                                                  window(fr[:, 0, :], n, [[NPAD, BH], [0, w]]), ALU.subtract)
                            if n < LEFT - 1:
                                ins.then_inc(S["edge_done"], 1)
                        pool.wait_ge(S["edge_done"], (LEFT - 1) * (p + 1))
                    ins.then_inc(S["x_ready"], 1)

                def normalise(t, k):
                    s = base + t
                    pool.wait_ge(S["r_ready"], s + 1)
                    freed(pool, s, "aT_psum")
                    g.tensor_tensor(by_head(at[0:ROWS, k, :]), by_head(ex[0:ROWS, k, :]),
                                    spread(heads(rs[0:ROWS, k, :]), SPAN), ALU.mult).then_inc(S["a_ready"], 1)

                form_x(0, 0)

                def step(t, k):
                    if not (isinstance(t, int) and t + 1 >= STEPS):
                        form_x(t + 1, 1 - k)
                    if live(t - 1):
                        normalise(t - 1, 1 - k)

                pipeline(pool, step, 1, {})

        @block.scalar
        def _(act):
            link = chain(act, "act_link")
            roots = [0]

            def root(n):
                roots[0] += 1
                act.wait_ge(S["var_ready"], roots[0])
                nc.scalar.activation(rstd[:, 0:n], mv[:, 0:n, 1], ACT.Sqrt, bias=eps_col[:, 0:1])\
                    .then_inc(S["std_ready"], 1)

            act.wait_ge(S["dve_link"], 3)
            act.wait_ge(S["consts"], 16 * 3)
            nc.scalar.copy(ident16[:, :], ident[:, :]).then_inc(S["ident16_ready"], 1)

            def prepare(q, j):
                u, l = PASSES[q]
                par = q % 2

                def sorted_out(b):
                    act.wait_ge(S["sorted_psum"], 2 * (BH * q + b + 1))
                    if b == 0:
                        act.wait_ge(S["zeroed"], 5)
                        past(act, q, "x_ready")
                        past(act, q, "v_psum")
                    n = 3 * (BH * q + b)
                    nc.scalar.copy(Sx[par][:, b, LEFT:LEFT + N], bank[SORT_BANK[b % 2]][:, :]).then_inc(S["sorted_sb"], 1)
                    act.wait_ge(S["sorted_sb"], n + 1)
                    nc.scalar.copy(Sx[par][:, b, LEFT + N:LEFT + N + 4],
                                   window(Sx[par][:, b, :], LEFT + N - 1, [[0, 4]])).then_inc(S["sorted_sb"], 1)
                    act.wait_ge(S["sorted_sb"], n + 2)
                    if q or b:
                        act.wait_ge(S["sorted_low"], BH * q + b)
                    nc.scalar.copy(s_hi[:, :], Sx[par][:, b, :]).then_inc(S["sorted_sb"], 1)
                    for h in range(HEADS):
                        ins = nc.scalar.activation(khi[par][:, b, h::HEADS], Sx[par][:, b, :], ACT.Copy,
                                                   scale=headmask[:, h:h + 1])
                    ins.then_inc(S["key_hi"], 1)

                def keys_low(b):
                    act.wait_ge(S["sorted_low"], BH * q + b + 1)
                    for h in range(HEADS):
                        ins = nc.scalar.activation(klo[par][:, b, h::HEADS], s_lo[:, :], ACT.Copy,
                                                   scale=headmask[:, h:h + 1])
                    ins.then_inc(S["key_lo"], 1)

                def z_out(g):
                    act.wait_ge(S["z_psum"], Z_BEFORE[q] + g + 1)
                    past(act, q, "ys_done")
                    nc.scalar.activation(z[:, par, g, 0:N], bank[7][:, :], ACT.Identity, bias=bias[l][:, 0:1])\
                        .then_inc(S["z_ready"], 1)

                if j == 0:
                    features_ready(act, u, l)
                    if q:
                        act.wait_ge(S["z_psum"], Z_BEFORE[q])
                    nc.scalar.copy(cen16[:, :], features(u, l)).then_inc(S["cen_done"], 1)
                    act.wait_ge(S["cen_done"], 2 * q + 1)
                    nc.scalar.copy(cen32[:, :], cen16[:, :]).then_inc(S["cen_done"], 1)
                elif j == 1:
                    act.wait_ge(S["fT_psum"], q + 1)
                    if q:
                        act.wait_ge(S["sorted_psum"], 2 * BH * q)
                    nc.scalar.copy(fT[:, 0, :], bank[6][:, :]).then_inc(S["fT_hi"], 1)
                elif j == 2:
                    z_out(0)
                elif j == 3 and l == 1:
                    z_out(1)
                elif 4 <= j < 4 + 2 * BH:
                    if j % 2 == 0:
                        sorted_out(j // 2 - 2)
                    elif q or j // 2 < 4:
                        keys_low(j // 2 - 2)

            def value_columns(p, c):
                act.wait_ge(S["vT_psum"], VC * p + c + 1)
                if p:
                    act.wait_ge(S["v_psum"], STEPS * p)
                nc.scalar.copy(vT[:, 0, VCW * c:VCW * c + VCW], bank[6 + c % 2][:, 0:VCW]).then_inc(S["vT_hi"], 1)

            def gates(u):
                for m in range(4):
                    act.wait_ge(S["ffn_h"], 4 * u + m + 1)
                    nc.scalar.activation(gate[:, m, 128 * u:128 * u + 128], bank[m][:, 0:128], ACT.Silu,
                                         bias=b12[:, m:m + 1]).then_inc(S["ffn_g"], 1)

            def after(u, j):
                if j in (1, 2, 7):
                    root(1)
                    if u == 1 and j == 2:
                        gates(0)
                elif j == 4:
                    for a in range(2):
                        act.wait_ge(S["att_T"], 2 * u + a + 1)
                        nc.scalar.copy(qkT[:, 4 * a:4 * a + 4, :], four(bank[6 + a][:, :])).then_inc(S["att_Tc"], 1)
                elif j == 5:
                    act.wait_ge(S["att_sc"], u + 1)
                    nc.scalar.activation(sg[:, :, :], four(bank[6][:, :]), ACT.Sigmoid, scale=4.0 * 128 ** -0.5)\
                        .then_inc(S["att_sg"], 1)
                elif j == 9:
                    act.wait_ge(S["ffn_T"], u + 1)
                    nc.scalar.copy(xnT[:, :, 128 * u:128 * u + 128], four(bank[6][:, :])).then_inc(S["ffn_Tc"], 1)

            for l in range(2):
                O = OUTS[l]
                act.wait_ge(S["folded"], 2 * l + 1)
                link(nc.scalar.activation(wfull[l], bank[0][:, 0:O], ACT.Copy, scale=W_SCALE))
                link(nc.scalar.copy(wv_hi[l][:, :], wfull[l]))
                nc.scalar.copy(wback[l], wv_hi[l][:, :]).then_inc(S["fold_taken"], 1)
                act.wait_ge(S["folded"], 2 * l + 2)
                for b in range(BH):
                    r = slice(C * b, C * b + C)
                    nc.scalar.copy(wcen[l][r, O * b:O * b + O], bank[1][r, 0:O])
                    nc.scalar.mul(wdif[l][r, O * b:O * b + O], bank[1][r, 64:64 + O], -1.0)
                nc.scalar.copy(bias[l][:, :], bank[1][:, 128:129]).then_inc(S["fold_taken"], 1)
                if l == 0:
                    root(2)
            for j in range(3):
                prepare(0, j)

            def count(j, i4):
                act.wait_ge(S["cmp_ready"], j + 1)
                for nt in range(NT):
                    ins = nc.scalar.activation(bank[i4 + nt][:, :], bank[i4 + nt][:, :], ACT.Sign,
                                               accum_out=counts[:, bass.ds(NT * j + nt, 1)])
                ins.then_inc(S["act_counted"], 1)

            with act.Fori(0, CMP // 2) as i:
                count(2 * i, 0)
                count(2 * i + 1, 4)

            for j in range(3, PREP):
                prepare(0, j)
            for p, (u, l) in enumerate(PASSES):
                O = OUTS[l]
                base = STEPS * p

                def step(t, k):
                    s = base + t
                    if live(t):
                        act.wait_ge(S["d_ready"], s + 1)
                        freed(act, s, "a_ready")
                        nc.scalar.activation(ex[0:ROWS, k, :], dif[0:ROWS, k, :], ACT.Exp,
                                             scale=HEAD_SCALE).then_inc(S["e_ready"], 1)
                    if live(t - 2):
                        act.wait_ge(S["aT_psum"], s - 1)
                        freed(act, s - 2, "y_psum")
                        nc.scalar.copy(atT[:, k, :], bank[2 + k][0:COLS, 0:BH * ROWS]).then_inc(S["aT_sb"], 1)
                        act.wait_ge(S["v_psum"], s - 1)
                        nc.scalar.activation(val[:, k, 0:BH * O], bank[VAL_BANK][0:COLS, 0:BH * O],
                                             ACT.Copy, scale=1.0 / W_SCALE).then_inc(S["v_sb"], 1)

                first = {1: [lambda p=p: root(PASSES[p - 1][1] + 1)]} if p else {}
                pipeline(act, step, 2, spare_work(p, first, value_columns, prepare, after))
            root(2)
            for j in range(AFTER):
                after(1, j)
            gates(1)

        @block.tensor
        def _(pe):
            def cols(v, start, n):
                return v[:, bass.ds(start, n)]

            def prepare(q, j):
                u, l = PASSES[q]
                par = q % 2
                F = features(u, l)

                def sort(b, half):
                    n = 2 * (BH * q + b) + half
                    pe.wait_ge(S["onehot"], n + 1)
                    if b >= 2 and half == 0:
                        pe.wait_ge(S["sorted_sb"], 3 * (BH * q + b - 2) + 1)
                    for i in range(2):
                        nt = 2 * half + i
                        for part in range(2):
                            for m in range(M):
                                ins = nc.tensor.matmul(bank[SORT_BANK[b % 2]][C * m:C * m + C, :],
                                                       fT[:, part, 128 * nt + C * b:128 * nt + C * b + C],
                                                       perm[:, n % 4, 2 * m + i, :],
                                                       start=(nt == 0 and part == 0), stop=(nt == NT - 1 and part == 1))
                    ins.then_inc(S["sorted_psum"], 1)

                def centre(g):
                    w = slice(128 * g, 128 * g + 128)
                    nc.tensor.matmul(bank[7][:, :], wcen[l][:, w], cen32[:, :], start=True, stop=False)
                    nc.tensor.matmul(bank[7][:, :], wdif[l][:, w], F, start=False, stop=True).then_inc(S["z_psum"], 1)

                if j == 0:
                    features_ready(pe, u, l)
                    if q:
                        pe.wait_ge(S["sorted_sb"], 3 * BH * q)
                        pe.wait_ge(S["vT_lo"], VC * min(q, 2))
                    for nt in range(NT):
                        ins = nc.tensor.transpose(bank[6][:, 128 * nt:128 * nt + 128], F[:, 128 * nt:128 * nt + 128],
                                                  ident[:, :])
                    ins.then_inc(S["fT_psum"], 1)
                elif j == 1:
                    pe.wait_ge(S["cen_done"], 2 * q + 2)
                    centre(0)
                    pe.wait_ge(S["fT_lo"], q + 1)
                    pe.wait_ge(S["fT_hi"], q + 1)
                elif 2 <= j < 2 + 2 * BH:
                    if j == 4:
                        pe.wait_ge(S["z_ready"], Z_BEFORE[q + 1])
                    sort((j - 2) // 2, j % 2)
                    if j == 2 and l == 1:
                        pe.wait_ge(S["z_ready"], Z_BEFORE[q] + 1)
                        centre(1)

            def value_columns(p, c):
                n = VC * p + c
                if c < 2:
                    pe.wait_ge(S["sorted_sb"], 3 * BH * (p + 1))
                else:
                    pe.wait_ge(S["vT_lo"], n - 1)
                for i, (w, keys) in enumerate(((wv_hi, khi), (wv_lo, khi), (wv_hi, klo))):
                    for b in range(BH):
                        ins = nc.tensor.matmul(bank[6 + c % 2][C * b:C * b + C, 0:VCW], w[0][:, :],
                                               keys[p % 2][:, b, VCW * c:VCW * c + VCW], start=(i == 0), stop=(i == 2))
                ins.then_inc(S["vT_psum"], 1)

            def ffn_hidden(u, m):
                for branch in range(2):
                    for c in range(4):
                        col = 128 * (m + 4 * branch)
                        ins = nc.tensor.matmul(bank[m][:, 128 * branch:128 * branch + 128], w12T[:, c, col:col + 128],
                                               xnT[:, c, 128 * u:128 * u + 128], start=(c == 0), stop=(c == 3))
                ins.then_inc(S["ffn_h"], 1)

            def ffn_out(u, m):
                pe.wait_ge(S["ffn_x4"], 4 * u + m + 1)
                ins = nc.tensor.matmul(bank[4 + u][:, :], x4T[:, m, 128 * u:128 * u + 128], w3T[:, m, :],
                                       start=(m == 0), stop=(m == 3))
                if m == 3:
                    ins.then_inc(S["ffn_o"], 1)

            def after(u, j):
                if j == 0:
                    if u == 0:
                        pe.wait_ge(S["weights"], 16 * (3 * BH + 1))
                        pe.wait_ge(S["sorted_sb"], 3 * BH * len(PASSES))
                    else:
                        pe.wait_ge(S["ffn_Tc"], 1)
                    parts = (FX[:, u, :], F1[:, u, :], F2[:, 0, :], F2[:, 1, :])
                    for i, f in enumerate(parts):
                        if i >= 2:
                            pe.wait_ge(S["f2_ready"], 2 * u + i - 1)
                        ins = nc.tensor.matmul(bank[6][:, :], w3bd[:, i, :], f, start=(i == 0), stop=(i == 3))
                    ins.then_inc(S["h3_psum"], 1)
                elif j == 3:
                    pe.wait_ge(S["att_in"], u + 1)
                    for a in range(2):
                        for h in range(4):
                            ins = nc.tensor.transpose(bank[6 + a][:, 128 * h:128 * h + 128],
                                                      qkv[:, a, 128 * h:128 * h + 128], ident[:, :])
                        ins.then_inc(S["att_T"], 1)
                elif j == 4:
                    pe.wait_ge(S["att_Tc"], 2 * u + 2)
                    for h in range(4):
                        ins = nc.tensor.matmul(bank[6][:, 128 * h:128 * h + 128], qkT[:, 4 + h, :], qkT[:, h, :],
                                               start=True, stop=True)
                    ins.then_inc(S["att_sc"], 1)
                    if u == 1:
                        ffn_out(0, 0)
                        ffn_out(0, 1)
                elif j == 6:
                    pe.wait_ge(S["att_m"], u + 1)
                    for h in range(4):
                        ins = nc.tensor.matmul(bank[7][:, 128 * h:128 * h + 128], sgm[:, h, :],
                                               qkv[:, 2, 128 * h:128 * h + 128], start=True, stop=True)
                    ins.then_inc(S["att_o"], 1)
                    if u == 1:
                        ffn_out(0, 2)
                        ffn_out(0, 3)
                elif j == 8:
                    pe.wait_ge(S["ffn_x"], u + 1)
                    for c in range(4):
                        ins = nc.tensor.transpose(bank[6][:, 128 * c:128 * c + 128], xn[:, u, 128 * c:128 * c + 128],
                                                  ident[:, :])
                    ins.then_inc(S["ffn_T"], 1)

            pe.wait_ge(S["first_consts"], 32)
            pe.wait_ge(S["scales_ready"], 1)
            for c in range(3):
                ins = nc.tensor.matmul(bank[7][:, 2 * c:2 * c + 2], to_points[:, 128 * c:128 * c + 128], cs[:, 0:5:4],
                                       start=True, stop=True)
            ins.then_inc(S["scales_psum"], 1)
            pe.wait_ge(S["fold_in"], 16 * 6)
            for l in range(2):
                O = OUTS[l]
                if l:
                    pe.wait_ge(S["fold_taken"], 2)
                for m in range(M):
                    slot = PERMS[l].index(m)
                    ins = nc.tensor.matmul(bank[0][C * m:C * m + C, 0:O], wlin[l][:, 4 * C + slot:8 * C:4],
                                           wconvT[l][:, 0:O], start=True, stop=True)
                ins.then_inc(S["folded"], 1)
                for b in range(BH):
                    for kind in range(2):
                        for slot in range(M):
                            nc.tensor.matmul(bank[1][C * b:C * b + C, 64 * kind:64 * kind + O],
                                             wlin[l][:, 4 * C * kind + slot:4 * C * (kind + 1):4],
                                             wconvT[l][:, 0:O], start=(slot == 0), stop=(slot == M - 1))
                nc.tensor.matmul(bank[1][:, 128:129], wconvT[l], blin[l][:, :], start=True, stop=True)\
                    .then_inc(S["folded"], 1)
            pe.wait_ge(S["fold_taken"], 4)
            pe.wait_ge(S["consts"], 16 * 3)
            prepare(0, 0)
            prepare(0, 1)

            def compare(j):
                freed(pe, j, "act_counted")
                for part, (L, R, rows) in enumerate(((LA, RA, 6), (LB, RB, 4))):
                    for nt in range(NT):
                        g = slice(32 * nt, 32 * nt + rows)
                        ins = nc.tensor.matmul(bank[4 * (j % 2) + nt][:, :], L[g, 128 * j:128 * j + 128],
                                               R[g, N * j:N * j + N], start=(part == 0), stop=(part == 1))
                ins.then_inc(S["cmp_ready"], 1)

            pe.wait_ge(S["chunk_in"], 16 * 8)
            pe.wait_ge(S["key_rows_in"], 16 * 12)
            pe.wait_ge(S["z_ready"], 1)
            for j in range(OWN_AT):
                compare(j)
            pe.wait_ge(S["act_counted"], OWN_AT - 1)
            pe.wait_ge(S["split_in"], 16)
            for a in range(2):
                ins = nc.tensor.transpose(bank[0][:, 64 * a:64 * a + 64], split_rows[:, a, :], ident[0:64, 0:64])
            ins.then_inc(S["own_psum"], 1)
            pe.wait_ge(S["own_ready"], 1)
            for j in range(OWN_AT, CMP):
                if j == 2 * B:
                    pe.wait_ge(S["chunk_h_in"], 16 * 8)
                compare(j)
            pe.wait_ge(S["act_counted"], CMP)
            pe.wait_ge(S["masks"], 16 * 3)
            pe.wait_ge(S["ident16_ready"], 1)

            for j in range(2, PREP):
                prepare(0, j)
            for p, (u, l) in enumerate(PASSES):
                O = OUTS[l]
                base = STEPS * p
                par = p % 2
                pe.wait_ge(S["folded_low"], 2)
                pe.wait_ge(S["key_hi"], BH * (p + 1))
                pe.wait_ge(S["key_lo"], BH * (p + 1))

                def scores(t, k):
                    s = base + t
                    edge = isinstance(t, int) and t == 0
                    freed(pe, s, "d_ready")
                    sc = bank[k][0:ROWS, 0:BH * COLS]
                    rows = 3 * G if edge else G
                    msk = (edge_mask if edge else inner_mask)[:, :]
                    msk = bass.AP(msk.tensor, msk.offset, [msk.ap[0], [0, BH], [1, SPAN], [0, HEADS]])
                    nc.tensor.matmul(sc, rows_ind[0:rows, :], msk, start=True, stop=False, skip_group_check=True)
                    pe.wait_ge(S["x_ready"], s + 1)
                    for b in range(BH):
                        for keys in (khi[par], klo[par]):
                            ins = nc.tensor.matmul(sc[:, COLS * b:COLS * b + COLS], xq[:, k, ROWS * b:ROWS * b + ROWS],
                                                   cols(keys[:, b, :], HEADS * G * t, COLS), start=False,
                                                   stop=True, skip_group_check=True)
                    ins.then_inc(S["sc_ready"], 1)

                def turn(t, k):
                    s = base + t
                    pe.wait_ge(S["a_ready"], s + 1)
                    freed(pe, s, "aT_sb")
                    for b in range(BH):
                        ins = nc.tensor.transpose(bank[2 + k][0:COLS, ROWS * b:ROWS * b + ROWS],
                                                  at[0:ROWS, k, COLS * b:COLS * b + COLS], ident[0:ROWS, 0:ROWS])
                    ins.then_inc(S["aT_psum"], 1)

                def values(t, k):
                    s = base + t
                    freed(pe, s, "v_sb", 1)
                    o = bank[VAL_BANK][0:COLS, 0:BH * O]
                    if l == 0:
                        if isinstance(t, int) and t < VC:
                            pe.wait_ge(S["vT_lo"], VC * p + t + 1)
                        for a in range(2):
                            ins = nc.tensor.matmul(o, cols(vT[:, a, :], HEADS * G * t, COLS), ident16[:, :],
                                                   start=(a == 0), stop=(a == 1))
                    else:
                        for b in range(BH):
                            hi, lo = (cols(keys[:, b, :], HEADS * G * t, COLS) for keys in (khi[par], klo[par]))
                            for i, (w, keys) in enumerate(((wv_hi, hi), (wv_lo, hi), (wv_hi, lo))):
                                ins = nc.tensor.matmul(o[:, O * b:O * b + O], keys, w[l][:, :],
                                                       start=(i == 0), stop=(i == 2))
                    ins.then_inc(S["v_psum"], 1)

                def products(t, k):
                    s = base + t
                    pe.wait_ge(S["aT_sb"], s + 1)
                    pe.wait_ge(S["v_sb"], s + 1)
                    freed(pe, s, "ys_done", 1)
                    for b in range(BH):
                        r, c = (C * b, 0) if l == 0 else (64 * (b % 2), ROWS * (b // 2))
                        ins = nc.tensor.matmul(bank[Y_BANK][r:r + O, c:c + ROWS], val[:, k, O * b:O * b + O],
                                               atT[:, k, ROWS * b:ROWS * b + ROWS], start=True, stop=True,
                                               skip_group_check=True)
                    ins.then_inc(S["y_psum"], 1)

                def step(t, k):
                    if live(t):
                        scores(t, k)
                    if live(t - 2):
                        turn(t - 2, k)
                        values(t - 2, k)
                    if live(t - 3):
                        products(t - 3, 1 - k)

                pipeline(pe, step, 3, spare_work(p, {}, value_columns, prepare, after))

            pe.wait_ge(S["ffn_w"], 32)
            pe.wait_ge(S["d_ready"], STEPS * len(PASSES))
            pe.wait_ge(S["aT_sb"], STEPS * len(PASSES))
            ffn_hidden(0, 0)
            ffn_hidden(0, 1)
            after(1, 0)
            ffn_hidden(0, 2)
            ffn_hidden(0, 3)
            pe.wait_ge(S["ymax_done"], STEPS * len(PASSES))
            for j in range(1, AFTER):
                after(1, j)
            pe.wait_ge(S["ffn_Tc"], 2)
            for m in range(4):
                ffn_hidden(1, m)
                if m >= 2:
                    ffn_out(1, m - 2)
            ffn_out(1, 2)
            ffn_out(1, 3)

        @block.vector
        def _(dve):
            v = nc.vector
            link = chain(dve, "dve_link")
            for l in range(2):
                v.memset(wcen[l][:, :], 0.0)
                link(v.memset(wdif[l][:, :], 0.0))
            link(v.memset(eps_col[:, :], EPS))
            variances = [0]

            def to_root(ins):
                variances[0] += 1
                ins.then_inc(S["var_ready"], 1)

            def inverse_root(n):
                dve.wait_ge(S["std_ready"], variances[0])
                link(v.reciprocal(rstd[:, 0:n], rstd[:, 0:n]))

            c1 = lambda i: cs[:, i:i + 1]
            dve.wait_ge(S["coords"], 48)
            v.tensor_reduce(c1(0), crd, AX.X, ALU.min)
            link(v.tensor_reduce(c1(1), crd, AX.X, ALU.max))
            link(v.tensor_tensor(c1(2), c1(1), c1(0), ALU.subtract))
            link(v.tensor_scalar(c1(2), c1(2), 1e-6, None, ALU.add))
            top = float(2 ** BITS - 1)
            v.tensor_scalar(c1(9), c1(2), 4097.0, None, ALU.mult)
            link(v.reciprocal(c1(3), c1(2)))
            v.tensor_tensor(c1(10), c1(9), c1(2), ALU.subtract)
            link(v.tensor_scalar(c1(4), c1(3), top, None, ALU.mult))
            v.tensor_tensor(c1(5), c1(9), c1(10), ALU.subtract)
            link(v.tensor_scalar(c1(13), c1(4), 4097.0, None, ALU.mult))
            v.tensor_tensor(c1(6), c1(2), c1(5), ALU.subtract)
            link(v.tensor_tensor(c1(14), c1(13), c1(4), ALU.subtract))
            link(v.tensor_tensor(c1(7), c1(13), c1(14), ALU.subtract))
            v.tensor_tensor(c1(8), c1(4), c1(7), ALU.subtract)
            link(v.tensor_tensor(c1(11), c1(5), c1(7), ALU.mult))
            link(v.tensor_scalar(c1(11), c1(11), -1.0, top, ALU.mult, ALU.add))
            for x, y, to in ((5, 8, 12), (6, 7, 13), (6, 8, 14)):
                ins = v.tensor_tensor(c1(to), c1(x), c1(y), ALU.mult)
            link(ins)
            for to in (12, 13, 14):
                link(v.tensor_tensor(c1(11), c1(11), c1(to), ALU.subtract))
            link(v.tensor_tensor(c1(12), c1(11), c1(3), ALU.mult))
            v.tensor_tensor(c1(4), c1(4), c1(12), ALU.add).then_inc(S["scales_ready"], 1)
            dve.wait_ge(S["scales_psum"], 1)
            link(v.tensor_copy(scales[:, :], bank[7][:, 0:6]))
            dve.wait_ge(S["points_in"], 16 * B)
            for c in range(3):
                ins = v.tensor_scalar(xyz[:, c, :], xyz[:, c, :], scales[:, 2 * c:2 * c + 1],
                                      scales[:, 2 * c + 1:2 * c + 2], ALU.subtract, ALU.mult)
            link(ins)
            link(v.tensor_copy(xyz_q, xyz))
            link(v.tensor_copy(xyz_r, xyz_q))
            link(v.tensor_tensor(xyz_up, xyz_r, xyz, ALU.is_gt))
            link(v.tensor_tensor(xyz_r, xyz_r, xyz_up, ALU.subtract))

            SHL, SHR, SAR = ALU.logical_shift_left, ALU.logical_shift_right, ALU.arith_shift_right
            AND, OR, XOR = ALU.bitwise_and, ALU.bitwise_or, ALU.bitwise_xor

            def words(to):
                v.tensor_scalar(to[:, :, 0, :], xyz_r, 0.0, top, ALU.max, ALU.min)
                for w, c in enumerate((1, 0, 2)):
                    ins = v.tensor_scalar(to[:, w, 1, :], xyz_r[:, c, :], 0.0, top, ALU.max, ALU.min)
                link(ins)

            words(XK)
            dve.wait_ge(S["first_consts"], 32)
            key = T2[:, 0, :, :].rearrange("p a j -> p (a j)")

            def join(X3):
                x3, s1 = (T.rearrange("p w a j -> p (w a j)") for T in (X3, T1))
                for sh, keep in ((16, 0x030000FF), (8, 0x0300F00F), (4, 0x030C30C3), (2, 0x09249249)):
                    link(v.scalar_tensor_tensor(s1, x3, sh, x3, SHL, OR))
                    link(v.tensor_scalar(x3, s1, keep, None, AND))
                word = [X3[:, w, :, :].rearrange("p a j -> p (a j)") for w in range(3)]
                k1 = T1[:, 0, :, :].rearrange("p a j -> p (a j)")
                link(v.scalar_tensor_tensor(k1, word[0], 1, word[1], SHL, OR))
                link(v.scalar_tensor_tensor(key, k1, 1, word[2], SHL, OR))

            def cut(w, out, name, rows=128):
                T, k = T3[0:rows, :, w], key[0:rows, w]
                nw = npoint[0:rows, w]
                v.tensor_scalar(T[:, 0, :], k, 127, 1, AND, SHL)
                link(v.tensor_scalar(T[:, 1, :], nw, 8, None, SHR))
                v.tensor_tensor(T[:, 0, :], T[:, 0, :], T[:, 1, :], OR)
                v.tensor_scalar(T[:, 2, :], k, 15, 255, SHR, AND)
                link(v.tensor_scalar(T[:, 3, :], k, 23, None, SHR))
                link(v.tensor_scalar(T[:, 1, :], k, 7, 255, SHR, AND))
                for j in range(4):
                    ins = v.tensor_scalar(out[:, j, :], T[:, j, :], float(2 ** (8 * j + 8)), None, ALU.mult)
                ins.then_inc(S[name], 1)

            join(XK)
            cut(slice(0, 64), chunks, "chunks_done")
            dve.wait_ge(S["x_in"], 32)
            for u in range(HALVES):
                link(v.bn_stats(bst[:, u, 0, :], X[:, u, :]))
                ins = v.bn_aggr(mv[:, u, :], bst[:, u, 0, :])
            to_root(ins)
            inverse_root(2)
            for u in range(HALVES):
                ins = v.tensor_scalar(FX[:, u, :], X[:, u, :], mv[:, u, 0:1], rstd[:, u:u + 1], ALU.subtract, ALU.mult)
            ins.then_inc(S["f0_ready"], 1)

            for l in range(2):
                dve.wait_ge(S["fold_taken"], 2 * l + 1)
                v.tensor_tensor(wv_lo[l][:, :], wfull[l], wback[l], ALU.subtract).then_inc(S["folded_low"], 1)

            def fT_low(q):
                v.tensor_tensor(fT[:, 1, :], bank[6][:, :], fT[:, 0, :], ALU.subtract).then_inc(S["fT_lo"], 1)

            dve.wait_ge(S["fT_hi"], 1)
            fT_low(0)
            words(XH)

            H = [XH[:, w, :, :].rearrange("p a j -> p (a j)") for w in range(3)]
            t1, t2, t3 = (T1[:, i, :, :].rearrange("p a j -> p (a j)") for i in range(3))
            t4 = T2[:, 1, :, :].rearrange("p a j -> p (a j)")
            for bit in range(BITS - 1, 0, -1):
                low = (1 << bit) - 1
                link(v.tensor_scalar(t1, H[0], 31 - bit, 31, SHL, SAR))
                link(v.scalar_tensor_tensor(H[0], t1, low, H[0], AND, XOR))
                for w in (1, 2):
                    v.tensor_scalar(t1, H[w], 31 - bit, 31, SHL, SAR)
                    link(v.tensor_tensor(t2, H[0], H[w], XOR))
                    link(v.tensor_tensor(t3, t2, t1, OR))
                    v.scalar_tensor_tensor(H[0], t3, low, H[0], AND, XOR)
                    link(v.tensor_tensor(t4, t3, t1, XOR))
                    link(v.scalar_tensor_tensor(H[w], t4, low, H[w], AND, XOR))
            link(v.tensor_tensor(H[1], H[1], H[0], XOR))
            link(v.tensor_tensor(H[2], H[2], H[1], XOR))
            link(v.tensor_scalar(t1, H[2], 1, None, SHR))
            for sh, src, dst in ((1, t1, t2), (2, t2, t3), (4, t3, t1), (8, t1, t2)):
                link(v.scalar_tensor_tensor(dst, src, sh, src, SHR, XOR))
            for w in range(3):
                ins = v.tensor_tensor(H[w], H[w], t2, XOR)
            link(ins)
            join(XH)
            link(v.tensor_scalar(T3[:, 0, :], key, 6, None, SHR))
            link(v.tensor_scalar(T3[:, 1, :], key, 63, 9, AND, SHL))
            link(v.tensor_tensor(T3[:, 2, :], T3[:, 1, :], npoint[:, :], OR))
            v.tensor_scalar(split[:, 0, :], T3[:, 0, :], float(2 ** 15), None, ALU.mult)
            v.tensor_copy(split[:, 1, :], T3[:, 2, :]).then_inc(S["split_done"], 1)
            dve.wait_ge(S["split_done"], 1)
            cut(slice(0, 32), chunks_h, "chunks_h_done", 64)

            dve.wait_ge(S["own_psum"], 1)
            v.tensor_copy(own[:, :, :], bank[0][:, 0:128].rearrange("p (a n) -> p a n", a=2)).then_inc(S["own_ready"], 1)
            dve.wait_ge(S["own_ready"], 1)

            for j in range(BH, 2 * B):
                i, slot, half = j - BH, j % 4, j % 2
                dve.wait_ge(S[f"rows_in{slot}"], 16 * (i // 4) + 16)
                for nt in range(NT):
                    dve.wait_ge(S["low_ready"], NT * i + nt + 1)
                    c, r = NT * j + nt, 2 * B * NT + NT * j + nt
                    ins = v.scalar_tensor_tensor(low_dif[:, 4 * half + nt, :], key_rows[:, slot, 0, :],
                                                 own[:, 0, c:c + 1], low_dif[:, 4 * half + nt, :],
                                                 ALU.subtract, ALU.is_lt, accum_out=ranks[:, r:r + 1])
                ins.then_inc(S["dve_counted"], 1)
            dve.wait_ge(S["act_counted"], CMP)
            dve.wait_ge(S["dve_counted"], 2 * B - BH)
            v.tensor_scalar(ranks[:, 0:CMP * NT], counts[:, :], -0.5, 0.5 * (N - 1), ALU.mult, ALU.add)\
                .then_inc(S["ranked"], 1)
            dve.wait_ge(S["ranked"], 1)

            def prepare(q, j):
                u, l = PASSES[q]
                par = q % 2

                def one_hot(b, half):
                    n = 2 * (BH * q + b) + half
                    if n >= 4:
                        dve.wait_ge(S["sorted_psum"], n - 3)
                    for m in range(M):
                        for i in range(2):
                            r = (m * B + BH * u + b) * NT + 2 * half + i
                            ins = v.tensor_scalar(perm[:, n % 4, 2 * m + i, :], iota[:, :],
                                                  ranks[:, r:r + 1], None, ALU.is_equal)
                    ins.then_inc(S["onehot"], 1)

                if j < 2 * BH:
                    one_hot(j // 2, j % 2)
                if j == 1 and q:
                    dve.wait_ge(S["fT_hi"], q + 1)
                    fT_low(q)
                elif 4 <= j < 4 + 2 * BH and j % 2 == 0:
                    b = j // 2 - 2
                    dve.wait_ge(S["sorted_sb"], 3 * (BH * q + b + 1))
                    if q or b:
                        dve.wait_ge(S["key_lo"], BH * q + b)
                    v.tensor_tensor(s_lo[:, :], Sx[par][:, b, :], s_hi[:, :], ALU.subtract).then_inc(S["sorted_low"], 1)
                if 4 <= j < 4 + 2 * BH and j % 2 and q == 0 and j // 2 >= 4:
                    b = j // 2 - 2
                    dve.wait_ge(S["sorted_low"], b + 1)
                    for h in range(HEADS):
                        ins = v.tensor_scalar(klo[par][:, b, h::HEADS], s_lo[:, :], headmask[:, h:h + 1], None, ALU.mult)
                    ins.then_inc(S["key_lo"], 1)

            def value_columns(p, c):
                w = slice(VCW * c, VCW * c + VCW)
                dve.wait_ge(S["vT_hi"], VC * p + c + 1)
                v.tensor_tensor(vT[:, 1, w], bank[6 + c % 2][:, 0:VCW], vT[:, 0, w], ALU.subtract)\
                    .then_inc(S["vT_lo"], 1)

            def finish(p):
                u, l = PASSES[p]
                inverse_root(l + 1)
                for g in range(l + 1):
                    link(v.tensor_scalar(ymax[:, g, 0:N], ymax[:, g, 0:N], mv[:, g, 0:1], rstd[:, g:g + 1],
                                         ALU.subtract, ALU.mult))
                    dst = F1[:, u, :] if l == 0 else F2[:, g, :]
                    v.scalar_tensor_tensor(dst, ymax[:, g, 0:N], 0.2, ymax[:, g, 0:N], ALU.mult, ALU.max)\
                        .then_inc(S["f1_ready" if l == 0 else "f2_ready"], 1)

            def stats(src):
                link(v.bn_stats(lst[:, :], src))
                to_root(v.bn_aggr(mv[:, 0, :], lst[:, :]))

            def gated(u):
                w = slice(128 * u, 128 * u + 128)
                for m in range(4):
                    dve.wait_ge(S["ffn_g"], 4 * u + m + 1)
                    v.scalar_tensor_tensor(x4T[:, m, w], bank[m][:, 128:256], b12[:, 4 + m:5 + m], gate[:, m, w],
                                           ALU.add, ALU.mult).then_inc(S["ffn_x4"], 1)

            def ffn_store(u):
                dve.wait_ge(S["ffn_o"], u + 1)
                v.tensor_tensor(outb[:, u, :], bank[4 + u][:, :], res[:, u, :], ALU.add).then_inc(S["out_ready"], 1)

            def after(u, j):
                x = X[:, u, :]
                if j == 0 and u == 0:
                    dve.wait_ge(S["bind_in"], 16 * 5)
                    wb, sgn = (a.rearrange("p a (h e) -> p (a h) e", h=4) for a in (bind, sgb))
                    link(v.tensor_reduce(alpha[:, :], wb, AX.X, ALU.add, apply_absolute_value=True))
                    link(v.tensor_scalar(alpha[:, :], alpha[:, :], 1.0 / 128, None, ALU.mult))
                    link(v.tensor_scalar(sgn, wb, 0.0, 2.0, ALU.is_ge, ALU.mult))
                    link(v.tensor_scalar(sgn, sgn, -1.0, None, ALU.add))
                    link(v.tensor_tensor(sgn, sgn, spread(alpha[:, :], 128), ALU.mult))
                    link(v.tensor_tensor(sgn, sgn, wb, ALU.subtract))
                    link(v.tensor_tensor(wb, sgn, wb, ALU.add))
                elif j == 1:
                    dve.wait_ge(S["h3_psum"], u + 1)
                    stats(bank[6][:, :])
                elif j == 2:
                    inverse_root(1)
                    link(v.tensor_scalar(tmp[:, 0, :], bank[6][:, :], mv[:, 0, 0:1], rstd[:, 0:1], ALU.subtract, ALU.mult))
                    link(v.scalar_tensor_tensor(tmp[:, 1, :], tmp[:, 0, :], 0.2, tmp[:, 0, :], ALU.mult, ALU.max))
                    link(v.tensor_tensor(x, x, tmp[:, 1, :], ALU.add))
                    stats(x)
                elif j == 3:
                    inverse_root(1)
                    link(v.tensor_scalar(xn[:, u, :], x, mv[:, 0, 0:1], rstd[:, 0:1], ALU.subtract, ALU.mult))
                    for a in range(3):
                        ins = v.tensor_tensor(qkv[:, a, :], xn[:, u, :], bind[:, a, :], ALU.mult)
                    ins.then_inc(S["att_in"], 1)
                    if u == 1:
                        gated(0)
                elif j == 5:
                    dve.wait_ge(S["att_sg"], u + 1)
                    v.tensor_tensor(sgm[:, :, :], sg[:, :, :], window(causal, 0, [[0, 4], [1, 128]]), ALU.mult)\
                        .then_inc(S["att_m"], 1)
                elif j == 7:
                    dve.wait_ge(S["att_o"], u + 1)
                    link(v.tensor_tensor(x, bank[7][:, :], x, ALU.add))
                    stats(x)
                elif j == 8:
                    inverse_root(1)
                    v.tensor_scalar(xn[:, u, :], x, mv[:, 0, 0:1], rstd[:, 0:1], ALU.subtract, ALU.mult)\
                        .then_inc(S["ffn_x"], 1)
                    v.tensor_tensor(res[:, u, :], x, b3row, ALU.add).then_inc(S["x_updated"], 1)
                    if u == 1:
                        dve.wait_ge(S["x_updated"], 2)
                        ffn_store(0)

            for j in range(PREP):
                prepare(0, j)
            for p, (u, l) in enumerate(PASSES):
                base = STEPS * p
                par = p % 2

                def softmax_in(t, k):
                    s = base + t
                    sc = by_head(bank[k][0:ROWS, 0:BH * COLS])
                    dve.wait_ge(S["sc_ready"], s + 1)
                    v.tensor_reduce(heads(mx[0:ROWS, k, :]), sc, AX.X, ALU.max).then_inc(S["mx_done"], 1)
                    dve.wait_ge(S["mx_done"], s + 1)
                    freed(dve, s, "e_ready")
                    v.tensor_tensor(by_head(dif[0:ROWS, k, :]), sc,
                                    spread(heads(mx[0:ROWS, k, :]), SPAN), ALU.subtract).then_inc(S["d_ready"], 1)

                def softmax_sum(t, k):
                    s = base + t
                    dve.wait_ge(S["e_ready"], s + 1)
                    v.tensor_reduce(heads(sm[0:ROWS, k, :]), by_head(ex[0:ROWS, k, :]),
                                    AX.X, ALU.add).then_inc(S["sum_done"], 1)
                    dve.wait_ge(S["sum_done"], s + 1)
                    freed(dve, s, "a_ready")
                    v.reciprocal(rs[0:ROWS, k, :], sm[0:ROWS, k, :]).then_inc(S["r_ready"], 1)

                def outputs(t, k):
                    s = base + t
                    w = ROWS * (l + 1)
                    dve.wait_ge(S["y_psum"], s + 1)
                    if isinstance(t, int) and t == 0:
                        dve.wait_ge(S["z_ready"], Z_BEFORE[p + 1])
                    freed(dve, s, "ymax_done")

                    def by_point(a):
                        return a.rearrange("p (g n i) -> p g n i", g=l + 1, n=G)

                    v.tensor_tensor(by_point(ys[:, k, 0:w]), by_point(bank[Y_BANK][:, 0:w]),
                                    window(z[:, par, 0, :], G * t, [[NPAD, l + 1], [1, G], [0, K]]), ALU.add)\
                        .then_inc(S["ys_done"], 1)
                    dve.wait_ge(S["ys_done"], s + 1)
                    real = LAST_ROWS if isinstance(t, int) and t == STEPS - 1 else ROWS
                    for g in range(l + 1):
                        v.bn_stats(bst[:, g, bass.ds(t, 1), :], ys[:, k, ROWS * g:ROWS * g + real])
                    v.tensor_reduce(ymax[:, 0:l + 1, bass.ds(G * t, G)], by_point(ys[:, k, 0:w]),
                                    AX.X, ALU.max).then_inc(S["ymax_done"], 1)

                def step(t, k):
                    if live(t - 4):
                        outputs(t - 4, k)
                    if live(t - 1):
                        softmax_sum(t - 1, 1 - k)
                    if live(t):
                        softmax_in(t, k)

                first = {3: [lambda p=p: finish(p - 1)]} if p else {}
                pipeline(dve, step, 4, spare_work(p, first, value_columns, prepare, after))
                dve.wait_ge(S["ymax_done"], base + STEPS)
                for g in range(l + 1):
                    ins = v.bn_aggr(mv[:, g, :], bst[:, g, :, :].rearrange("p a b -> p (a b)"))
                to_root(ins)
            finish(len(PASSES) - 1)
            for j in range(AFTER):
                after(1, j)
            gated(1)
            ffn_store(1)


def kernel(**inputs):
    import concourse.bacc as bacc
    from concourse.bass_utils import run_bass_kernel_spmd

    pre = "L0_"
    arrays = {
        "x": inputs["x"], "ctx_4096": inputs["ctx_4096"],
        "wl0": inputs[pre + "xattn_W_lin1"], "wl1": inputs[pre + "xattn_W_lin2"],
        "bl0": inputs[pre + "xattn_b_lin1"], "bl1": inputs[pre + "xattn_b_lin2"],
        "wc0T": np.transpose(inputs[pre + "xattn_W_conv1"]), "wc1T": np.transpose(inputs[pre + "xattn_W_conv2"]),
        "w3cT": np.transpose(inputs[pre + "xattn_W_conv3"]),
        "bv_q": inputs[pre + "attn_bv_q"], "bv_k": inputs[pre + "attn_bv_k"], "bv_v": inputs[pre + "attn_bv_v"],
        "w12T": np.transpose(inputs[pre + "ffn_w12"]), "b12": np.transpose(np.reshape(inputs[pre + "ffn_b12"], (8, 128))),
        "w3T": np.transpose(inputs[pre + "ffn_w3"]), "b3": inputs[pre + "ffn_b3"],
        **constants(),
    }
    arrays = {f"in_{k}": np.ascontiguousarray(v) for k, v in arrays.items()}
    nc = bacc.Bacc("TRN2", target_bir_lowering=False, num_devices=1)
    d = {k[3:]: nc.dram_tensor(k, a.shape, mybir.dt.from_np(a.dtype), kind="ExternalInput").ap()
         for k, a in arrays.items()}
    d["out"] = nc.dram_tensor("out", (B, C, N), F32, kind="ExternalOutput").ap()
    build(nc, d)
    result = run_bass_kernel_spmd(nc, [arrays], core_ids=[0])
    return result.results[0]["out"]
```

```python
from contextlib import ExitStack
from math import log, sqrt

import numpy as np

import concourse.bass as bass
from concourse import mybir
from concourse.alu_op_type import AluOpType as ALU

ACT = mybir.ActivationFunctionType
AX = mybir.AxisListType
F32 = mybir.dt.float32
F16 = mybir.dt.float16
BF16 = mybir.dt.bfloat16
I32 = mybir.dt.int32

B, C, N = 8, 32, 512
BH = 4
HALVES = B // BH
M = 4
K = 10
HEADS = 4
BITS = 10
NT = N // 128
CMP = 2 * B + BH
EPS = 1e-5

G = 12
ROWS = G * K
SPAN = G + K - 1
COLS = HEADS * SPAN
STEPS = -(-N // G)
NPAD = STEPS * G
LEFT = K // 2
SW = 528
HEAD_SCALE = 1.0 / sqrt(32.0)
W_SCALE = 1024.0
PERMS = ([2, 0, 3, 1], [1, 3, 0, 2])
OUTS = (32, 64)
LAST_ROWS = (N - (STEPS - 1) * G) * K


def constants():
    def short(a):
        return (a.astype(np.float32).view(np.uint32) & np.uint32(0xFFFF0000)).view(np.float32)

    def pairs(a):
        w = a.astype(np.float32).view(np.uint32) >> np.uint32(16)
        return (w[:, 0::2] | (w[:, 1::2] << np.uint32(16))).view(np.int32)

    n, p = np.arange(G)[:, None], np.arange(SPAN)[None, :]
    far = float(short(np.array(-1e30)))
    inner = np.where((p >= n) & (p <= n + K - 1), 0.0, far)
    edge = np.where(p < LEFT, far, inner)
    for i in range(LEFT):
        edge[i, i + K] = sqrt(32.0) * log(LEFT - i)
    parts, rest = [], edge.astype(np.float64)
    for _ in range(3):
        part = short(rest)
        rest = np.where(edge == far, 0.0, rest - part.astype(np.float64))
        parts.append(part)
    edge3 = np.concatenate(parts, 0)
    ind = np.repeat(np.eye(G), K, axis=1)
    q = np.arange(128)
    s, t = q[:, None], q[None, :]
    return {
        "c_ident": np.eye(128, dtype=np.float32),
        "c_rows": np.pad(np.concatenate([ind] * 3, 0), ((0, 0), (0, 128 - ROWS))).astype(np.float32),
        "c_inner": inner.astype(np.float32),
        "c_edge": edge3.astype(np.float32),
        "c_headmask": ((q[:, None] % C) // 8 == np.arange(HEADS)).astype(np.float32),
        "c_iota": np.tile(np.arange(N, dtype=np.float16), (128, 1)),
        "c_causal": ((s // C == t // C) & (s <= t)).astype(np.float32),
        "c_key_rows": pairs(np.stack([np.ones(CMP * N), -np.ones(CMP * N), np.tile(np.arange(N) % 256, CMP)])),
        "c_to_points": (np.eye(3)[:, None, :, None] * (q // 16 == np.arange(B)[:, None])[None, :, None, :])
        .reshape(3 * B, 3 * 128).astype(np.float32),
        "c_n": np.tile((q[:, None] % 16) * 32 + np.arange(32), (1, 2)).astype(np.int32),
    }


def build(nc, d):
    ctx = ExitStack()
    with ctx:
        def sb(name, shape, dt):
            return ctx.enter_context(nc.sbuf_tensor(name, shape, dt))

        def sem(name):
            return ctx.enter_context(nc.semaphore(name))

        bank = [ctx.enter_context(nc.psum_tensor(f"bank{i}", [128, 512], F32)) for i in range(8)]

        chunk_dram = nc.dram_tensor("chunk_scratch", (4, CMP * N), BF16, kind="Internal").ap()
        split_dram = nc.dram_tensor("split_scratch", (2, 2, B * N), F32, kind="Internal").ap()

        ident = sb("ident", [128, 128], F32)
        rows_ind = sb("rows_ind", [3 * G, 128], BF16)
        inner_mask = sb("inner_mask", [G, SPAN], BF16)
        edge_mask = sb("edge_mask", [3 * G, SPAN], BF16)
        headmask = sb("headmask", [128, HEADS], F32)
        iota = sb("iota", [128, N], F16)
        ident16 = sb("ident16", [128, 128], F16)
        npoint = sb("npoint", [128, 2 * 32], I32)
        blin = [sb(f"blin{l}", [64, 1], F32) for l in range(2)]
        w3bd = sb("w3bd", [128, 4, 128], F32)
        wv_hi = [sb(f"wv_hi{l}", [128, OUTS[l]], F16) for l in range(2)]
        wv_lo = [sb(f"wv_lo{l}", [128, OUTS[l]], F16) for l in range(2)]
        wcen = [sb(f"wcen{l}", [128, BH * OUTS[l]], F32) for l in range(2)]
        wdif = [sb(f"wdif{l}", [128, BH * OUTS[l]], F32) for l in range(2)]
        bias = [sb(f"bias{l}", [128, 1], F32) for l in range(2)]
        eps_col = sb("eps_col", [128, 1], F32)

        X = sb("X", [128, HALVES, N], F32)
        FX = sb("FX", [128, HALVES, N], F32)
        F1 = sb("F1", [128, HALVES, N], F32)
        ymax = sb("ymax", [128, 4, NPAD], F32)
        z = sb("z", [128, 2, 2, NPAD], F32)
        cen16 = sb("cen16", [128, N], F16)
        cen32 = sb("cen32", [128, N], F32)
        fT = sb("fT", [128, 2, 512], F16)
        bst = sb("bst", [128, 2, STEPS, 6], F32)
        mv = sb("mv", [128, 2, 2], F32)
        rstd = sb("rstd", [128, 2], F32)
        nmr = sb("nmr", [128, 2], F32)
        ranks = sb("ranks", [128, M * B * NT], F32)
        counts = sb("counts", [128, CMP * NT], F32)
        lst = sb("lst", [128, 6], F32)


        xq = sb("xq", [128, 2, (BH - 1) * ROWS + 128], F16)
        dif = sb("dif", [128, 2, BH * COLS], F32)
        mx = sb("mx", [128, 2, BH * HEADS], F32)
        ex = sb("ex", [128, 2, BH * COLS], F32)
        sm = sb("sm", [128, 2, BH * HEADS], F32)
        rs = sb("rs", [128, 2, BH * HEADS], F32)
        at = sb("at", [128, 2, BH * COLS], F32)
        atT = sb("atT", [COLS, 2, BH * ROWS], F32)
        wlin = [at[0:64, l, 0:256] for l in range(2)]
        wconvT = [atT[0:64, l, 0:128] for l in range(2)]
        val = sb("val", [COLS, 2, BH * 64], F32)
        ys = sb("ys", [128, 2, 2 * ROWS], F32)

        VW = HEADS * (SW - 3)
        SET = 2 * BH * HEADS * SW + 2 * BH * SW + 2 * BH * NPAD
        AREA = 2 * M * NT * N + 2 * SET + 2 * VW
        arena = sb("arena", [128, AREA], BF16)
        at_, operands = 0, []
        for width in (CMP * N, CMP * N, CMP * 128, CMP * 128):
            operands.append(arena[:, at_:at_ + width])
            at_ += width
        RA, RB, LA, LB = operands

        def carver(v, at):
            def take(count, dt=F32):
                nonlocal at
                n = count * (2 if dt == F32 else 1)
                at += n
                return v[:, at - n:at].bitcast(dt)
            return take

        take = carver(arena, 0)
        perm = take(2 * M * NT * N, F16).rearrange("p (s m r) -> p s m r", s=8, r=N)
        khi, klo, Sx, Frep = [], [], [], []
        for _ in range(2):
            khi.append(take(BH * HEADS * SW, F16).rearrange("p (b c) -> p b c", b=BH))
            klo.append(take(BH * HEADS * SW, F16).rearrange("p (b c) -> p b c", b=BH))
            Sx.append(take(BH * SW).rearrange("p (b s) -> p b s", b=BH))
            Frep.append(take(BH * NPAD).rearrange("p (b n) -> p b n", b=BH))
        vT = take(2 * VW, F16).rearrange("p (a c) -> p a c", a=2)
        take = carver(arena, 2 * M * NT * N + SET)
        key_rows = take(4 * 2 * N).rearrange("p (s a n) -> p s a n", s=4, a=2)
        low_dif = take(8 * N).rearrange("p (s n) -> p s n", s=8)
        XK, T1, T2, XH = (take(3 * 64).bitcast(I32).rearrange("p (w a j) -> p w a j", w=3, a=2) for _ in range(4))
        T3 = take(4 * 64).bitcast(I32).rearrange("p (c j) -> p c j", c=4)
        split = take(2 * 64).rearrange("p (c j) -> p c j", c=2)
        xyz, xyz_r, xyz_up = (take(3 * 32).rearrange("p (c j) -> p c j", c=3) for _ in range(3))
        xyz_q = take(3 * 32).bitcast(I32).rearrange("p (c j) -> p c j", c=3)
        to_points = take(3 * 128)[0:3 * B, :]
        wfull, wback = ([take(OUTS[l]) for l in range(2)] for _ in range(2))
        crd = ymax[0:3 * B, 0, 0:N]
        cs = sb("cs", [3 * B, 16], F32)
        scales = sb("scales", [128, 6], F32)

        chunks = ys[:, 0, 0:128].bitcast(BF16).rearrange("p (c j) -> p c j", c=4)
        chunks_h = ys[0:64, 0, 128:192].bitcast(BF16).rearrange("p (c j) -> p c j", c=4)
        split_rows = ex[0:2 * B * NT, :, :].rearrange("p a b -> p (a b)")[:, 0:256].rearrange("p (a n) -> p a n", a=2)
        s_hi = sb("s_hi", [128, SW], F16)
        s_lo = sb("s_lo", [128, SW], F16)
        own = sb("own", [128, 2, 2 * B * NT], F32)

        take = carver(arena, 0)
        w12T = take(4 * 1024).rearrange("p (k m) -> p k m", k=4)
        w3T = take(4 * 512).rearrange("p (k m) -> p k m", k=4)
        bind, sgb = (take(3 * N).rearrange("p (a n) -> p a n", a=3) for _ in range(2))
        b12 = sb("b12", [128, 8], F32)
        F2 = take(2 * N).rearrange("p (a n) -> p a n", a=2)
        tmp = take(2 * N).rearrange("p (a n) -> p a n", a=2)
        b3row, causal = take(N), take(128)
        qkv = take(3 * N).rearrange("p (a n) -> p a n", a=3)
        qkT = take(8 * 128).rearrange("p (a n) -> p a n", a=8)
        sg = take(4 * 128).rearrange("p (a n) -> p a n", a=4)
        sgm = take(4 * 128).rearrange("p (a n) -> p a n", a=4)
        xn = take(2 * N).rearrange("p (a n) -> p a n", a=2)
        xnT = take(4 * 256).rearrange("p (a n) -> p a n", a=4)
        gate = take(4 * 256).rearrange("p (a n) -> p a n", a=4)
        x4T = take(4 * 256).rearrange("p (a n) -> p a n", a=4)
        outb = take(2 * N).rearrange("p (a n) -> p a n", a=2)
        res = take(2 * N).rearrange("p (a n) -> p a n", a=2)

        alpha = sb("alpha", [128, 12], F32)

        def spread(v, n):
            return bass.AP(v.tensor, v.offset, list(v.ap) + [[0, n]])

        S = {name: sem(name) for name in (
            "coords x_in consts masks fold_in key_rows_in weights first_consts points_in chunk_out chunk_in split_out split_in rows_in0 rows_in1 rows_in2 rows_in3 "
            "bind_in ffn_w alpha_ready bound frep0 frep1 stored "
            "scales_ready scales_psum chunks_done chunks_h_done chunk_h_in split_done own_psum own_ready cmp_ready act_counted low_ready dve_counted ranked "
            "folded fold_taken folded_low zeroed ident16_ready "
            "dve_link act_link pool_link "
            "f0_ready f1_ready f2_ready fT_psum fT_hi fT_lo onehot sorted_psum sorted_sb sorted_low key_hi key_lo "
            "cen_done z_psum z_ready vT_psum vT_hi vT_lo "
            "x_main edge_done x_ready sc_ready mx_done d_ready e_ready sum_done r_ready a_ready aT_psum aT_sb "
            "v_psum v_sb y_psum ys_done ymax_done "
            "var_ready std_ready "
            "h3_psum x_updated att_in att_T att_Tc att_sc att_sg att_m att_o ffn_x ffn_T ffn_Tc "
            "ffn_h ffn_g ffn_x4 ffn_o out_ready").split()}

        block = ctx.enter_context(nc.Block())

        def chain(eng, name):
            count = [0]

            def link(ins):
                count[0] += 1
                ins.then_inc(S[name], 1)
                eng.wait_ge(S[name], count[0])
            return link

        PEEL = 6

        def pipeline(eng, p, step, lag, inserts):
            def insert(t):
                for work in inserts.get(t, ()):
                    work()

            for t in range(PEEL):
                step(p, t, (p + t) % 2)
                insert(t)
            end = STEPS - 1
            busy = [i for i in range(PEEL // 2, end // 2) if 2 * i in inserts or 2 * i + 1 in inserts]
            lo = PEEL // 2
            for pair in busy + [end // 2]:
                if lo < pair:
                    with eng.Fori(lo, pair) as i:
                        step(p, 2 * i, p % 2)
                        step(p, 2 * i + 1, 1 - p % 2)
                if pair < end // 2:
                    for t in (2 * pair, 2 * pair + 1):
                        step(p, t, (p + t) % 2)
                        insert(t)
                lo = pair + 1
            for t in range(end, STEPS + (lag if p == len(PASSES) - 1 else 0)):
                step(p, t, (p + t) % 2)

        def behind(stage, p, t, k):
            if not isinstance(t, int) or 0 <= t < STEPS:
                stage(p, t, k)
            elif t < 0 < p:
                stage(p - 1, STEPS + t, k)

        def features_ready(eng, u, l):
            eng.wait_ge(S["f0_ready" if l == 0 else "f1_ready"], 1 if l == 0 else u + 1)

        def freed(eng, s, name, lag=2):
            if not isinstance(s, int) or s >= lag:
                eng.wait_ge(S[name], s + 1 - lag)

        def past(eng, q, name, each=1):
            if q >= 2:
                eng.wait_ge(S[name], each * STEPS * (q - 1))

        OWN_AT = 10
        PASSES = [(u, l) for l in range(2) for u in range(HALVES)]
        Z_BEFORE = [0, 1, 2, 4, 6]
        ROOT_AT, FINISH_AT = 4, 5
        VC = 5
        VCW = VW // VC
        PREP = 24
        AFTER = 16

        def features(u, l):
            return FX[:, u, :] if l == 0 else F1[:, u, :]

        def ymax_of(p):
            return (ymax[:, 0:1], ymax[:, 1:2], ymax[:, 2:4], ymax[:, 0:2])[p]

        def spare_work(p, first, values, prepare, after, behind_by=0):
            plan = {t: list(work) for t, work in first.items()}
            if PASSES[p][1] == 0:
                for c in range(VC):
                    plan.setdefault(c + behind_by, []).append(lambda c=c: values(p, c))
            if p + 1 < len(PASSES):
                for j in range(PREP):
                    plan.setdefault(7 + j, []).append(lambda j=j: prepare(p + 1, j))
            else:
                for j in range(AFTER):
                    plan.setdefault(11 + 2 * j, []).append(lambda j=j: after(0, j))
            return plan

        def window(base, n0, step_list):
            v = base[:, bass.ds(n0, 1)]
            return bass.AP(v.tensor, v.offset, [v.ap[0]] + step_list)

        def by_head(v):
            return v.rearrange("p (b s h) -> p b h s", b=BH, h=HEADS)

        def heads(v):
            return v.rearrange("p (b h) -> p b h", b=BH)

        def spread(v, n):
            return bass.AP(v.tensor, v.offset, list(v.ap) + [[0, n]])

        def four(v):
            return v.rearrange("p (a n) -> p a n", a=4)

        SORT_BANK = (6, 7)
        VAL_BANK, Y_BANK = 4, 5

        @block.sync
        def _(sp):
            ctx4 = d["ctx_4096"]
            for c in range(3):
                sp.dma_start(crd[8 * c:8 * c + 8, :], ctx4[:, c, :]).then_inc(S["coords"], 16)
            sp.dma_start(to_points, d["c_to_points"]).then_inc(S["first_consts"], 16)
            for b in range(B):
                sp.dma_start(xyz[16 * b:16 * b + 16, :, :], ctx4[b, 0:3, :].rearrange("c (p j) -> p c j", j=32))\
                    .then_inc(S["points_in"], 16)
            sp.dma_start(npoint[:, :], d["c_n"]).then_inc(S["first_consts"], 16)
            for u in range(HALVES):
                sp.dma_start(X[:, u, :], d["x"][BH * u:BH * u + BH].rearrange("b c n -> (b c) n"))\
                    .then_inc(S["x_in"], 16)
            for dst, name in ((ident, "c_ident"), (headmask, "c_headmask"), (iota, "c_iota")):
                sp.dma_start(dst[:, :], d[name]).then_inc(S["consts"], 16)
            for l in range(2):
                src = d[f"wc{l}T"]
                sp.dma_start(wconvT[l].rearrange("k (r o) -> k r o", o=OUTS[l]),
                             bass.AP(src.tensor, src.offset, [src.ap[0], [0, 128 // OUTS[l]], src.ap[1]]))\
                    .then_inc(S["fold_in"], 16)
                sp.dma_start(wlin[l], d[f"wl{l}"]).then_inc(S["fold_in"], 16)
                sp.dma_start(blin[l][:, :], d[f"bl{l}"].rearrange("(j a) -> j a", a=1)).then_inc(S["fold_in"], 16)
            def constant_rows(v, rows, row):
                tiles = v.shape[1] == CMP * 128
                reps, words = (CMP, 64) if tiles else (1, v.shape[1] // 2)
                src = d["c_key_rows"][row:row + 1, :]
                for r in rows:
                    sp.dma_start(v[r::32, :].bitcast(I32).rearrange("g (b n) -> g b n", b=reps),
                                 bass.AP(src.tensor, src.offset, [[64 if tiles else 0, NT], [0, reps], [1, words]]))\
                        .then_inc(S["key_rows_in"], 16)

            constant_rows(RA, (3, 4, 5), 1)
            constant_rows(LA, (0, 1, 2), 0)
            for v, rows, row in ((RB, (2, 3), 1), (RB, (1,), 2), (LB, (0, 1), 0), (LB, (3,), 2)):
                constant_rows(v, rows, row)
            def operands_in(j0, j1, name):
                for i, (R, L, r, l) in enumerate(((RB, LB, 0, 2), (RA, LA, 0, 3), (RA, LA, 1, 4), (RA, LA, 2, 5))):
                    src = chunk_dram[i:i + 1, N * j0:N * j1]
                    sp.dma_start(R[r::32, N * j0:N * j1], bass.AP(src.tensor, src.offset, [[0, NT], src.ap[1]]))\
                        .then_inc(S[name], 16)
                    sp.dma_start(L[l::32, 128 * j0:128 * j1].rearrange("g (j n) -> g j n", n=128),
                                 src[0].rearrange("(j g n) -> g j n", g=NT, n=128)).then_inc(S[name], 16)

            sp.wait_ge(S["chunks_done"], 1)
            for m in range(2):
                sp.dma_start(chunk_dram[:, B * N * m:B * N * (m + 1)].rearrange("c (p j) -> p c j", j=32),
                             chunks[:, :, 32 * m:32 * m + 32]).then_inc(S["chunk_out"], 16)
            sp.wait_ge(S["chunk_out"], 16 * 2)
            operands_in(0, 2 * B, "chunk_in")
            sp.wait_ge(S["split_done"], 1)
            sp.dma_start(split_dram.rearrange("a m (p j) -> p a m j", j=32),
                         split.rearrange("p a (m j) -> p a m j", m=2)).then_inc(S["split_out"], 16)
            sp.wait_ge(S["split_out"], 16)
            flat = split_dram.rearrange("a m n -> a (m n)")
            sp.dma_start(split_rows, flat.rearrange("a (r p) -> r a p", p=128)).then_inc(S["split_in"], 16)

            def key_rows_of(j):
                i = j - BH
                row = flat[:, N * j:N * j + N]
                sp.dma_start(key_rows[:, i % 4, :, :],
                             bass.AP(row.tensor, row.offset, [[0, 128], [2 * B * N, 2], [1, N]]))\
                    .then_inc(S[f"rows_in{i % 4}"], 16)

            for j in range(BH, BH + 4):
                key_rows_of(j)
            sp.wait_ge(S["chunks_h_done"], 1)
            sp.dma_start(chunk_dram[:, 2 * B * N:].rearrange("c (p j) -> p c j", j=32), chunks_h[:, :, :])\
                .then_inc(S["chunk_out"], 16)
            sp.wait_ge(S["chunk_out"], 16 * 3)
            operands_in(2 * B, CMP, "chunk_h_in")
            for j in range(BH + 4, 2 * B):
                sp.wait_ge(S["dve_counted"], j - BH - 3)
                key_rows_of(j)

            for p, (u, l) in enumerate(PASSES):
                F = features(u, l)
                features_ready(sp, u, l)
                sp.wait_ge(S["zeroed"], 5)
                past(sp, p, "x_ready")
                for m in range(M):
                    for b in range(BH):
                        sp.dma_start(Frep[p % 2][C * m:C * m + C, b, 0:N], F[C * b:C * b + C, :])\
                            .then_inc(S[f"frep{p % 2}"], 16)
            sp.wait_ge(S["v_psum"], STEPS * 3)
            sp.wait_ge(S["x_ready"], STEPS * 3)
            for i, name in enumerate(("bv_q", "bv_k", "bv_v")):
                row = d[name].rearrange("h e -> (h e)")
                sp.dma_start(bind[:, i, :], bass.AP(row.tensor, row.offset, [[0, 128], [1, N]]))\
                    .then_inc(S["bind_in"], 16)
            b3 = d["b3"]
            sp.dma_start(b3row, bass.AP(b3.tensor, b3.offset, [[0, 128], [1, N]])).then_inc(S["bind_in"], 16)
            sp.dma_start(causal, d["c_causal"]).then_inc(S["bind_in"], 16)
            sp.dma_start(w12T, d["w12T"].rearrange("(k p) m -> p k m", p=128)).then_inc(S["ffn_w"], 16)
            sp.dma_start(w3T, d["w3T"].rearrange("(k p) m -> p k m", p=128)).then_inc(S["ffn_w"], 16)
            for u in range(HALVES):
                sp.wait_ge(S["out_ready"], u + 1)
                sp.dma_start(d["out"][BH * u:BH * u + BH].rearrange("b c n -> (b c) n"), outb[:, u, :])\
                    .then_inc(S["stored"], 16)
            sp.wait_ge(S["stored"], 16 * HALVES)

        @block.gpsimd
        def _(pool):
            g = nc.gpsimd
            link = chain(pool, "pool_link")
            for dst, name in ((rows_ind, "c_rows"), (inner_mask, "c_inner"), (edge_mask, "c_edge")):
                pool.dma_start(dst[:, :], d[name]).then_inc(S["masks"], 16)
            link(g.memset(w3bd[:, :, :], 0.0))
            for b in range(BH):
                o = slice(C * b, C * b + C)
                r = 64 * (b % 2)
                for dst, src in ((w3bd[o, 0, o], d["w3cT"][0:C, :]), (w3bd[o, 1, o], d["w3cT"][C:2 * C, :]),
                                 (w3bd[r:r + 64, 2 + b // 2, o], d["w3cT"][2 * C:4 * C, :])):
                    pool.dma_start(dst, src).then_inc(S["weights"], 16)
            pool.dma_start(b12[:, :], d["b12"]).then_inc(S["weights"], 16)
            g.memset(xq[:, :, BH * ROWS:], 0.0)
            g.memset(z[:, :, :, N:NPAD], 0.0).then_inc(S["zeroed"], 1)

            pool.wait_ge(S["own_ready"], 1)

            def lower_differences(j):
                i, slot, half = j - BH, j % 4, j % 2
                pool.wait_ge(S[f"rows_in{slot}"], 16 * (i // 4) + 16)
                freed(pool, i, "dve_counted")
                for nt in range(NT):
                    g.tensor_scalar(low_dif[:, 4 * half + nt, :], key_rows[:, slot, 1, :], -1.0,
                                    own[:, 1, NT * j + nt:NT * j + nt + 1], ALU.mult, ALU.add)\
                        .then_inc(S["low_ready"], 1)

            for j in range(BH, 2 * B):
                lower_differences(j)

            pool.wait_ge(S["ranked"], 1)
            for k in range(2):
                g.memset(Sx[k][:, :, 0:LEFT], 0.0)
                g.memset(Sx[k][:, :, LEFT + N + 4:SW], 0.0).then_inc(S["zeroed"], 1)
                g.memset(Frep[k][:, :, N:NPAD], 0.0).then_inc(S["zeroed"], 1)

            def form_x(p, t, k):
                s = STEPS * p + t
                sx, fr = Sx[p % 2], Frep[p % 2]
                freed(pool, s, "sc_ready")
                if isinstance(t, int) and t == 0:
                    pool.wait_ge(S[f"frep{p % 2}"], 16 * 16 * (p // 2 + 1))
                    pool.wait_ge(S["sorted_sb"], 3 * BH * (p + 1))
                src = window(sx[:, 0, :], G * t, [[SW, BH], [1, G], [1, K]])
                cen = window(fr[:, 0, :], G * t, [[NPAD, BH], [1, G], [0, K]])
                out = xq[:, k, 0:BH * ROWS].rearrange("p (b n i) -> p b n i", b=BH, n=G)
                ins = g.tensor_tensor(out, src, cen, ALU.subtract)
                if isinstance(t, int) and t == 0:
                    ins.then_inc(S["x_main"], 1)
                    pool.wait_ge(S["x_main"], p + 1)
                    for n in range(LEFT):
                        w = LEFT - n
                        ins = g.tensor_tensor(out[:, :, n, 0:w], window(sx[:, 0, :], n + K, [[SW, BH], [0, w]]),
                                              window(fr[:, 0, :], n, [[NPAD, BH], [0, w]]), ALU.subtract)
                        if n < LEFT - 1:
                            ins.then_inc(S["edge_done"], 1)
                    pool.wait_ge(S["edge_done"], (LEFT - 1) * (p + 1))
                ins.then_inc(S["x_ready"], 1)

            def normalise(p, t, k):
                s = STEPS * p + t
                pool.wait_ge(S["r_ready"], s + 1)
                freed(pool, s, "aT_psum")
                g.tensor_tensor(by_head(at[0:ROWS, k, :]), by_head(ex[0:ROWS, k, :]),
                                spread(heads(rs[0:ROWS, k, :]), SPAN), ALU.mult).then_inc(S["a_ready"], 1)

            def step(p, t, k):
                if isinstance(t, int) and t + 1 >= STEPS:
                    if t + 1 == STEPS and p + 1 < len(PASSES):
                        form_x(p + 1, 0, 1 - k)
                else:
                    form_x(p, t + 1, 1 - k)
                behind(normalise, p, t - 1, 1 - k)

            def binding(a, i):
                wb, sgn = (x[:, a, :].rearrange("p (h e) -> p h e", h=4) for x in (bind, sgb))
                if i == 0:
                    pool.wait_ge(S["alpha_ready"], a + 1)
                    link(g.tensor_scalar(sgn, wb, 0.0, 2.0, ALU.is_ge, ALU.mult))
                elif i == 1:
                    link(g.tensor_scalar(sgn, sgn, -1.0, None, ALU.add))
                elif i == 2:
                    link(g.tensor_tensor(sgn, sgn, spread(alpha[:, 4 * a:4 * a + 4], 128), ALU.mult))
                elif i == 3:
                    link(g.tensor_tensor(sgn, sgn, wb, ALU.subtract))
                else:
                    g.tensor_tensor(wb, sgn, wb, ALU.add).then_inc(S["bound"], 1)

            form_x(0, 0, 0)
            for p in range(len(PASSES)):
                spare = {}
                if p == len(PASSES) - 1:
                    for a in range(3):
                        for i in range(5):
                            spare[6 + 5 * a + i] = [lambda a=a, i=i: binding(a, i)]
                pipeline(pool, p, step, 1, spare)

        @block.scalar
        def _(act):
            link = chain(act, "act_link")
            roots = [0]

            def root(n):
                roots[0] += 1
                act.wait_ge(S["var_ready"], roots[0])
                nc.scalar.activation(rstd[:, 0:n], mv[:, 0:n, 1], ACT.Sqrt, bias=eps_col[:, 0:1])\
                    .then_inc(S["std_ready"], 1)

            act.wait_ge(S["dve_link"], 3)
            act.wait_ge(S["consts"], 16 * 3)
            nc.scalar.copy(ident16[:, :], ident[:, :]).then_inc(S["ident16_ready"], 1)

            def prepare(q, j):
                u, l = PASSES[q]
                par = q % 2

                def sorted_out(b):
                    act.wait_ge(S["sorted_psum"], NT * (BH * q + b + 1))
                    if b == 0:
                        act.wait_ge(S["zeroed"], 5)
                        past(act, q, "x_ready")
                        past(act, q, "v_psum")
                    n = 3 * (BH * q + b)
                    nc.scalar.copy(Sx[par][:, b, LEFT:LEFT + N], bank[SORT_BANK[b % 2]][:, :]).then_inc(S["sorted_sb"], 1)
                    act.wait_ge(S["sorted_sb"], n + 1)
                    nc.scalar.copy(Sx[par][:, b, LEFT + N:LEFT + N + 4],
                                   window(Sx[par][:, b, :], LEFT + N - 1, [[0, 4]])).then_inc(S["sorted_sb"], 1)
                    act.wait_ge(S["sorted_sb"], n + 2)
                    if q or b:
                        act.wait_ge(S["sorted_low"], BH * q + b)
                    nc.scalar.copy(s_hi[:, :], Sx[par][:, b, :]).then_inc(S["sorted_sb"], 1)

                def by_heads(keys, src, b, h0, name):
                    for h in (h0, h0 + 1):
                        ins = nc.scalar.activation(keys[par][:, b, h::HEADS], src, ACT.Copy, scale=headmask[:, h:h + 1])
                    if h0:
                        ins.then_inc(S[name], 1)

                def keys_low(b, h0):
                    act.wait_ge(S["sorted_low"], BH * q + b + 1)
                    by_heads(klo, s_lo[:, :], b, h0, "key_lo")

                def z_out(g):
                    act.wait_ge(S["z_psum"], Z_BEFORE[q] + g + 1)
                    past(act, q, "ys_done")
                    nc.scalar.activation(z[:, par, g, 0:N], bank[7][:, :], ACT.Identity, bias=bias[l][:, 0:1])\
                        .then_inc(S["z_ready"], 1)

                if j == 0:
                    features_ready(act, u, l)
                    if q:
                        act.wait_ge(S["z_psum"], Z_BEFORE[q])
                    nc.scalar.copy(cen16[:, :], features(u, l)).then_inc(S["cen_done"], 1)
                    act.wait_ge(S["cen_done"], 2 * q + 1)
                    nc.scalar.copy(cen32[:, :], cen16[:, :]).then_inc(S["cen_done"], 1)
                elif j == 1:
                    act.wait_ge(S["fT_psum"], q + 1)
                    if q:
                        act.wait_ge(S["sorted_psum"], NT * BH * q)
                    nc.scalar.copy(fT[:, 0, :], bank[6][:, :]).then_inc(S["fT_hi"], 1)
                elif j == 3:
                    z_out(0)
                elif j == 6 and l == 1:
                    z_out(1)
                for b in range(BH):
                    at_ = j - 7 - NT * b
                    if at_ in (3, 4) and (q or b < 2):
                        keys_low(b, 2 * (at_ - 3))
                for b in range(BH):
                    at_ = j - 7 - NT * b
                    if at_ == 0:
                        sorted_out(b)
                    elif at_ in (1, 2):
                        by_heads(khi, Sx[par][:, b, :], b, 2 * (at_ - 1), "key_hi")

            def value_columns(p, c):
                act.wait_ge(S["vT_psum"], VC * p + c + 1)
                if p:
                    act.wait_ge(S["v_psum"], STEPS * p)
                nc.scalar.copy(vT[:, 0, VCW * c:VCW * c + VCW], bank[6 + c % 2][:, 0:VCW]).then_inc(S["vT_hi"], 1)

            def gates(u):
                for m in range(4):
                    act.wait_ge(S["ffn_h"], 4 * u + m + 1)
                    nc.scalar.activation(gate[:, m, 128 * u:128 * u + 128], bank[m][:, 0:128], ACT.Silu,
                                         bias=b12[:, m:m + 1]).then_inc(S["ffn_g"], 1)

            def after(u, j):
                if j in (1, 3, 12):
                    root(1)
                    if u == 1 and j == 3:
                        gates(0)
                elif j == 7:
                    for a in range(2):
                        act.wait_ge(S["att_T"], 2 * u + a + 1)
                        nc.scalar.copy(qkT[:, 4 * a:4 * a + 4, :], four(bank[6 + a][:, :])).then_inc(S["att_Tc"], 1)
                elif j == 9:
                    act.wait_ge(S["att_sc"], u + 1)
                    nc.scalar.activation(sg[:, :, :], four(bank[6][:, :]), ACT.Sigmoid, scale=4.0 * 128 ** -0.5)\
                        .then_inc(S["att_sg"], 1)
                elif j == 15:
                    act.wait_ge(S["ffn_T"], u + 1)
                    nc.scalar.copy(xnT[:, :, 128 * u:128 * u + 128], four(bank[6][:, :])).then_inc(S["ffn_Tc"], 1)

            for l in range(2):
                O = OUTS[l]
                act.wait_ge(S["folded"], 2 * l + 1)
                link(nc.scalar.activation(wfull[l], bank[0][:, 0:O], ACT.Copy, scale=W_SCALE))
                link(nc.scalar.copy(wv_hi[l][:, :], wfull[l]))
                nc.scalar.copy(wback[l], wv_hi[l][:, :]).then_inc(S["fold_taken"], 1)
                act.wait_ge(S["folded"], 2 * l + 2)
                for b in range(BH):
                    r = slice(C * b, C * b + C)
                    nc.scalar.copy(wcen[l][r, O * b:O * b + O], bank[1][r, 0:O])
                    nc.scalar.mul(wdif[l][r, O * b:O * b + O], bank[1][r, 64:64 + O], -1.0)
                nc.scalar.copy(bias[l][:, :], bank[1][:, 128:129]).then_inc(S["fold_taken"], 1)
                if l == 0:
                    root(2)
            for j in range(4):
                prepare(0, j)

            def count(j, i4):
                act.wait_ge(S["cmp_ready"], j + 1)
                for nt in range(NT):
                    ins = nc.scalar.activation(bank[i4 + nt][:, :], bank[i4 + nt][:, :], ACT.Sign,
                                               accum_out=counts[:, bass.ds(NT * j + nt, 1)])
                ins.then_inc(S["act_counted"], 1)

            with act.Fori(0, CMP // 2) as i:
                count(2 * i, 0)
                count(2 * i + 1, 4)

            for j in range(4, PREP):
                prepare(0, j)
            def exponentials(p, t, k):
                s = STEPS * p + t
                act.wait_ge(S["d_ready"], s + 1)
                freed(act, s, "a_ready")
                nc.scalar.activation(ex[0:ROWS, k, :], dif[0:ROWS, k, :], ACT.Exp, scale=HEAD_SCALE)\
                    .then_inc(S["e_ready"], 1)

            def factors(p, t, k):
                s, O = STEPS * p + t, OUTS[PASSES[p][1]]
                act.wait_ge(S["aT_psum"], s + 1)
                freed(act, s, "y_psum")
                nc.scalar.copy(atT[:, k, :], bank[2 + k][0:COLS, 0:BH * ROWS]).then_inc(S["aT_sb"], 1)
                act.wait_ge(S["v_psum"], s + 1)
                nc.scalar.activation(val[:, k, 0:BH * O], bank[VAL_BANK][0:COLS, 0:BH * O],
                                     ACT.Copy, scale=1.0 / W_SCALE).then_inc(S["v_sb"], 1)

            def step(p, t, k):
                behind(exponentials, p, t, k)
                behind(factors, p, t - 2, k)

            for p in range(len(PASSES)):
                first = {ROOT_AT: [lambda p=p: root(PASSES[p - 1][1] + 1)]} if p else {}
                pipeline(act, p, step, 2, spare_work(p, first, value_columns, prepare, after))
            root(2)
            for j in range(AFTER):
                after(1, j)
            gates(1)

        @block.tensor
        def _(pe):
            def cols(v, start, n):
                return v[:, bass.ds(start, n)]

            def prepare(q, j):
                u, l = PASSES[q]
                par = q % 2
                F = features(u, l)

                def sort(b, nt):
                    n = NT * (BH * q + b) + nt
                    pe.wait_ge(S["onehot"], n + 1)
                    if b >= 2 and nt == 0:
                        pe.wait_ge(S["sorted_sb"], 3 * (BH * q + b - 2) + 1)
                    for part in range(2):
                        for m in range(M):
                            ins = nc.tensor.matmul(bank[SORT_BANK[b % 2]][C * m:C * m + C, :],
                                                   fT[:, part, 128 * nt + C * b:128 * nt + C * b + C],
                                                   perm[:, n % 8, m, :],
                                                   start=(nt == 0 and part == 0), stop=(nt == NT - 1 and part == 1))
                    ins.then_inc(S["sorted_psum"], 1)

                def centre(g, part):
                    w = slice(128 * g, 128 * g + 128)
                    if part == 0:
                        nc.tensor.matmul(bank[7][:, :], wcen[l][:, w], cen32[:, :], start=True, stop=False)
                    else:
                        nc.tensor.matmul(bank[7][:, :], wdif[l][:, w], F, start=False, stop=True).then_inc(S["z_psum"], 1)

                if j == 0:
                    features_ready(pe, u, l)
                    if q:
                        pe.wait_ge(S["sorted_sb"], 3 * BH * q)
                        pe.wait_ge(S["vT_lo"], VC * min(q, 2))
                    for nt in range(NT):
                        ins = nc.tensor.transpose(bank[6][:, 128 * nt:128 * nt + 128], F[:, 128 * nt:128 * nt + 128],
                                                  ident[:, :])
                    ins.then_inc(S["fT_psum"], 1)
                elif j in (1, 2):
                    pe.wait_ge(S["cen_done"], 2 * q + 2)
                    centre(0, j - 1)
                elif j in (4, 5) and l == 1:
                    pe.wait_ge(S["z_ready"], Z_BEFORE[q] + 1)
                    centre(1, j - 4)
                if j == 3:
                    pe.wait_ge(S["fT_lo"], q + 1)
                    pe.wait_ge(S["fT_hi"], q + 1)
                if 3 <= j < 3 + NT * BH:
                    if j == 3 + NT:
                        pe.wait_ge(S["z_ready"], Z_BEFORE[q + 1])
                    sort((j - 3) // NT, (j - 3) % NT)

            def value_columns(p, c):
                n = VC * p + c
                if c < 2:
                    pe.wait_ge(S["sorted_sb"], 3 * BH * (p + 1))
                else:
                    pe.wait_ge(S["vT_lo"], n - 1)
                for i, (w, keys) in enumerate(((wv_hi, khi), (wv_lo, khi), (wv_hi, klo))):
                    for b in range(BH):
                        ins = nc.tensor.matmul(bank[6 + c % 2][C * b:C * b + C, 0:VCW], w[0][:, :],
                                               keys[p % 2][:, b, VCW * c:VCW * c + VCW], start=(i == 0), stop=(i == 2))
                ins.then_inc(S["vT_psum"], 1)

            def ffn_hidden(u, m):
                for branch in range(2):
                    for c in range(4):
                        col = 128 * (m + 4 * branch)
                        ins = nc.tensor.matmul(bank[m][:, 128 * branch:128 * branch + 128], w12T[:, c, col:col + 128],
                                               xnT[:, c, 128 * u:128 * u + 128], start=(c == 0), stop=(c == 3))
                ins.then_inc(S["ffn_h"], 1)

            def ffn_out(u, m):
                pe.wait_ge(S["ffn_x4"], 4 * u + m + 1)
                ins = nc.tensor.matmul(bank[4 + u][:, :], x4T[:, m, 128 * u:128 * u + 128], w3T[:, m, :],
                                       start=(m == 0), stop=(m == 3))
                if m == 3:
                    ins.then_inc(S["ffn_o"], 1)

            def after(u, j):
                if j == 0:
                    if u == 0:
                        pe.wait_ge(S["weights"], 16 * (3 * BH + 1))
                        pe.wait_ge(S["sorted_sb"], 3 * BH * len(PASSES))
                    else:
                        pe.wait_ge(S["ffn_Tc"], 1)
                    parts = (FX[:, u, :], F1[:, u, :], F2[:, 0, :], F2[:, 1, :])
                    for i, f in enumerate(parts):
                        if i >= 2:
                            pe.wait_ge(S["f2_ready"], 2 * u + i - 1)
                        ins = nc.tensor.matmul(bank[6][:, :], w3bd[:, i, :], f, start=(i == 0), stop=(i == 3))
                    ins.then_inc(S["h3_psum"], 1)
                elif j == 6:
                    pe.wait_ge(S["att_in"], 2 * u + 1)
                    for a in range(2):
                        for h in range(4):
                            ins = nc.tensor.transpose(bank[6 + a][:, 128 * h:128 * h + 128],
                                                      qkv[:, a, 128 * h:128 * h + 128], ident[:, :])
                        ins.then_inc(S["att_T"], 1)
                elif j == 8:
                    pe.wait_ge(S["att_Tc"], 2 * u + 2)
                    for h in range(4):
                        ins = nc.tensor.matmul(bank[6][:, 128 * h:128 * h + 128], qkT[:, 4 + h, :], qkT[:, h, :],
                                               start=True, stop=True)
                    ins.then_inc(S["att_sc"], 1)
                    if u == 1:
                        ffn_out(0, 0)
                        ffn_out(0, 1)
                elif j == 11:
                    pe.wait_ge(S["att_in"], 2 * u + 2)
                    pe.wait_ge(S["att_m"], u + 1)
                    for h in range(4):
                        ins = nc.tensor.matmul(bank[7][:, 128 * h:128 * h + 128], sgm[:, h, :],
                                               qkv[:, 2, 128 * h:128 * h + 128], start=True, stop=True)
                    ins.then_inc(S["att_o"], 1)
                    if u == 1:
                        ffn_out(0, 2)
                        ffn_out(0, 3)
                elif j == 14:
                    pe.wait_ge(S["ffn_x"], u + 1)
                    for c in range(4):
                        ins = nc.tensor.transpose(bank[6][:, 128 * c:128 * c + 128], xn[:, u, 128 * c:128 * c + 128],
                                                  ident[:, :])
                    ins.then_inc(S["ffn_T"], 1)

            pe.wait_ge(S["first_consts"], 32)
            pe.wait_ge(S["scales_ready"], 1)
            for c in range(3):
                ins = nc.tensor.matmul(bank[7][:, 2 * c:2 * c + 2], to_points[:, 128 * c:128 * c + 128], cs[:, 0:5:4],
                                       start=True, stop=True)
            ins.then_inc(S["scales_psum"], 1)
            pe.wait_ge(S["fold_in"], 16 * 6)
            for l in range(2):
                O = OUTS[l]
                if l:
                    pe.wait_ge(S["fold_taken"], 2)
                for m in range(M):
                    slot = PERMS[l].index(m)
                    ins = nc.tensor.matmul(bank[0][C * m:C * m + C, 0:O], wlin[l][:, 4 * C + slot:8 * C:4],
                                           wconvT[l][:, 0:O], start=True, stop=True)
                ins.then_inc(S["folded"], 1)
                for b in range(BH):
                    for kind in range(2):
                        for slot in range(M):
                            nc.tensor.matmul(bank[1][C * b:C * b + C, 64 * kind:64 * kind + O],
                                             wlin[l][:, 4 * C * kind + slot:4 * C * (kind + 1):4],
                                             wconvT[l][:, 0:O], start=(slot == 0), stop=(slot == M - 1))
                nc.tensor.matmul(bank[1][:, 128:129], wconvT[l], blin[l][:, :], start=True, stop=True)\
                    .then_inc(S["folded"], 1)
            pe.wait_ge(S["fold_taken"], 4)
            pe.wait_ge(S["consts"], 16 * 3)
            for j in range(3):
                prepare(0, j)

            def compare(j):
                freed(pe, j, "act_counted")
                for part, (L, R, rows) in enumerate(((LA, RA, 6), (LB, RB, 4))):
                    for nt in range(NT):
                        g = slice(32 * nt, 32 * nt + rows)
                        ins = nc.tensor.matmul(bank[4 * (j % 2) + nt][:, :], L[g, 128 * j:128 * j + 128],
                                               R[g, N * j:N * j + N], start=(part == 0), stop=(part == 1))
                ins.then_inc(S["cmp_ready"], 1)

            pe.wait_ge(S["chunk_in"], 16 * 8)
            pe.wait_ge(S["key_rows_in"], 16 * 12)
            pe.wait_ge(S["z_ready"], 1)
            pe.wait_ge(S["fT_lo"], 1)
            for j in range(OWN_AT):
                compare(j)
            pe.wait_ge(S["act_counted"], OWN_AT - 1)
            pe.wait_ge(S["split_in"], 16)
            for a in range(2):
                ins = nc.tensor.transpose(bank[0][:, 64 * a:64 * a + 64], split_rows[:, a, :], ident[0:64, 0:64])
            ins.then_inc(S["own_psum"], 1)
            pe.wait_ge(S["own_ready"], 1)
            for j in range(OWN_AT, CMP):
                if j == 2 * B:
                    pe.wait_ge(S["chunk_h_in"], 16 * 8)
                compare(j)
            pe.wait_ge(S["act_counted"], CMP)
            pe.wait_ge(S["masks"], 16 * 3)
            pe.wait_ge(S["ident16_ready"], 1)

            for j in range(3, PREP):
                prepare(0, j)
            def scores(p, t, k):
                s, par = STEPS * p + t, p % 2
                edge = isinstance(t, int) and t == 0
                freed(pe, s, "d_ready")
                sc = bank[k][:, 0:BH * COLS]
                rows = 3 * G if edge else G
                msk = (edge_mask if edge else inner_mask)[:, :]
                msk = bass.AP(msk.tensor, msk.offset, [msk.ap[0], [0, BH], [1, SPAN], [0, HEADS]])
                nc.tensor.matmul(sc, rows_ind[0:rows, :], msk, start=True, stop=False, skip_group_check=True)
                if edge:
                    pe.wait_ge(S["key_hi"], BH * (p + 1))
                    pe.wait_ge(S["key_lo"], BH * (p + 1))
                pe.wait_ge(S["x_ready"], s + 1)
                for b in range(BH):
                    for keys in (khi[par], klo[par]):
                        ins = nc.tensor.matmul(sc[:, COLS * b:COLS * b + COLS], xq[:, k, ROWS * b:ROWS * b + 128],
                                               cols(keys[:, b, :], HEADS * G * t, COLS), start=False,
                                               stop=True, skip_group_check=True)
                ins.then_inc(S["sc_ready"], 1)

            def turn(p, t, k):
                s = STEPS * p + t
                pe.wait_ge(S["a_ready"], s + 1)
                freed(pe, s, "aT_sb")
                for b in range(BH):
                    ins = nc.tensor.transpose(bank[2 + k][0:COLS, ROWS * b:ROWS * b + ROWS],
                                              at[0:ROWS, k, COLS * b:COLS * b + COLS], ident[0:ROWS, 0:ROWS])
                ins.then_inc(S["aT_psum"], 1)

            def values(p, t, k):
                l, par = PASSES[p][1], p % 2
                s, O = STEPS * p + t, OUTS[l]
                freed(pe, s, "v_sb", 1)
                o = bank[VAL_BANK][0:COLS, 0:BH * O]
                if l == 0:
                    if isinstance(t, int) and t < VC:
                        pe.wait_ge(S["vT_lo"], VC * p + t + 1)
                    for a in range(2):
                        ins = nc.tensor.matmul(o, cols(vT[:, a, :], HEADS * G * t, COLS), ident16[:, :],
                                               start=(a == 0), stop=(a == 1))
                else:
                    width = COLS if isinstance(t, int) and t == STEPS - 1 else 128
                    o = bank[VAL_BANK][0:width, 0:BH * O]
                    for b in range(BH):
                        hi, lo = (cols(keys[:, b, :], HEADS * G * t, width) for keys in (khi[par], klo[par]))
                        for i, (w, keys) in enumerate(((wv_hi, hi), (wv_lo, hi), (wv_hi, lo))):
                            ins = nc.tensor.matmul(o[:, O * b:O * b + O], keys, w[l][:, :],
                                                   start=(i == 0), stop=(i == 2))
                ins.then_inc(S["v_psum"], 1)

            def products(p, t, k):
                l = PASSES[p][1]
                s, O = STEPS * p + t, OUTS[l]
                pe.wait_ge(S["aT_sb"], s + 1)
                pe.wait_ge(S["v_sb"], s + 1)
                freed(pe, s, "ys_done", 1)
                for b in range(BH):
                    r, c = (C * b, 0) if l == 0 else (64 * (b % 2), ROWS * (b // 2))
                    ins = nc.tensor.matmul(bank[Y_BANK][r:r + O, c:c + ROWS], val[:, k, O * b:O * b + O],
                                           atT[:, k, ROWS * b:ROWS * b + ROWS], start=True, stop=True,
                                           skip_group_check=True)
                ins.then_inc(S["y_psum"], 1)

            def step(p, t, k):
                behind(scores, p, t, k)
                behind(turn, p, t - 2, k)
                behind(values, p, t - 2, k)
                behind(products, p, t - 3, 1 - k)

            pe.wait_ge(S["folded_low"], 2)
            for p in range(len(PASSES)):
                pipeline(pe, p, step, 3, spare_work(p, {}, value_columns, prepare, after))

            pe.wait_ge(S["ffn_w"], 32)
            pe.wait_ge(S["d_ready"], STEPS * len(PASSES))
            pe.wait_ge(S["aT_sb"], STEPS * len(PASSES))
            ffn_hidden(0, 0)
            ffn_hidden(0, 1)
            after(1, 0)
            ffn_hidden(0, 2)
            ffn_hidden(0, 3)
            pe.wait_ge(S["ymax_done"], STEPS * len(PASSES))
            for j in range(1, AFTER):
                after(1, j)
            pe.wait_ge(S["ffn_Tc"], 2)
            for m in range(4):
                ffn_hidden(1, m)
                if m >= 2:
                    ffn_out(1, m - 2)
            ffn_out(1, 2)
            ffn_out(1, 3)

        @block.vector
        def _(dve):
            v = nc.vector
            link = chain(dve, "dve_link")
            for l in range(2):
                v.memset(wcen[l][:, :], 0.0)
                link(v.memset(wdif[l][:, :], 0.0))
            link(v.memset(eps_col[:, :], EPS))
            variances = [0]

            def to_root(ins):
                variances[0] += 1
                ins.then_inc(S["var_ready"], 1)

            def inverse_root(n):
                dve.wait_ge(S["std_ready"], variances[0])
                link(v.reciprocal(rstd[:, 0:n], rstd[:, 0:n]))

            c1 = lambda i: cs[:, i:i + 1]
            dve.wait_ge(S["coords"], 48)
            v.tensor_reduce(c1(0), crd, AX.X, ALU.min)
            link(v.tensor_reduce(c1(1), crd, AX.X, ALU.max))
            link(v.tensor_tensor(c1(2), c1(1), c1(0), ALU.subtract))
            link(v.tensor_scalar(c1(2), c1(2), 1e-6, None, ALU.add))
            top = float(2 ** BITS - 1)
            v.tensor_scalar(c1(9), c1(2), 4097.0, None, ALU.mult)
            link(v.reciprocal(c1(3), c1(2)))
            v.tensor_tensor(c1(10), c1(9), c1(2), ALU.subtract)
            link(v.tensor_scalar(c1(4), c1(3), top, None, ALU.mult))
            v.tensor_tensor(c1(5), c1(9), c1(10), ALU.subtract)
            link(v.tensor_scalar(c1(13), c1(4), 4097.0, None, ALU.mult))
            v.tensor_tensor(c1(6), c1(2), c1(5), ALU.subtract)
            link(v.tensor_tensor(c1(14), c1(13), c1(4), ALU.subtract))
            link(v.tensor_tensor(c1(7), c1(13), c1(14), ALU.subtract))
            v.tensor_tensor(c1(8), c1(4), c1(7), ALU.subtract)
            link(v.tensor_tensor(c1(11), c1(5), c1(7), ALU.mult))
            link(v.tensor_scalar(c1(11), c1(11), -1.0, top, ALU.mult, ALU.add))
            for x, y, to in ((5, 8, 12), (6, 7, 13), (6, 8, 14)):
                ins = v.tensor_tensor(c1(to), c1(x), c1(y), ALU.mult)
            link(ins)
            for to in (12, 13, 14):
                link(v.tensor_tensor(c1(11), c1(11), c1(to), ALU.subtract))
            link(v.tensor_tensor(c1(12), c1(11), c1(3), ALU.mult))
            v.tensor_tensor(c1(4), c1(4), c1(12), ALU.add).then_inc(S["scales_ready"], 1)
            dve.wait_ge(S["scales_psum"], 1)
            link(v.tensor_copy(scales[:, :], bank[7][:, 0:6]))
            dve.wait_ge(S["points_in"], 16 * B)
            for c in range(3):
                ins = v.tensor_scalar(xyz[:, c, :], xyz[:, c, :], scales[:, 2 * c:2 * c + 1],
                                      scales[:, 2 * c + 1:2 * c + 2], ALU.subtract, ALU.mult)
            link(ins)
            link(v.tensor_copy(xyz_q, xyz))
            link(v.tensor_copy(xyz_r, xyz_q))
            link(v.tensor_tensor(xyz_up, xyz_r, xyz, ALU.is_gt))
            link(v.tensor_tensor(xyz_r, xyz_r, xyz_up, ALU.subtract))

            SHL, SHR, SAR = ALU.logical_shift_left, ALU.logical_shift_right, ALU.arith_shift_right
            AND, OR, XOR = ALU.bitwise_and, ALU.bitwise_or, ALU.bitwise_xor

            def words(to):
                v.tensor_scalar(to[:, :, 0, :], xyz_r, 0.0, top, ALU.max, ALU.min)
                for w, c in enumerate((1, 0, 2)):
                    ins = v.tensor_scalar(to[:, w, 1, :], xyz_r[:, c, :], 0.0, top, ALU.max, ALU.min)
                link(ins)

            words(XK)
            dve.wait_ge(S["first_consts"], 32)
            key = T2[:, 0, :, :].rearrange("p a j -> p (a j)")

            def join(X3):
                x3, s1 = (T.rearrange("p w a j -> p (w a j)") for T in (X3, T1))
                for sh, keep in ((16, 0x030000FF), (8, 0x0300F00F), (4, 0x030C30C3), (2, 0x09249249)):
                    link(v.scalar_tensor_tensor(s1, x3, sh, x3, SHL, OR))
                    link(v.tensor_scalar(x3, s1, keep, None, AND))
                word = [X3[:, w, :, :].rearrange("p a j -> p (a j)") for w in range(3)]
                k1 = T1[:, 0, :, :].rearrange("p a j -> p (a j)")
                link(v.scalar_tensor_tensor(k1, word[0], 1, word[1], SHL, OR))
                link(v.scalar_tensor_tensor(key, k1, 1, word[2], SHL, OR))

            def cut(w, out, name, rows=128):
                T, k = T3[0:rows, :, w], key[0:rows, w]
                nw = npoint[0:rows, w]
                v.tensor_scalar(T[:, 0, :], k, 127, 1, AND, SHL)
                link(v.tensor_scalar(T[:, 1, :], nw, 8, None, SHR))
                v.tensor_tensor(T[:, 0, :], T[:, 0, :], T[:, 1, :], OR)
                v.tensor_scalar(T[:, 2, :], k, 15, 255, SHR, AND)
                link(v.tensor_scalar(T[:, 3, :], k, 23, None, SHR))
                link(v.tensor_scalar(T[:, 1, :], k, 7, 255, SHR, AND))
                for j in range(4):
                    ins = v.tensor_scalar(out[:, j, :], T[:, j, :], float(2 ** (8 * j + 8)), None, ALU.mult)
                ins.then_inc(S[name], 1)

            join(XK)
            cut(slice(0, 64), chunks, "chunks_done")
            dve.wait_ge(S["x_in"], 32)
            for u in range(HALVES):
                link(v.bn_stats(bst[:, u, 0, :], X[:, u, :]))
                ins = v.bn_aggr(mv[:, u, :], bst[:, u, 0, :])
            to_root(ins)
            inverse_root(2)
            for u in range(HALVES):
                ins = v.tensor_scalar(FX[:, u, :], X[:, u, :], mv[:, u, 0:1], rstd[:, u:u + 1], ALU.subtract, ALU.mult)
            ins.then_inc(S["f0_ready"], 1)

            for l in range(2):
                dve.wait_ge(S["fold_taken"], 2 * l + 1)
                v.tensor_tensor(wv_lo[l][:, :], wfull[l], wback[l], ALU.subtract).then_inc(S["folded_low"], 1)

            def fT_low(q):
                v.tensor_tensor(fT[:, 1, :], bank[6][:, :], fT[:, 0, :], ALU.subtract).then_inc(S["fT_lo"], 1)

            dve.wait_ge(S["fT_hi"], 1)
            fT_low(0)
            words(XH)

            H = [XH[:, w, :, :].rearrange("p a j -> p (a j)") for w in range(3)]
            t1, t2, t3 = (T1[:, i, :, :].rearrange("p a j -> p (a j)") for i in range(3))
            t4 = T2[:, 1, :, :].rearrange("p a j -> p (a j)")
            for bit in range(BITS - 1, 0, -1):
                low = (1 << bit) - 1
                link(v.tensor_scalar(t1, H[0], 31 - bit, 31, SHL, SAR))
                link(v.scalar_tensor_tensor(H[0], t1, low, H[0], AND, XOR))
                for w in (1, 2):
                    v.tensor_scalar(t1, H[w], 31 - bit, 31, SHL, SAR)
                    link(v.tensor_tensor(t2, H[0], H[w], XOR))
                    link(v.tensor_tensor(t3, t2, t1, OR))
                    v.scalar_tensor_tensor(H[0], t3, low, H[0], AND, XOR)
                    link(v.tensor_tensor(t4, t3, t1, XOR))
                    link(v.scalar_tensor_tensor(H[w], t4, low, H[w], AND, XOR))
            link(v.tensor_tensor(H[1], H[1], H[0], XOR))
            link(v.tensor_tensor(H[2], H[2], H[1], XOR))
            link(v.tensor_scalar(t1, H[2], 1, None, SHR))
            for sh, src, dst in ((1, t1, t2), (2, t2, t3), (4, t3, t1), (8, t1, t2)):
                link(v.scalar_tensor_tensor(dst, src, sh, src, SHR, XOR))
            for w in range(3):
                ins = v.tensor_tensor(H[w], H[w], t2, XOR)
            link(ins)
            join(XH)
            link(v.tensor_scalar(T3[:, 0, :], key, 6, None, SHR))
            link(v.tensor_scalar(T3[:, 1, :], key, 63, 9, AND, SHL))
            link(v.tensor_tensor(T3[:, 2, :], T3[:, 1, :], npoint[:, :], OR))
            v.tensor_scalar(split[:, 0, :], T3[:, 0, :], float(2 ** 15), None, ALU.mult)
            v.tensor_copy(split[:, 1, :], T3[:, 2, :]).then_inc(S["split_done"], 1)
            dve.wait_ge(S["split_done"], 1)
            cut(slice(0, 32), chunks_h, "chunks_h_done", 64)

            dve.wait_ge(S["own_psum"], 1)
            v.tensor_copy(own[:, :, :], bank[0][:, 0:128].rearrange("p (a n) -> p a n", a=2)).then_inc(S["own_ready"], 1)
            dve.wait_ge(S["own_ready"], 1)

            for j in range(BH, 2 * B):
                i, slot, half = j - BH, j % 4, j % 2
                dve.wait_ge(S[f"rows_in{slot}"], 16 * (i // 4) + 16)
                for nt in range(NT):
                    dve.wait_ge(S["low_ready"], NT * i + nt + 1)
                    c, r = NT * j + nt, 2 * B * NT + NT * j + nt
                    ins = v.scalar_tensor_tensor(low_dif[:, 4 * half + nt, :], key_rows[:, slot, 0, :],
                                                 own[:, 0, c:c + 1], low_dif[:, 4 * half + nt, :],
                                                 ALU.subtract, ALU.is_lt, accum_out=ranks[:, r:r + 1])
                ins.then_inc(S["dve_counted"], 1)
            dve.wait_ge(S["act_counted"], CMP)
            dve.wait_ge(S["dve_counted"], 2 * B - BH)
            v.tensor_scalar(ranks[:, 0:CMP * NT], counts[:, :], -0.5, 0.5 * (N - 1), ALU.mult, ALU.add)\
                .then_inc(S["ranked"], 1)
            dve.wait_ge(S["ranked"], 1)

            def prepare(q, j):
                u, l = PASSES[q]
                par = q % 2

                if j < NT * BH:
                    b, nt = j // NT, j % NT
                    n = NT * BH * q + j
                    if n >= 8:
                        dve.wait_ge(S["sorted_psum"], n - 7)
                    for m in range(M):
                        r = (m * B + BH * u + b) * NT + nt
                        ins = v.tensor_scalar(perm[:, n % 8, m, :], iota[:, :], ranks[:, r:r + 1], None, ALU.is_equal)
                    ins.then_inc(S["onehot"], 1)
                if j == 2 and q:
                    dve.wait_ge(S["fT_hi"], q + 1)
                    fT_low(q)
                for b in range(BH):
                    at_ = j - 8 - NT * b
                    if at_ == 0:
                        dve.wait_ge(S["sorted_sb"], 3 * (BH * q + b + 1))
                        if q or b:
                            dve.wait_ge(S["key_lo"], BH * q + b)
                        v.tensor_tensor(s_lo[:, :], Sx[par][:, b, :], s_hi[:, :], ALU.subtract)\
                            .then_inc(S["sorted_low"], 1)
                    elif at_ == 1 and q == 0 and b >= 2:
                        dve.wait_ge(S["sorted_low"], b + 1)
                        for h in range(HEADS):
                            ins = v.tensor_scalar(klo[par][:, b, h::HEADS], s_lo[:, :], headmask[:, h:h + 1], None,
                                                  ALU.mult)
                        ins.then_inc(S["key_lo"], 1)

            def value_columns(p, c):
                w = slice(VCW * c, VCW * c + VCW)
                dve.wait_ge(S["vT_hi"], VC * p + c + 1)
                v.tensor_tensor(vT[:, 1, w], bank[6 + c % 2][:, 0:VCW], vT[:, 0, w], ALU.subtract)\
                    .then_inc(S["vT_lo"], 1)

            def finish(p):
                u, l = PASSES[p]
                inverse_root(l + 1)
                for g in range(l + 1):
                    y = ymax_of(p)[:, g, 0:N]
                    link(v.tensor_scalar(y, y, mv[:, g, 0:1], rstd[:, g:g + 1],
                                         ALU.subtract, ALU.mult))
                    dst = F1[:, u, :] if l == 0 else F2[:, g, :]
                    v.scalar_tensor_tensor(dst, y, 0.2, y, ALU.mult, ALU.max)\
                        .then_inc(S["f1_ready" if l == 0 else "f2_ready"], 1)

            def stats(src):
                link(v.bn_stats(lst[:, :], src))
                to_root(v.bn_aggr(mv[:, 0, :], lst[:, :]))

            def gated(u):
                w = slice(128 * u, 128 * u + 128)
                for m in range(4):
                    dve.wait_ge(S["ffn_g"], 4 * u + m + 1)
                    v.scalar_tensor_tensor(x4T[:, m, w], bank[m][:, 128:256], b12[:, 4 + m:5 + m], gate[:, m, w],
                                           ALU.add, ALU.mult).then_inc(S["ffn_x4"], 1)

            def ffn_store(u):
                dve.wait_ge(S["ffn_o"], u + 1)
                v.tensor_tensor(outb[:, u, :], bank[4 + u][:, :], res[:, u, :], ALU.add).then_inc(S["out_ready"], 1)

            def after(u, j):
                x = X[:, u, :]
                if j == 1:
                    dve.wait_ge(S["h3_psum"], u + 1)
                    stats(bank[6][:, :])
                elif j == 2:
                    inverse_root(1)
                    link(v.tensor_scalar(tmp[:, 0, :], bank[6][:, :], mv[:, 0, 0:1], rstd[:, 0:1], ALU.subtract, ALU.mult))
                    link(v.scalar_tensor_tensor(tmp[:, 1, :], tmp[:, 0, :], 0.2, tmp[:, 0, :], ALU.mult, ALU.max))
                elif j == 3:
                    link(v.tensor_tensor(x, x, tmp[:, 1, :], ALU.add))
                    stats(x)
                elif j == 4:
                    inverse_root(1)
                    link(v.tensor_scalar(xn[:, u, :], x, mv[:, 0, 0:1], rstd[:, 0:1], ALU.subtract, ALU.mult))
                elif j in (5, 6):
                    dve.wait_ge(S["bound"], 2 + j - 5)
                    for a in ((0, 1), (2,))[j - 5]:
                        ins = v.tensor_tensor(qkv[:, a, :], xn[:, u, :], bind[:, a, :], ALU.mult)
                    ins.then_inc(S["att_in"], 1)
                    if u == 1 and j == 6:
                        gated(0)
                elif j == 10:
                    dve.wait_ge(S["att_sg"], u + 1)
                    v.tensor_tensor(sgm[:, :, :], sg[:, :, :], window(causal, 0, [[0, 4], [1, 128]]), ALU.mult)\
                        .then_inc(S["att_m"], 1)
                elif j == 12:
                    dve.wait_ge(S["att_o"], u + 1)
                    link(v.tensor_tensor(x, bank[7][:, :], x, ALU.add))
                    stats(x)
                elif j == 13:
                    inverse_root(1)
                    v.tensor_scalar(xn[:, u, :], x, mv[:, 0, 0:1], rstd[:, 0:1], ALU.subtract, ALU.mult)\
                        .then_inc(S["ffn_x"], 1)
                    v.tensor_tensor(res[:, u, :], x, b3row, ALU.add).then_inc(S["x_updated"], 1)
                    if u == 1:
                        dve.wait_ge(S["x_updated"], 2)
                        ffn_store(0)

            for j in range(PREP):
                prepare(0, j)
            def score_columns(k):
                return by_head(bank[k][0:ROWS, 0:BH * COLS])

            def score_max(p, t, k):
                s = STEPS * p + t
                dve.wait_ge(S["sc_ready"], s + 1)
                v.tensor_reduce(heads(mx[0:ROWS, k, :]), score_columns(k), AX.X, ALU.max).then_inc(S["mx_done"], 1)

            def score_dif(p, t, k):
                s = STEPS * p + t
                dve.wait_ge(S["mx_done"], s + 1)
                freed(dve, s, "e_ready")
                v.tensor_tensor(by_head(dif[0:ROWS, k, :]), score_columns(k),
                                spread(heads(mx[0:ROWS, k, :]), SPAN), ALU.subtract).then_inc(S["d_ready"], 1)

            def exp_sum(p, t, k):
                dve.wait_ge(S["e_ready"], STEPS * p + t + 1)
                v.tensor_reduce(heads(sm[0:ROWS, k, :]), by_head(ex[0:ROWS, k, :]),
                                AX.X, ALU.add).then_inc(S["sum_done"], 1)

            def exp_factor(p, t, k):
                s = STEPS * p + t
                dve.wait_ge(S["sum_done"], s + 1)
                freed(dve, s, "a_ready")
                v.reciprocal(rs[0:ROWS, k, :], sm[0:ROWS, k, :]).then_inc(S["r_ready"], 1)

            def by_point(a, l):
                return a.rearrange("p (g n i) -> p g n i", g=l + 1, n=G)

            def output_add(p, t, k):
                l, par = PASSES[p][1], p % 2
                s, w = STEPS * p + t, ROWS * (l + 1)
                dve.wait_ge(S["y_psum"], s + 1)
                if isinstance(t, int) and t == 0:
                    dve.wait_ge(S["z_ready"], Z_BEFORE[p + 1])
                freed(dve, s, "ymax_done")
                v.tensor_tensor(by_point(ys[:, k, 0:w], l), by_point(bank[Y_BANK][:, 0:w], l),
                                window(z[:, par, 0, :], G * t, [[NPAD, l + 1], [1, G], [0, K]]), ALU.add)\
                    .then_inc(S["ys_done"], 1)

            def output_stats(p, t, k):
                dve.wait_ge(S["ys_done"], STEPS * p + t + 1)
                real = LAST_ROWS if isinstance(t, int) and t == STEPS - 1 else ROWS
                for g in range(PASSES[p][1] + 1):
                    v.bn_stats(bst[:, g, bass.ds(t, 1), :], ys[:, k, ROWS * g:ROWS * g + real])

            def output_max(p, t, k):
                l = PASSES[p][1]
                v.tensor_reduce(ymax_of(p)[:, :, bass.ds(G * t, G)], by_point(ys[:, k, 0:ROWS * (l + 1)], l),
                                AX.X, ALU.max).then_inc(S["ymax_done"], 1)

            def variance(p):
                dve.wait_ge(S["ymax_done"], STEPS * (p + 1))
                for g in range(PASSES[p][1] + 1):
                    ins = v.bn_aggr(mv[:, g, :], bst[:, g, :, :].rearrange("p a b -> p (a b)"))
                to_root(ins)
                dve.wait_ge(S["var_ready"], variances[0])

            def step(p, t, k):
                behind(output_add, p, t - 4, k)
                behind(exp_sum, p, t - 1, 1 - k)
                behind(output_stats, p, t - 4, k)
                behind(exp_factor, p, t - 1, 1 - k)
                behind(score_max, p, t, k)
                behind(output_max, p, t - 4, k)
                behind(score_dif, p, t, k)

            def binding_scales(a):
                if a == 0:
                    dve.wait_ge(S["bind_in"], 16 * 5)
                al = alpha[:, 4 * a:4 * a + 4]
                link(v.tensor_reduce(al, bind[:, a, :].rearrange("p (h e) -> p h e", h=4), AX.X, ALU.add,
                                     apply_absolute_value=True))
                v.tensor_scalar(al, al, 1.0 / 128, None, ALU.mult).then_inc(S["alpha_ready"], 1)

            for p in range(len(PASSES)):
                first = {3: [lambda p=p: variance(p - 1)], FINISH_AT: [lambda p=p: finish(p - 1)]} if p else {}
                if p == len(PASSES) - 1:
                    for a in range(3):
                        first[6 + a] = [lambda a=a: binding_scales(a)]
                pipeline(dve, p, step, 4, spare_work(p, first, value_columns, prepare, after, 1))
            variance(len(PASSES) - 1)
            finish(len(PASSES) - 1)
            for j in range(AFTER):
                after(1, j)
            gated(1)
            ffn_store(1)


def kernel(**inputs):
    import concourse.bacc as bacc
    from concourse.bass_utils import run_bass_kernel_spmd

    pre = "L0_"
    arrays = {
        "x": inputs["x"], "ctx_4096": inputs["ctx_4096"],
        "wl0": inputs[pre + "xattn_W_lin1"], "wl1": inputs[pre + "xattn_W_lin2"],
        "bl0": inputs[pre + "xattn_b_lin1"], "bl1": inputs[pre + "xattn_b_lin2"],
        "wc0T": np.transpose(inputs[pre + "xattn_W_conv1"]), "wc1T": np.transpose(inputs[pre + "xattn_W_conv2"]),
        "w3cT": np.transpose(inputs[pre + "xattn_W_conv3"]),
        "bv_q": inputs[pre + "attn_bv_q"], "bv_k": inputs[pre + "attn_bv_k"], "bv_v": inputs[pre + "attn_bv_v"],
        "w12T": np.transpose(inputs[pre + "ffn_w12"]), "b12": np.transpose(np.reshape(inputs[pre + "ffn_b12"], (8, 128))),
        "w3T": np.transpose(inputs[pre + "ffn_w3"]), "b3": inputs[pre + "ffn_b3"],
        **constants(),
    }
    arrays = {f"in_{k}": np.ascontiguousarray(v) for k, v in arrays.items()}
    nc = bacc.Bacc("TRN2", target_bir_lowering=False, num_devices=1)
    d = {k[3:]: nc.dram_tensor(k, a.shape, mybir.dt.from_np(a.dtype), kind="ExternalInput").ap()
         for k, a in arrays.items()}
    d["out"] = nc.dram_tensor("out", (B, C, N), F32, kind="ExternalOutput").ap()
    build(nc, d)
    result = run_bass_kernel_spmd(nc, [arrays], core_ids=[0])
    return result.results[0]["out"]
```
